# Optimizing a Trainium2 kernel written in Bass

```python
import numpy as np
import jax
import jax.numpy as jnp

def _softmax(x, axis=-1):
    return jax.nn.softmax(x, axis=axis)

def _gelu(x):
    return jax.nn.gelu(x, approximate=True)

def _silu(x):
    return jax.nn.silu(x)

def _sigmoid(x):
    return jax.nn.sigmoid(x)

def _layernorm(x, axis=-1, eps=1e-05):
    m = jnp.mean(x, axis=axis, keepdims=True)
    v = jnp.var(x, axis=axis, keepdims=True)
    return (x - m) / jnp.sqrt(v + eps)

def _scatter_add(tgt, idx, src, axis=0):
    return tgt.at[idx].add(src)

def _segment_sum(src, seg, n):
    return jax.ops.segment_sum(src, seg, n)
kernel_name = 'mk_gnn_resnorm_d2_gnn_r32_113548'

def setup_inputs(seed: int=0):
    np.random.seed(seed)
    _w = jnp.asarray

    def _rec_inputs():
        import jax
        import jax.numpy as jnp
        _gk = jax.random.key(seed)
        x = -6.415e-05 + 1 * jax.random.normal(jax.random.fold_in(_gk, 1), (10000, 512), jnp.float32)
        src = jax.random.randint(jax.random.fold_in(_gk, 2), (10000,), 0, 10000, jnp.int32)
        dst = jax.random.randint(jax.random.fold_in(_gk, 3), (10000,), 0, 10000, jnp.int32)
        _o = jnp.argsort(dst, stable=True)
        src = src[_o]
        dst = dst[_o]
        return (x, src, dst)
    x, src, dst = _rec_inputs()

    def _L0_gnn_setup():
        import jax, jax.numpy as jnp
        import numpy as np
        N = 625
        E = 250000
        B = 128
        Fin = 512
        Fqk = 512
        Fv = 512
        H = 8
        key = jax.random.key(seed)
        k1, k2, k3, k4 = jax.random.split(key, 4)
        x = jax.random.normal(k1, (N, Fin), dtype=jnp.float32)
        batch = jnp.sort(jax.random.randint(k2, (N,), 0, B)).astype(jnp.int32)
        ei = jax.random.randint(k3, (2, E), 0, N).astype(jnp.int32)
        W = jax.random.normal(k4, (Fin, 2 * Fqk + Fv), dtype=jnp.float32) / np.sqrt(Fin).astype(np.float32)
        return {'x': x, 'batch': batch, 'ei': ei, 'W': W}
    _L0_gnn_all = _L0_gnn_setup()
    _L0_gnn_in = {k: v for k, v in _L0_gnn_all.items() if k in ('W',)}
    del _L0_gnn_all

    def _L1_gnn_setup():
        import jax, jax.numpy as jnp
        import numpy as np
        B = 32
        MAXN = 64
        HEADS = 8
        DH = 64
        M = 256
        D = 512
        EPS = 1e-05
        KEPS = 1e-06

        def _batchnorm(x, g, b):
            mu = jnp.mean(x, axis=0)
            var = jnp.mean((x - mu) ** 2, axis=0)
            return (x - mu) * jax.lax.rsqrt(var + EPS) * g + b

        def _forward(x, batch, edge_index, norm1_g, norm1_b, norm2_g, norm2_b, W_conv, b_conv, Wq, Wk, Wv, Wo, proj):
            N = x.shape[0]
            E = edge_index.shape[1]
            h = x
            xn = _batchnorm(x, norm1_g, norm1_b)
            msg = xn[edge_index[0]]
            agg = jax.ops.segment_sum(msg, edge_index[1], num_segments=N)
            deg = jax.ops.segment_sum(jnp.ones((E,), x.dtype), edge_index[1], num_segments=N)
            agg = agg / jnp.maximum(deg, 1.0)[:, None]
            conv_out = jax.nn.relu(agg @ W_conv + b_conv)
            counts = jax.ops.segment_sum(jnp.ones((N,), jnp.int32), batch, num_segments=B)
            offsets = jnp.concatenate([jnp.zeros((1,), jnp.int32), jnp.cumsum(counts)[:-1]])
            pos = jnp.arange(N, dtype=jnp.int32) - offsets[batch]
            h_dense = jnp.zeros((B, MAXN, D), x.dtype).at[batch, pos].set(h)
            mask = jnp.zeros((B, MAXN), bool).at[batch, pos].set(True)

            def heads(t, W):
                return (t @ W).reshape(B, MAXN, HEADS, DH).transpose(0, 2, 1, 3)
            q, k, v = (heads(h_dense, Wq), heads(h_dense, Wk), heads(h_dense, Wv))
            scale = DH ** (-0.25)

            def phi(t, is_query):
                t = t * scale
                u = jnp.einsum('bhnd,md->bhnm', t, proj)
                diag = 0.5 * jnp.sum(t * t, axis=-1, keepdims=True)
                if is_query:
                    m_ = jnp.max(u, axis=-1, keepdims=True)
                else:
                    m_ = jnp.max(u, axis=(-2, -1), keepdims=True)
                return jnp.exp(u - diag - jax.lax.stop_gradient(m_)) / np.sqrt(M) + KEPS
            qf = phi(q, True)
            kf = phi(k, False) * mask[:, None, :, None]
            vm = v * mask[:, None, :, None]
            kv = jnp.einsum('bhnm,bhnd->bhmd', kf, vm)
            z = 1.0 / (jnp.einsum('bhnm,bhm->bhn', qf, kf.sum(axis=2)) + KEPS)
            attn = jnp.einsum('bhnm,bhmd->bhnd', qf, kv) * z[..., None]
            attn = attn.transpose(0, 2, 1, 3).reshape(B, MAXN, D) @ Wo
            h_attn = attn[batch, pos]
            return _batchnorm(conv_out + h_attn + h, norm2_g, norm2_b)
        key = jax.random.key(seed)
        ks = jax.random.split(key, 10)
        sizes = 1024 + np.arange(B) * 131 % 1025
        N = int(sizes.sum())
        E = N * 8
        batch = jnp.asarray(np.repeat(np.arange(B), sizes), dtype=jnp.int32)
        edge_index = jax.random.randint(ks[0], (2, E), 0, N, dtype=jnp.int32)
        s = 1.0 / np.sqrt(D)
        return {'x': jax.random.normal(ks[1], (N, D), jnp.float32), 'batch': batch, 'edge_index': edge_index, 'norm1_g': jnp.ones((D,), jnp.float32), 'norm1_b': jnp.zeros((D,), jnp.float32), 'norm2_g': jnp.ones((D,), jnp.float32), 'norm2_b': jnp.zeros((D,), jnp.float32), 'W_conv': jax.random.normal(ks[2], (D, D), jnp.float32) * s, 'b_conv': jnp.zeros((D,), jnp.float32), 'Wq': jax.random.normal(ks[3], (D, D), jnp.float32) * s, 'Wk': jax.random.normal(ks[4], (D, D), jnp.float32) * s, 'Wv': jax.random.normal(ks[5], (D, D), jnp.float32) * s, 'Wo': jax.random.normal(ks[6], (D, D), jnp.float32) * s, 'proj': jax.random.normal(ks[7], (M, DH), jnp.float32)}
    _L1_gnn_all = _L1_gnn_setup()
    _L1_gnn_in = {k: v for k, v in _L1_gnn_all.items() if k in ('norm1_g', 'norm1_b', 'norm2_g', 'norm2_b', 'W_conv', 'b_conv', 'Wq', 'Wk', 'Wv', 'Wo', 'proj')}
    del _L1_gnn_all
    return {'x': x, 'src': src, 'dst': dst, 'L0_gnn_W': _L0_gnn_in['W'], 'L1_gnn_norm1_g': _L1_gnn_in['norm1_g'], 'L1_gnn_norm1_b': _L1_gnn_in['norm1_b'], 'L1_gnn_norm2_g': _L1_gnn_in['norm2_g'], 'L1_gnn_norm2_b': _L1_gnn_in['norm2_b'], 'L1_gnn_W_conv': _L1_gnn_in['W_conv'], 'L1_gnn_b_conv': _L1_gnn_in['b_conv'], 'L1_gnn_Wq': _L1_gnn_in['Wq'], 'L1_gnn_Wk': _L1_gnn_in['Wk'], 'L1_gnn_Wv': _L1_gnn_in['Wv'], 'L1_gnn_Wo': _L1_gnn_in['Wo'], 'L1_gnn_proj': _L1_gnn_in['proj']}

def reference(x, src, dst, L0_gnn_W, L1_gnn_norm1_g, L1_gnn_norm1_b, L1_gnn_norm2_g, L1_gnn_norm2_b, L1_gnn_W_conv, L1_gnn_b_conv, L1_gnn_Wq, L1_gnn_Wk, L1_gnn_Wv, L1_gnn_Wo, L1_gnn_proj):
    import jax
    import jax.numpy as jnp

    def _L0_gnn_ref(x, batch, ei, W):
        import jax, jax.numpy as jnp
        import numpy as np
        N = 625
        E = 250000
        B = 128
        Fin = 512
        Fqk = 512
        Fv = 512
        H = 8
        src, dest = (ei[0], ei[1])
        n = x.shape[0]
        Fh = Fqk // H
        Fhv = Fv // H
        scaling = float(Fh) ** (-0.5)
        qkv = x @ W
        q, k, v = jnp.split(qkv, [Fqk, 2 * Fqk], axis=-1)
        q = (q * scaling).reshape(n, H, Fh)
        k = k.reshape(n, H, Fh)
        v = v.reshape(n, H, Fhv)
        qs = q[src]
        ks = k[dest]
        vs = v[dest]
        aw = jnp.einsum('ehf,ehf->eh', qs, ks)
        m = jax.ops.segment_max(aw, src, num_segments=n)
        e = jnp.exp(aw - m[src])
        denom = jax.ops.segment_sum(e, src, num_segments=n)
        alpha = e / denom[src]
        out = jax.ops.segment_sum(alpha[:, :, None] * vs, src, num_segments=n)
        return out.reshape(n, Fv)

    def _L1_gnn_ref(x, batch, edge_index, norm1_g, norm1_b, norm2_g, norm2_b, W_conv, b_conv, Wq, Wk, Wv, Wo, proj):
        import jax, jax.numpy as jnp
        import numpy as np
        B = 32
        MAXN = 64
        HEADS = 8
        DH = 64
        M = 256
        D = 512
        EPS = 1e-05
        KEPS = 1e-06

        def _batchnorm(x, g, b):
            mu = jnp.mean(x, axis=0)
            var = jnp.mean((x - mu) ** 2, axis=0)
            return (x - mu) * jax.lax.rsqrt(var + EPS) * g + b

        def _forward(x, batch, edge_index, norm1_g, norm1_b, norm2_g, norm2_b, W_conv, b_conv, Wq, Wk, Wv, Wo, proj):
            N = x.shape[0]
            E = edge_index.shape[1]
            h = x
            xn = _batchnorm(x, norm1_g, norm1_b)
            msg = xn[edge_index[0]]
            agg = jax.ops.segment_sum(msg, edge_index[1], num_segments=N)
            deg = jax.ops.segment_sum(jnp.ones((E,), x.dtype), edge_index[1], num_segments=N)
            agg = agg / jnp.maximum(deg, 1.0)[:, None]
            conv_out = jax.nn.relu(agg @ W_conv + b_conv)
            counts = jax.ops.segment_sum(jnp.ones((N,), jnp.int32), batch, num_segments=B)
            offsets = jnp.concatenate([jnp.zeros((1,), jnp.int32), jnp.cumsum(counts)[:-1]])
            pos = jnp.arange(N, dtype=jnp.int32) - offsets[batch]
            h_dense = jnp.zeros((B, MAXN, D), x.dtype).at[batch, pos].set(h)
            mask = jnp.zeros((B, MAXN), bool).at[batch, pos].set(True)

            def heads(t, W):
                return (t @ W).reshape(B, MAXN, HEADS, DH).transpose(0, 2, 1, 3)
            q, k, v = (heads(h_dense, Wq), heads(h_dense, Wk), heads(h_dense, Wv))
            scale = DH ** (-0.25)

            def phi(t, is_query):
                t = t * scale
                u = jnp.einsum('bhnd,md->bhnm', t, proj)
                diag = 0.5 * jnp.sum(t * t, axis=-1, keepdims=True)
                if is_query:
                    m_ = jnp.max(u, axis=-1, keepdims=True)
                else:
                    m_ = jnp.max(u, axis=(-2, -1), keepdims=True)
                return jnp.exp(u - diag - jax.lax.stop_gradient(m_)) / np.sqrt(M) + KEPS
            qf = phi(q, True)
            kf = phi(k, False) * mask[:, None, :, None]
            vm = v * mask[:, None, :, None]
            kv = jnp.einsum('bhnm,bhnd->bhmd', kf, vm)
            z = 1.0 / (jnp.einsum('bhnm,bhm->bhn', qf, kf.sum(axis=2)) + KEPS)
            attn = jnp.einsum('bhnm,bhmd->bhnd', qf, kv) * z[..., None]
            attn = attn.transpose(0, 2, 1, 3).reshape(B, MAXN, D) @ Wo
            h_attn = attn[batch, pos]
            return _batchnorm(conv_out + h_attn + h, norm2_g, norm2_b)
        return _forward(x, batch, edge_index, norm1_g, norm1_b, norm2_g, norm2_b, W_conv, b_conv, Wq, Wk, Wv, Wo, proj)
    edge_index = jnp.stack([src, dst])
    batch0 = jnp.zeros((10000,), jnp.int32)
    x = _layernorm(x + _L0_gnn_ref(x, batch0, edge_index, L0_gnn_W), axis=-1)
    x = _layernorm(x + _L1_gnn_ref(x, batch0, edge_index, L1_gnn_norm1_g, L1_gnn_norm1_b, L1_gnn_norm2_g, L1_gnn_norm2_b, L1_gnn_W_conv, L1_gnn_b_conv, L1_gnn_Wq, L1_gnn_Wk, L1_gnn_Wv, L1_gnn_Wo, L1_gnn_proj), axis=-1)
    return x

_drawn_inputs = setup_inputs


def setup_inputs(seed=0):
    import zlib

    import numpy as np

    out = dict(_drawn_inputs(seed))
    spreads = {'L1_gnn_norm1_g': (1.0, 0.2),
     'L1_gnn_norm1_b': (0.0, 0.359),
     'L1_gnn_norm2_g': (1.0, 0.2),
     'L1_gnn_norm2_b': (0.0, 0.1),
     'L1_gnn_b_conv': (0.0, 0.452)}
    factors = {'L1_gnn_Wq': 8.0, 'L1_gnn_Wk': 8.0, 'L1_gnn_Wv': 8.0, 'L1_gnn_Wo': 8.0, 'L1_gnn_proj': 8.0}
    for name, (base, spread) in spreads.items():
        noise = np.random.default_rng([zlib.crc32(name.encode()), seed]).standard_normal(out[name].shape)
        drawn = base * np.exp(spread * noise) if base else spread * noise
        out[name] = jnp.asarray(drawn.astype(out[name].dtype))
    for name, factor in factors.items():
        out[name] = (out[name] * factor).astype(out[name].dtype)
    return out
```

```python
from contextlib import ExitStack

import concourse.bass as bass
from concourse import mybir

F32 = mybir.dt.float32
F32R = mybir.dt.float32r
BF16 = mybir.dt.bfloat16
I32 = mybir.dt.int32
U32 = mybir.dt.uint32
ALU = mybir.AluOpType
ACT = mybir.ActivationFunctionType
AX = mybir.AxisListType

N = 10000
E = 10000
D = 512
H = 8
DH = D // H
KC = D // 128
ROWS = 125
T = N // ROWS
SLOTS = ROWS + 1
NEVER = 16384
BIG = 1e30
ROUND = 12582912.0
LN_EPS = 1e-5
BN_EPS = 1e-5
KEPS = 1e-6
MAXN = 64
M = 256

ds = bass.ds


class Semaphores:

    def __init__(self, nc, own):
        self.nc, self.own, self.numbers = nc, own, []
        own.callback(self.clear)

    def take(self, name):
        s = self.own.enter_context(self.nc.semaphore(name))
        self.numbers.append(s.num)
        return s

    def clear(self):
        numbers = sorted(self.numbers)
        with self.nc.Block() as block:
            @block.gpsimd
            def _(pool):
                lo = 0
                for k in range(1, len(numbers) + 1):
                    if k == len(numbers) or numbers[k] != numbers[k - 1] + 1:
                        pool.sem_clear(range(numbers[lo], numbers[k - 1] + 1))
                        lo = k


class Buffers:
    pass


def lasting_constants(nc, ctx):
    c = Buffers()
    c.ident = ctx.enter_context(nc.sbuf_tensor("ident", [128, 128], F32))
    c.ones = ctx.enter_context(nc.sbuf_tensor("ones", [128, 128], F32))
    c.ln_eps = ctx.enter_context(nc.sbuf_tensor("ln_eps", [128, 1], F32))
    c.pool_dma = lambda name: ctx.enter_context(nc.semaphore(name))
    return c


def make_constants(nc, ctx, c):

    def sb(name, shape, dt=F32):
        return ctx.enter_context(nc.sbuf_tensor(name, shape, dt))

    c.ramp_i = sb("ramp_i", [128, 128], I32)
    c.ramp = sb("ramp", [128, 128])
    c.row_i = sb("row_i", [128, 1], I32)
    c.row = sb("row", [128, 1])
    c.node_i = sb("node_i", [ROWS, T], I32)
    c.node = sb("node", [ROWS, T])
    c.before = sb("before", [128, 128])
    c.upper = sb("upper", [128, 128])
    c.shift = sb("shift", [SLOTS, SLOTS])
    c.wrap = sb("wrap", [SLOTS, SLOTS])
    c.keep = sb("keep", [SLOTS, SLOTS])
    c.lift = sb("lift", [SLOTS, SLOTS])
    c.zeros = sb("zeros", [128, 512])
    semaphores = Semaphores(nc, ctx)
    made = semaphores.take("constants_made")
    cleared = semaphores.take("constants_cleared")
    ramps = semaphores.take("ramps_made")

    with nc.Block() as block:
        @block.gpsimd
        def _(pool):
            g = nc.gpsimd
            g.iota(c.ramp_i[:, :], [[1, 128]], base=0, channel_multiplier=0).then_inc(ramps, 1)
            g.iota(c.row_i[:, :], [[0, 1]], base=0, channel_multiplier=1).then_inc(ramps, 1)
            g.iota(c.node_i[:, :], [[ROWS, T]], base=0, channel_multiplier=1).then_inc(ramps, 1)
            pool.wait_ge(cleared, 7)
            for mat, size, base in ((c.ident, 128, 0), (c.shift, SLOTS, -1)):
                g.affine_select(out=mat[0:size, 0:size], in_=mat[0:size, 0:size], compare_op=ALU.not_equal,
                                fill=1.0, base=-base, pattern=[[-1, size]], channel_multiplier=1).then_inc(made, 1)
            g.affine_select(out=c.keep[:, :], in_=c.keep[:, :], compare_op=ALU.not_equal, fill=1.0,
                            base=0, pattern=[[-1, SLOTS]], channel_multiplier=1).then_inc(made, 1)
            g.affine_select(out=c.before[:, :], in_=c.ones[:, :], compare_op=ALU.is_gt, fill=0.0,
                            base=0, pattern=[[-1, 128]], channel_multiplier=1).then_inc(made, 1)
            g.affine_select(out=c.upper[:, :], in_=c.ones[:, :], compare_op=ALU.is_gt, fill=0.0,
                            base=0, pattern=[[1, 128]], channel_multiplier=-1).then_inc(made, 1)
            g.affine_select(out=c.wrap[:, :], in_=c.wrap[:, :], compare_op=ALU.not_equal, fill=1.0,
                            base=-(ROWS * 128 + 1), pattern=[[1, SLOTS]], channel_multiplier=128).then_inc(made, 1)
            g.affine_select(out=c.lift[:, :], in_=c.lift[:, :], compare_op=ALU.not_equal, fill=1.0,
                            base=-128, pattern=[[1, SLOTS]], channel_multiplier=128).then_inc(made, 1)

        @block.vector
        def _(dve):
            v = nc.vector
            for mat in (c.ident, c.shift, c.keep, c.wrap, c.lift, c.zeros):
                v.memset(mat[:, :], 0.0).then_inc(cleared, 1)
            v.memset(c.ones[:, :], 1.0).then_inc(cleared, 1)
            v.memset(c.ln_eps[:, :], LN_EPS)
            dve.wait_ge(ramps, 3)
            v.tensor_copy(c.ramp[:, :], c.ramp_i[:, :])
            v.tensor_copy(c.row[:, :], c.row_i[:, :])
            v.tensor_copy(c.node[:, :], c.node_i[:, :])
            dve.wait_ge(made, 7)
            v.memset(c.keep[0:1, 0:1], 0.0)
            v.memset(c.shift[0:1, 0:2], 0.0)


def pairs(eng, body):
    body(0)
    with eng.Fori(1, T // 2) as i:
        body(i)


def divide(v, dve, link, out, x, rows):
    link(v.tensor_scalar(out[0:rows, :], x[0:rows, :], -62.0, 1.0 / ROWS, ALU.add, ALU.mult))
    link(v.tensor_scalar(out[0:rows, :], out[0:rows, :], ROUND, None, ALU.add))
    link(v.tensor_scalar(out[0:rows, :], out[0:rows, :], -ROUND, None, ALU.add))


def edge_tables(nc, ctx, tag, brief):
    o = Buffers()

    def keep(name, shape, dt=F32):
        return ctx.enter_context(nc.sbuf_tensor(f"{tag}_{name}", shape, dt))

    def only_full(*a):
        return None if brief else keep(*a)

    o.key_row = only_full("key_row", [SLOTS, T], U32)
    o.val_row = keep("val_row", [SLOTS, T], U32)
    o.first_row = only_full("first_row", [SLOTS, T], U32)
    o.first = only_full("first", [SLOTS, T])
    o.key_in = keep("key_in", [SLOTS, T])
    o.key_out = keep("key_out", [SLOTS, T])
    o.cut = only_full("cut", [SLOTS, T])
    o.empty = only_full("empty", [ROWS, T])
    o.empty_row = only_full("empty_row", [SLOTS, T], U32)
    o.has = keep("has", [ROWS, T])
    o.inverse = keep("inverse", [SLOTS, T])
    o.sum_row = keep("sum_row", [SLOTS, T], U32)
    return o


def sort_edges(nc, c, tag, o, key_d, val_d):
    with ExitStack() as own:
        semaphores = Semaphores(nc, own)
        def sb(name, shape, dt=F32):
            return own.enter_context(nc.sbuf_tensor(f"{tag}_{name}", shape, dt))

        def pb(name, shape):
            return own.enter_context(nc.psum_tensor(f"{tag}_{name}", shape, F32))

        def sem(name):
            return semaphores.take(f"{tag}_{name}")

        key_i = sb("key_i", [ROWS, T], I32)
        val_i = sb("val_i", [ROWS, T], I32)
        digits = sb("digits", [ROWS, T, 2])
        key = sb("key", [ROWS, T])
        key_tile = sb("key_tile", [ROWS, T])
        key_slot = sb("key_slot", [ROWS, T])
        key1 = sb("key1", [ROWS, T])
        val1 = sb("val1", [ROWS, T])
        slot_hot = [sb(f"slot_hot{u}", [ROWS, ROWS], BF16) for u in range(2)]
        tile_hot = [sb(f"tile_hot{u}", [ROWS, T], BF16) for u in range(2)]
        counts = sb("counts", [ROWS, T, T])
        summed = sb("summed", [ROWS, T, T])
        base = sb("base", [ROWS, 1])
        column = [sb(f"column{u}", [ROWS, 2]) for u in range(2)]
        slot_hot_t = [sb(f"slot_hot_t{u}", [ROWS, ROWS]) for u in range(2)]
        junk = [sb(f"junk{u}", [ROWS, ROWS]) for u in range(2)]
        junk2 = [sb(f"junk2{u}", [ROWS, T]) for u in range(2)]
        rank = sb("rank", [ROWS, T])
        start = sb("start", [ROWS, T])
        pos = sb("pos", [ROWS, T])
        pos_tile = sb("pos_tile", [ROWS, T])
        pos_slot = sb("pos_slot", [ROWS, T])
        out_hot = [sb(f"out_hot{u}", [ROWS, SLOTS]) for u in range(2)]
        payload = [sb(f"payload{u}", [ROWS, 2, T]) for u in range(2)]
        ks = sb("ks", [SLOTS, T + 2])
        vs = sb("vs", [SLOTS, T])
        same = sb("same", [SLOTS, T])
        tmp = sb("tmp", [SLOTS, T])
        tmp_i = sb("tmp_i", [SLOTS, T], I32)
        node_cnt, empty = sb("node_cnt", [ROWS, T]), sb("empty_", [ROWS, T])

        hist = [pb(f"hist{u}", [ROWS, 512]) for u in range(2)]
        rows_p = [pb(f"rows_p{u}", [ROWS, 512]) for u in range(2)]
        look = [pb(f"look{u}", [ROWS, 512]) for u in range(2)]
        sorted_p = pb("sorted_p", [SLOTS, 512])
        edge_p = pb("edge_p", [SLOTS, 512])

        loaded = sem("loaded")
        chain = sem("chain")
        hot_ready = [sem(f"hot_ready{u}") for u in range(2)]
        hist_ready = [sem(f"hist_ready{u}") for u in range(2)]
        hist_kept = [sem(f"hist_kept{u}") for u in range(2)]
        base_asked = sem("base_asked")
        base_ready = sem("base_ready")
        starts_ready = sem("starts_ready")
        column_ready = [sem(f"column_ready{u}") for u in range(2)]
        rows_ready = [sem(f"rows_ready{u}") for u in range(2)]
        hot_t_ready = [sem(f"hot_t_ready{u}") for u in range(2)]
        ranked = [sem(f"ranked{u}") for u in range(2)]
        look_ready = [sem(f"look_ready{u}") for u in range(2)]
        looked = [sem(f"looked{u}") for u in range(2)]
        payload_ready = [sem(f"payload_ready{u}") for u in range(2)]
        payload_used = [sem(f"payload_used{u}") for u in range(2)]
        sorted_ready = sem("sorted_ready")
        sorted_kept = sem("sorted_kept")
        edges_ready = sem("edges_ready")
        tidy = sem("tidy")

        with nc.Block() as block:
            @block.sync
            def _(sp):
                sp.dma_start(key_i[:, :], key_d.rearrange("(p t) -> p t", t=T)).then_inc(loaded, 16)
                sp.dma_start(val_i[:, :], val_d.rearrange("(p t) -> p t", t=T)).then_inc(loaded, 16)

            @block.vector
            def _(dve):
                v = nc.vector
                done = [0]

                def link(ins):
                    done[0] += 1
                    ins.then_inc(chain, 1)
                    dve.wait_ge(chain, done[0])

                dve.wait_ge(loaded, 32)
                v.tensor_copy(key[:, :], key_i[:, :])
                link(v.tensor_copy(val1[:, :], val_i[:, :]))
                v.tensor_scalar(key1[:, :], key[:, :], 1.0, None, ALU.add)
                link(v.tensor_scalar(val1[:, :], val1[:, :], 1.0, None, ALU.add))
                divide(v, dve, link, key_tile, key, ROWS)
                link(v.scalar_tensor_tensor(key_slot[:, :], key_tile[:, :], -float(ROWS), key[:, :],
                                            ALU.mult, ALU.add))
                v.tensor_copy(digits[:, :, 0], key[:, :])
                link(v.tensor_copy(digits[:, :, 1], key_slot[:, :]))

                def one_hot(i):
                    for u in range(2):
                        dve.wait_ge(hist_ready[u], i)
                        v.tensor_scalar(slot_hot[u][:, :], c.ramp[0:ROWS, 0:ROWS],
                                        key_slot[:, ds(2 * i + u, 1)], None, ALU.is_equal)
                        v.tensor_scalar(tile_hot[u][:, :], c.ramp[0:ROWS, 0:T],
                                        key_tile[:, ds(2 * i + u, 1)], None,
                                        ALU.is_equal).then_inc(hot_ready[u], 1)
                pairs(dve, one_hot)
                for u in range(2):
                    dve.wait_ge(hist_kept[u], T // 2)
                link(v.tensor_tensor_scan(summed[:, :, :].rearrange("p a t -> p (a t)"),
                                          counts[:, :, :].rearrange("p a t -> p (a t)"),
                                          counts[:, :, :].rearrange("p a t -> p (a t)"),
                                          0.0, ALU.add, ALU.bypass))
                v.memset(ks[:, :], 0.0).then_inc(base_asked, 1)
                dve.wait_ge(base_ready, 1)
                link(v.tensor_copy(base[:, :], edge_p[0:ROWS, 0:1]))
                link(v.tensor_scalar(node_cnt[:, :], summed[:, :, T - 1], base[:, :], None, ALU.add))
                v.scalar_tensor_tensor(counts[:, :, :].rearrange("p a t -> p (a t)"),
                                       summed[:, :, :].rearrange("p a t -> p (a t)"), base[:, :],
                                       counts[:, :, :].rearrange("p a t -> p (a t)"),
                                       ALU.add, ALU.subtract).then_inc(starts_ready, 1)
                dve.wait_ge(starts_ready, 1)
                link(v.tensor_tensor(node_cnt[:, :], node_cnt[:, :], counts[:, :, 0], ALU.subtract))
                link(v.tensor_scalar(o.has[:, :], node_cnt[:, :], 1.0, None, ALU.min))
                link(v.tensor_scalar(empty[:, :], o.has[:, :], -1.0, 1.0, ALU.mult, ALU.add))
                link(v.tensor_scalar(tmp[0:ROWS, :], node_cnt[:, :], 1.0, None, ALU.max))
                link(v.memset(o.inverse[:, :], 0.0))
                link(v.reciprocal(tmp[0:ROWS, :], tmp[0:ROWS, :]))
                link(v.tensor_tensor(o.inverse[0:ROWS, :], tmp[0:ROWS, :], o.has[:, :], ALU.mult))
                link(v.memset(tmp_i[:, :], NEVER))
                if o.empty_row is not None:
                    v.tensor_copy(o.empty[:, :], empty[:, :])
                    link(v.scalar_tensor_tensor(tmp_i[0:ROWS, :], o.has[:, :], float(NEVER), c.node[:, :],
                                                ALU.mult, ALU.add))
                    link(v.tensor_copy(o.empty_row[:, :], tmp_i[:, :]))
                link(v.tensor_copy(start[:, :], counts[:, :, 0]))
                divide(v, dve, link, pos_tile, start, ROWS)
                link(v.scalar_tensor_tensor(start[:, :], start[:, :], 1.0, pos_tile[:, :], ALU.add, ALU.add))
                link(v.scalar_tensor_tensor(start[:, :], empty[:, :], float(NEVER), start[:, :],
                                            ALU.mult, ALU.add))
                link(v.tensor_copy(tmp_i[0:ROWS, :], start[:, :]))
                link(v.tensor_copy(o.sum_row[:, :], tmp_i[:, :]))

                def place(i, u):
                    dve.wait_ge(look_ready[u], i + 1)
                    v.scalar_tensor_tensor(junk2[u][:, :], c.ramp[0:ROWS, 0:T],
                                           key_tile[:, ds(2 * i + u, 1)], look[u][:, 0:T],
                                           ALU.is_equal, ALU.mult,
                                           accum_out=start[:, ds(2 * i + u, 1)]).then_inc(looked[u], 1)

                def place_edges(i):
                    for u in range(2):
                        dve.wait_ge(rows_ready[u], i)
                        v.tensor_copy(column[u][:, :], digits[:, ds(2 * i + u, 1), :]
                                      .rearrange("p a b -> p (a b)")).then_inc(column_ready[u], 1)
                    for u in range(2):
                        dve.wait_ge(rows_ready[u], i + 1)
                        dve.wait_ge(look_ready[u], i)
                        v.tensor_scalar(slot_hot_t[u][:, :], rows_p[u][:, ROWS:2 * ROWS], c.row[0:ROWS, :],
                                        None, ALU.is_equal).then_inc(hot_t_ready[u], 1)
                        dve.wait_ge(ranked[u], i)
                        v.scalar_tensor_tensor(junk[u][:, :], rows_p[u][:, 0:ROWS],
                                               digits[:, ds(2 * i + u, 1), 0:1].rearrange("p a b -> p (a b)"),
                                               c.before[0:ROWS, 0:ROWS], ALU.is_equal, ALU.mult,
                                               accum_out=rank[:, ds(2 * i + u, 1)]).then_inc(ranked[u], 1)
                    for u in range(2):
                        dve.wait_ge(looked[u], i)
                        place(i, u)
                pairs(dve, place_edges)
                for u in range(2):
                    dve.wait_ge(looked[u], T // 2)
                    dve.wait_ge(ranked[u], T // 2)
                link(v.tensor_tensor(pos[:, :], start[:, :], rank[:, :], ALU.add))
                divide(v, dve, link, pos_tile, pos, ROWS)
                link(v.scalar_tensor_tensor(pos_slot[:, :], pos_tile[:, :], -float(ROWS), pos[:, :],
                                            ALU.mult, ALU.add))
                link(v.tensor_scalar(pos_slot[:, :], pos_slot[:, :], 1.0, None, ALU.add))
                def permute(i):
                    for u in range(2):
                        t = 2 * i + u
                        dve.wait_ge(payload_used[u], i)
                        v.tensor_scalar(out_hot[u][:, :], c.ramp[0:ROWS, 0:SLOTS], pos_slot[:, ds(t, 1)],
                                        None, ALU.is_equal)
                        v.tensor_scalar(payload[u][:, 0, :], c.ramp[0:ROWS, 0:T], pos_tile[:, ds(t, 1)],
                                        key1[:, ds(t, 1)], ALU.is_equal, ALU.mult)
                        v.tensor_scalar(payload[u][:, 1, :], c.ramp[0:ROWS, 0:T], pos_tile[:, ds(t, 1)],
                                        val1[:, ds(t, 1)], ALU.is_equal, ALU.mult).then_inc(payload_ready[u], 1)
                pairs(dve, permute)
                dve.wait_ge(sorted_ready, 1)
                v.memset(ks[:, 0:1], -1.0)
                v.memset(ks[:, T + 1:T + 2], -2.0)
                v.tensor_copy(ks[:, 1:T + 1], sorted_p[:, 0:T]).then_inc(sorted_kept, 1)
                link(v.tensor_copy(vs[:, :], sorted_p[:, T:2 * T]))
                link(v.tensor_scalar(tmp[:, :], vs[:, :], -1.0, 0.0, ALU.add, ALU.max))
                link(v.tensor_copy(tmp_i[:, :], tmp[:, :]))
                link(v.tensor_copy(o.val_row[:, :], tmp_i[:, :]))
                dve.wait_ge(sorted_kept, 1)
                link(v.tensor_scalar(tmp[:, :], ks[:, 1:T + 1], -1.0, 0.0, ALU.add, ALU.max))
                link(v.tensor_copy(tmp_i[:, :], tmp[:, :]))
                if o.key_row is not None:
                    link(v.tensor_copy(o.key_row[:, :], tmp_i[:, :]))
                dve.wait_ge(edges_ready, 1)
                v.tensor_copy(o.key_in[:, :], edge_p[:, T:2 * T])
                v.tensor_copy(o.key_out[:, :], edge_p[:, 2 * T:3 * T])
                if o.first is not None:
                    link(v.tensor_tensor(same[:, :], ks[:, 1:T + 1], edge_p[:, 0:T], ALU.is_equal))
                    v.tensor_scalar(o.first[:, :], same[:, :], -1.0, 1.0, ALU.mult, ALU.add)
                    v.tensor_scalar(o.cut[:, :], same[:, :], -1.0, BIG, ALU.add, ALU.mult)
                    link(v.scalar_tensor_tensor(tmp_i[:, :], same[:, :], float(NEVER), tmp[:, :],
                                                ALU.mult, ALU.add))
                    v.tensor_copy(o.first_row[:, :], tmp_i[:, :])

            @block.scalar
            def _(act):
                def keep_counts(i):
                    for u in range(2):
                        act.wait_ge(hist_ready[u], i + 1)
                        nc.scalar.activation(counts[:, :, ds(2 * i + u, 1)].rearrange("p a b -> p (a b)"),
                                             hist[u][:, 0:T], ACT.Copy).then_inc(hist_kept[u], 1)
                pairs(act, keep_counts)

            @block.tensor
            def _(pe):
                t_ = nc.tensor
                def count(i):
                    for u in range(2):
                        pe.wait_ge(hist_kept[u], i)
                        pe.wait_ge(hot_ready[u], i + 1)
                        t_.matmul(hist[u][:, 0:T], slot_hot[u][:, :], tile_hot[u][:, :],
                                  start=True, stop=True).then_inc(hist_ready[u], 1)
                pairs(pe, count)
                pe.wait_ge(base_asked, 1)
                t_.matmul(edge_p[0:ROWS, 0:1], c.upper[0:ROWS, 0:ROWS],
                          summed[:, T - 1, T - 1:T], start=True, stop=True).then_inc(base_ready, 1)
                pe.wait_ge(starts_ready, 1)
                def look_up(i):
                    for u in range(2):
                        pe.wait_ge(column_ready[u], i + 1)
                        pe.wait_ge(ranked[u], i)
                        pe.wait_ge(hot_t_ready[u], i)
                        t_.matmul(rows_p[u][:, 0:ROWS], column[u][:, 0:1].to_broadcast([ROWS, ROWS]),
                                  c.ident[0:ROWS, 0:ROWS], start=True, stop=True)
                        t_.matmul(rows_p[u][:, ROWS:2 * ROWS], column[u][:, 1:2].to_broadcast([ROWS, ROWS]),
                                  c.ident[0:ROWS, 0:ROWS], start=True, stop=True).then_inc(rows_ready[u], 1)
                    for u in range(2):
                        pe.wait_ge(looked[u], i)
                        pe.wait_ge(hot_t_ready[u], i + 1)
                        t_.matmul(look[u][:, 0:T], slot_hot_t[u][:, :],
                                  counts[:, :, ds(2 * i + u, 1)].rearrange("p a b -> p (a b)"),
                                  start=True, stop=True).then_inc(look_ready[u], 1)
                pairs(pe, look_up)
                t_.matmul(sorted_p[:, 0:2 * T], c.zeros[:, 0:SLOTS], c.zeros[:, 0:2 * T], start=True, stop=False)
                def gather_permuted(i):
                    for u in range(2):
                        pe.wait_ge(payload_ready[u], i + 1)
                        t_.matmul(sorted_p[:, 0:2 * T], out_hot[u][:, :],
                                  payload[u][:, :, :].rearrange("p a b -> p (a b)"),
                                  start=False, stop=False).then_inc(payload_used[u], 1)
                pairs(pe, gather_permuted)
                t_.matmul(sorted_p[:, 0:2 * T], c.zeros[:, 0:SLOTS], c.zeros[:, 0:2 * T],
                          start=False, stop=True).then_inc(sorted_ready, 1)
                pe.wait_ge(sorted_kept, 1)
                t_.matmul(edge_p[:, 0:T], c.shift[:, :], ks[:, 1:T + 1], start=True, stop=False)
                t_.matmul(edge_p[:, 0:T], c.wrap[:, :], ks[:, 0:T], start=False, stop=True)
                t_.matmul(edge_p[:, T:2 * T], c.keep[:, :], ks[:, 1:T + 1], start=True, stop=False)
                t_.matmul(edge_p[:, T:2 * T], c.lift[:, :], ks[:, 2:T + 2], start=False, stop=True)
                t_.matmul(edge_p[:, 2 * T:3 * T], c.keep[:, :], ks[:, 1:T + 1], start=True, stop=False)
                t_.matmul(edge_p[:, 2 * T:3 * T], c.lift[:, :], ks[:, 1:T + 1],
                          start=False, stop=True).then_inc(edges_ready, 1)
    return o


def settle(eng):
    eng.nop(nofuse=True)


class Tile:

    def __init__(self, period, i, c):
        self.period, self.i, self.c = period, i, c
        self.par = c % period
        self.turn = i + c // period
        self.num = period * i + c

    def before(self, n=1):
        return Tile(self.period, self.i, self.c - n)

    def after(self):
        return Tile(self.period, self.i, self.c + 1)

    def is_last(self):
        return isinstance(self.i, int) and self.num == T - 1

    def is_zero(self):
        return isinstance(self.i, int) and self.num == 0


def sweep(eng, body, period, ahead, behind):
    lo = 1 - (-behind // period)
    hi = (T - ahead) // period

    def fixed(s):
        def at(k):
            return Tile(period, 0, s + k) if 0 <= s + k < T else None
        body(at)

    for s in range(-ahead, lo * period):
        fixed(s)
    with eng.Fori(lo, hi) as i:
        for c in range(period):
            body(lambda k, c=c: Tile(period, i, c + k))
    for s in range(hi * period, T + behind):
        fixed(s)


class Chain:

    def __init__(self, eng, sem, each):
        self.eng, self.sem, self.each = eng, sem, each

    def at(self, x):
        k = [0]

        def link(ins):
            k[0] += 1
            ins.then_inc(self.sem, 1)
            self.eng.wait_ge(self.sem, self.each * x.num + k[0])
        return link


ROWS_CUT = ((0, 112), (112, ROWS))
TABLES = "natural_log_exp_and_others"


def split_weights(nc, ctx, semaphores, name, w_d, lo_col, hi_col):
    n = hi_col - lo_col
    hi = ctx.enter_context(nc.sbuf_tensor(f"{name}_hi", [128, KC, n], F32R))
    lo = ctx.enter_context(nc.sbuf_tensor(f"{name}_lo", [128, KC, n], F32R))
    with nc.sbuf_tensor(f"{name}_raw", [128, KC, n], F32) as raw, \
            nc.Block() as block:
        loaded, high = semaphores.take(f"{name}_loaded"), semaphores.take(f"{name}_high")

        @block.sync
        def _(sp):
            sp.dma_start(raw[:, :, :], w_d.rearrange("(k p) n -> p k n", p=128)[:, :, lo_col:hi_col]) \
                .then_inc(loaded, 16)

        @block.scalar
        def _(act):
            act.wait_ge(loaded, 16)
            nc.scalar.copy(hi[:, :, :], raw[:, :, :]).then_inc(high, 1)

        @block.vector
        def _(dve):
            dve.wait_ge(high, 1)
            nc.vector.tensor_tensor(lo[:, :, :], raw[:, :, :], hi[:, :, :].bitcast(F32), ALU.subtract)
    return hi, lo


def product(t, out, x_hi, x_lo, w_hi, w_lo, rows):
    for k in range(KC):
        xh = x_hi[:, k * rows:(k + 1) * rows]
        t.matmul(out, xh, w_hi[:, k, :], start=(k == 0), stop=False)
        t.matmul(out, xh, w_lo[:, k, :], start=False, stop=False)
        last = t.matmul(out, x_lo[:, k * rows:(k + 1) * rows], w_hi[:, k, :], start=False, stop=(k == KC - 1))
    return last


def edge_scores(nc, ctx, c, s, x_d, w_d, x1_d, acc):
    o = Buffers()
    o.aw = ctx.enter_context(nc.sbuf_tensor("aw_all", [H, E], F32))
    o.cut = ctx.enter_context(nc.sbuf_tensor("cut_all", [H, E + 1], BF16))
    o.run_max = ctx.enter_context(nc.sbuf_tensor("run_max", [H, E + 1], F32))
    with ExitStack() as own:
        semaphores = Semaphores(nc, own)
        def sb(name, shape, dt=F32):
            return own.enter_context(nc.sbuf_tensor(f"a_{name}", shape, dt))

        def pb(name, shape):
            return own.enter_context(nc.psum_tensor(f"a_{name}", shape, F32))

        def sem(name):
            return semaphores.take(f"a_{name}")

        def two(make, name, *a):
            return [make(f"{name}{u}", *a) for u in range(2)]

        wq = split_weights(nc, own, semaphores, "wq", w_d, 0, D)
        wk = split_weights(nc, own, semaphores, "wk", w_d, D, 2 * D)

        src_idx, dst_idx = two(sb, "src_idx", [SLOTS, 1], U32), two(sb, "dst_idx", [SLOTS, 1], U32)
        empty_idx = two(sb, "empty_idx", [SLOTS, 1], U32)
        xs, xd = two(sb, "xs", [SLOTS, D]), two(sb, "xd", [SLOTS, D])
        xs_hi, xs_lo = two(sb, "xs_hi", [128, KC * SLOTS], F32R), two(sb, "xs_lo", [128, KC * SLOTS], F32R)
        xd_hi, xd_lo = two(sb, "xd_hi", [128, KC * SLOTS], F32R), two(sb, "xd_lo", [128, KC * SLOTS], F32R)
        q = two(sb, "q", [SLOTS, D])
        qk = two(sb, "qk", [SLOTS, D])
        aw_col, cut_col = two(sb, "aw_col", [SLOTS, H]), two(sb, "cut_col", [SLOTS, H])
        xn = two(sb, "xn", [ROWS, D])
        x1n = two(sb, "x1n", [SLOTS, D])
        sq = two(sb, "sq", [ROWS, D])
        stats, moments = two(sb, "stats", [ROWS, 6]), two(sb, "moments", [ROWS, 2])
        logv, rstd, shift = two(sb, "logv", [ROWS, 1]), two(sb, "rstd", [ROWS, 1]), two(sb, "shift", [ROWS, 1])

        turned_s, turned_d = pb("turned_s", [128, 512]), pb("turned_d", [128, 512])
        q_p, k_p = two(pb, "q_p", [SLOTS, 512]), two(pb, "k_p", [SLOTS, 512])
        score_p = two(pb, "score_p", [H, 512])

        cleared = sem("cleared")
        idx_ready = two(sem, "idx_ready")
        xs_in, xd_in = two(c.pool_dma, "a_xs_in"), two(c.pool_dma, "a_xd_in")
        turned_s_ready, turned_d_ready = two(sem, "turned_s_ready"), two(sem, "turned_d_ready")
        hi_s_ready, hi_d_ready = two(sem, "hi_s_ready"), two(sem, "hi_d_ready")
        lo_s_ready, lo_d_ready = two(sem, "lo_s_ready"), two(sem, "lo_d_ready")
        q_ready, k_ready, q_kept = two(sem, "q_ready"), two(sem, "k_ready"), two(sem, "q_kept")
        prod_ready, aw_ready = two(sem, "prod_ready"), two(sem, "aw_ready")
        score_ready, scanned = two(sem, "score_ready"), two(sem, "scanned")
        xn_in, stats_ready, moments_ready = two(sem, "xn_in"), two(sem, "stats_ready"), two(sem, "moments_ready")
        log_ready, rstd_ready, shift_ready = two(sem, "log_ready"), two(sem, "rstd_ready"), two(sem, "shift_ready")
        x1n_ready, sq_ready = two(sem, "x1n_ready"), two(sem, "sq_ready")
        summed, summed_sq = two(sem, "summed"), two(sem, "summed_sq")
        cut_kept = sem("cut_kept")
        empty_idx_ready, x1n_out = two(sem, "empty_idx_ready"), two(c.pool_dma, "a_x1n_out")

        AHEAD, BEHIND = 2, 2
        with nc.Block() as block:
            @block.sync
            def _(sp):
                def load_nodes(x):
                    sp.wait_ge(x1n_ready[x.par], x.turn)
                    sp.wait_ge(stats_ready[x.par], x.turn)
                    for a, b in ROWS_CUT:
                        sp.dma_start(xn[x.par][a:b, :], x_d[ds(ROWS * x.num + a, b - a), :]) \
                            .then_inc(xn_in[x.par], 16)

                def body(at):
                    if x := at(2):
                        load_nodes(x)
                sweep(sp, body, 2, AHEAD, BEHIND)

            @block.gpsimd
            def _(pool):
                g = nc.gpsimd

                def gather(x):
                    p = x.par
                    pool.wait_ge(turned_s_ready[p], x.turn)
                    pool.wait_ge(turned_d_ready[p], x.turn)
                    g.tensor_copy(src_idx[p][:, :], s.key_row[:, ds(x.num, 1)])
                    g.tensor_copy(dst_idx[p][:, :], s.val_row[:, ds(x.num, 1)]).then_inc(idx_ready[p], 1)
                    pool.wait_ge(idx_ready[p], x.turn + 1)
                    settle(pool)
                    g.indirect_dma_start(xs[p][:, :], None, x_d, bass.IndirectOffsetOnAxis(src_idx[p][:, :], 0)) \
                        .then_inc(xs_in[p], 16)
                    settle(pool)
                    g.indirect_dma_start(xd[p][:, :], None, x_d, bass.IndirectOffsetOnAxis(dst_idx[p][:, :], 0)) \
                        .then_inc(xd_in[p], 16)

                def scatter_empty(x):
                    p = x.par
                    pool.wait_ge(x1n_out[p], 16 * x.turn)
                    g.tensor_copy(empty_idx[p][:, :], s.empty_row[:, ds(x.num, 1)]).then_inc(empty_idx_ready[p], 1)
                    pool.wait_ge(empty_idx_ready[p], x.turn + 1)
                    pool.wait_ge(x1n_ready[p], x.turn + 1)
                    settle(pool)
                    g.indirect_dma_start(x1_d, bass.IndirectOffsetOnAxis(empty_idx[p][:, :], 0), x1n[p][:, :], None,
                                         bounds_check=N - 1, oob_is_err=False).then_inc(x1n_out[p], 16)

                pool.wait_ge(cleared, 1)
                def body(at):
                    if x := at(2):
                        gather(x)
                    if x := at(-1):
                        scatter_empty(x)
                sweep(pool, body, 2, AHEAD, BEHIND)
                for u in range(2):
                    pool.wait_ge(x1n_out[u], 16 * (T // 2))

            @block.tensor
            def _(pe):
                t_ = nc.tensor

                def turn(x):
                    p = x.par
                    for x_in, rows, out, lo_ready, ready in (
                            (xs_in, xs, turned_s, lo_s_ready, turned_s_ready),
                            (xd_in, xd, turned_d, lo_d_ready, turned_d_ready)):
                        pe.wait_ge(x_in[p], 16 * (x.turn + 1))
                        if not x.is_zero():
                            b = x.before()
                            pe.wait_ge(lo_ready[b.par], b.turn + 1)
                        for k in range(KC):
                            last = t_.transpose(out[:, k * SLOTS:(k + 1) * SLOTS],
                                                rows[p][:, k * 128:(k + 1) * 128], c.ident[0:SLOTS, 0:SLOTS])
                        last.then_inc(ready[p], 1)

                def query(x):
                    p = x.par
                    pe.wait_ge(hi_s_ready[p], x.turn + 1)
                    pe.wait_ge(lo_s_ready[p], x.turn + 1)
                    pe.wait_ge(q_kept[p], x.turn)
                    product(t_, q_p[p][:, 0:D], xs_hi[p], xs_lo[p], *wq, SLOTS).then_inc(q_ready[p], 1)

                def keys(x):
                    p = x.par
                    pe.wait_ge(hi_d_ready[p], x.turn + 1)
                    pe.wait_ge(lo_d_ready[p], x.turn + 1)
                    pe.wait_ge(prod_ready[p], x.turn)
                    product(t_, k_p[p][:, 0:D], xd_hi[p], xd_lo[p], *wk, SLOTS).then_inc(k_ready[p], 1)

                def scores(x):
                    p = x.par
                    pe.wait_ge(aw_ready[p], x.turn + 1)
                    pe.wait_ge(scanned[p], x.turn)
                    t_.transpose(score_p[p][:, 0:SLOTS], aw_col[p][:, :], c.ident[0:SLOTS, 0:SLOTS])
                    t_.transpose(score_p[p][:, SLOTS:2 * SLOTS], cut_col[p][:, :], c.ident[0:SLOTS, 0:SLOTS]) \
                        .then_inc(score_ready[p], 1)

                def body(at):
                    if x := at(1):
                        turn(x)
                    if x := at(0):
                        query(x)
                    if x := at(-1):
                        scores(x)
                    if x := at(0):
                        keys(x)
                sweep(pe, body, 2, AHEAD, BEHIND)

            @block.scalar
            def _(act):
                a = nc.scalar
                a.preload_act_table_set(TABLES)

                def high(x):
                    p = x.par
                    act.wait_ge(turned_s_ready[p], x.turn + 1)
                    act.wait_ge(q_ready[p], x.turn)
                    a.copy(xs_hi[p][:, :], turned_s[:, 0:KC * SLOTS]).then_inc(hi_s_ready[p], 1)
                    act.wait_ge(turned_d_ready[p], x.turn + 1)
                    act.wait_ge(k_ready[p], x.turn)
                    a.copy(xd_hi[p][:, :], turned_d[:, 0:KC * SLOTS]).then_inc(hi_d_ready[p], 1)

                def norm(x):
                    p = x.par
                    act.wait_ge(moments_ready[p], x.turn + 1)
                    a.activation(logv[p][:, :], moments[p][:, 1:2], ACT.Ln, bias=c.ln_eps[0:ROWS, :]) \
                        .then_inc(log_ready[p], 1)
                    act.wait_ge(log_ready[p], x.turn + 1)
                    a.activation(rstd[p][:, :], logv[p][:, :], ACT.Exp, scale=-0.5).then_inc(rstd_ready[p], 1)
                    act.wait_ge(shift_ready[p], x.turn + 1)
                    act.wait_ge(x1n_out[p], 16 * x.turn)
                    act.wait_ge(summed[p], x.turn)
                    a.activation(x1n[p][0:ROWS, :], xn[p][:, :], ACT.Identity, bias=shift[p][:, :],
                                 scale=rstd[p][:, :]).then_inc(x1n_ready[p], 1)
                    act.wait_ge(x1n_ready[p], x.turn + 1)
                    act.wait_ge(summed_sq[p], x.turn)
                    a.activation(sq[p][:, :], x1n[p][0:ROWS, :], ACT.Square).then_inc(sq_ready[p], 1)

                def keep_q(x):
                    p = x.par
                    act.wait_ge(q_ready[p], x.turn + 1)
                    act.wait_ge(prod_ready[p], x.turn)
                    a.mul(q[p][:, :], q_p[p][:, 0:D], DH ** -0.5).then_inc(q_kept[p], 1)

                act.wait_ge(cleared, 1)
                def body(at):
                    if x := at(1):
                        high(x)
                    if x := at(0):
                        norm(x)
                        keep_q(x)
                sweep(act, body, 2, AHEAD, BEHIND)

            @block.vector
            def _(dve):
                v = nc.vector
                v.memset(o.cut[:, E:E + 1], -BIG)
                v.memset(o.run_max[:, 0:1], -BIG)
                for u in range(2):
                    v.memset(x1n[u][:, :], 0.0)
                for m in acc:
                    v.memset(m[:, :], 0.0)
                v.memset(sq[0][:, 0:1], 0.0).then_inc(cleared, 1)
                dve.wait_ge(cleared, 1)

                def low(x):
                    p = x.par
                    for hi_ready, out, turned, hi, ready in ((hi_s_ready, xs_lo, turned_s, xs_hi, lo_s_ready),
                                                             (hi_d_ready, xd_lo, turned_d, xd_hi, lo_d_ready)):
                        dve.wait_ge(hi_ready[p], x.turn + 1)
                        v.tensor_tensor(out[p][:, :], turned[:, 0:KC * SLOTS], hi[p][:, :].bitcast(F32),
                                        ALU.subtract).then_inc(ready[p], 1)

                def measure(x):
                    p = x.par
                    dve.wait_ge(xn_in[p], 32 * (x.turn + 1))
                    dve.wait_ge(rstd_ready[p], x.turn)
                    v.bn_stats(stats[p][:, :], xn[p][:, :]).then_inc(stats_ready[p], 1)
                    dve.wait_ge(stats_ready[p], x.turn + 1)
                    settle(dve)
                    v.bn_aggr(moments[p][:, :], stats[p][:, :]).then_inc(moments_ready[p], 1)

                def centre(x):
                    p = x.par
                    dve.wait_ge(rstd_ready[p], x.turn + 1)
                    dve.wait_ge(moments_ready[p], x.turn + 1)
                    v.tensor_scalar(shift[p][:, :], moments[p][:, 0:1], -1.0, rstd[p][:, :], ALU.mult, ALU.mult) \
                        .then_inc(shift_ready[p], 1)

                def sum_up(x):
                    p, b = x.par, x.before()
                    dve.wait_ge(x1n_ready[p], x.turn + 1)
                    if not x.is_zero():
                        dve.wait_ge(summed[b.par], b.turn + 1)
                        dve.wait_ge(summed_sq[b.par], b.turn + 1)
                    v.scalar_tensor_tensor(acc[0][0:ROWS, :], x1n[p][0:ROWS, :], s.empty[:, ds(x.num, 1)],
                                           acc[0][0:ROWS, :], ALU.mult, ALU.add).then_inc(summed[p], 1)
                    dve.wait_ge(sq_ready[p], x.turn + 1)
                    v.scalar_tensor_tensor(acc[1][0:ROWS, :], sq[p][:, :], s.empty[:, ds(x.num, 1)],
                                           acc[1][0:ROWS, :], ALU.mult, ALU.add).then_inc(summed_sq[p], 1)

                def scan(x):
                    p = x.par
                    dve.wait_ge(score_ready[p], x.turn + 1)
                    v.tensor_copy(o.aw[:, ds(ROWS * x.num, ROWS)], score_p[p][:, 1:SLOTS])
                    v.tensor_copy(o.cut[:, ds(ROWS * x.num, ROWS)], score_p[p][:, SLOTS + 1:2 * SLOTS]) \
                        .then_inc(cut_kept, 1)
                    dve.wait_ge(cut_kept, x.num + 1)
                    if not x.is_zero():
                        b = x.before()
                        dve.wait_ge(scanned[b.par], b.turn + 1)
                    v.tensor_tensor_scan(o.run_max[:, ds(ROWS * x.num + 1, ROWS)], o.cut[:, ds(ROWS * x.num, ROWS)],
                                         score_p[p][:, 1:SLOTS], o.run_max[:, ds(ROWS * x.num, 1)],
                                         ALU.add, ALU.max).then_inc(scanned[p], 1)

                def score(x):
                    p = x.par
                    dve.wait_ge(score_ready[p], x.turn)
                    v.tensor_copy(cut_col[p][:, :], s.cut[:, ds(x.num, 1)].to_broadcast([SLOTS, H]))
                    dve.wait_ge(q_kept[p], x.turn + 1)
                    dve.wait_ge(k_ready[p], x.turn + 1)
                    dve.wait_ge(aw_ready[p], x.turn)
                    v.tensor_tensor(qk[p][:, :], q[p][:, :], k_p[p][:, 0:D], ALU.mult).then_inc(prod_ready[p], 1)
                    dve.wait_ge(prod_ready[p], x.turn + 1)
                    v.tensor_reduce(aw_col[p][:, :], qk[p][:, :].rearrange("p (h d) -> p h d", h=H),
                                    op=ALU.add, axis=AX.X).then_inc(aw_ready[p], 1)

                def body(at):
                    if x := at(1):
                        low(x)
                    if x := at(0):
                        measure(x)
                    if x := at(-2):
                        scan(x)
                    if x := at(-1):
                        sum_up(x)
                    if x := at(0):
                        centre(x)
                        score(x)
                sweep(dve, body, 2, AHEAD, BEHIND)
    return o


def attend_edges(nc, ctx, c, s, e, x_d, w_d, x1_d, acc):
    with ExitStack() as own:
        semaphores = Semaphores(nc, own)
        def sb(name, shape, dt=F32):
            return own.enter_context(nc.sbuf_tensor(f"b_{name}", shape, dt))

        def pb(name, shape):
            return own.enter_context(nc.psum_tensor(f"b_{name}", shape, F32))

        def sem(name):
            return semaphores.take(f"b_{name}")

        def two(make, name, *a):
            return [make(f"{name}{u}", *a) for u in range(2)]

        wv = split_weights(nc, own, semaphores, "wv", w_d, 2 * D, 3 * D)

        dst_idx, res_idx, out_idx = (two(sb, n, [SLOTS, 1], U32) for n in ("dst_idx", "res_idx", "out_idx"))
        xd, xr = two(sb, "xd", [SLOTS, D]), two(sb, "xr", [SLOTS, D])
        xd_hi, xd_lo = two(sb, "xd_hi", [128, KC * SLOTS], F32R), two(sb, "xd_lo", [128, KC * SLOTS], F32R)
        top = two(sb, "top", [H, SLOTS])
        gap = two(sb, "gap", [H, ROWS])
        cut_next, run_max = two(sb, "cut_next", [H, ROWS]), two(sb, "run_max", [H, ROWS])
        prob = two(sb, "prob", [H, SLOTS])
        key_col = two(sb, "key_col", [SLOTS, 1])
        group = two(sb, "group", [SLOTS, SLOTS])
        pv = two(sb, "pv", [SLOTS, D + H])
        recip = two(sb, "recip", [SLOTS, H])
        mixed = two(sb, "mixed", [SLOTS, D])
        x1 = two(sb, "x1", [SLOTS, D])
        sq = two(sb, "sq", [SLOTS, D])
        stats, moments = two(sb, "stats", [SLOTS, 6]), two(sb, "moments", [SLOTS, 2])
        logv, rstd, shift = two(sb, "logv", [SLOTS, 1]), two(sb, "rstd", [SLOTS, 1]), two(sb, "shift", [SLOTS, 1])

        turned_p = pb("turned_p", [128, 512])
        v_p, acc_p = two(pb, "v_p", [SLOTS, 512]), two(pb, "acc_p", [SLOTS, 512])
        small_p = two(pb, "small_p", [SLOTS, 512])
        weight_p = pb("weight_p", [SLOTS, 512])
        KEYS, PROB = slice(0, SLOTS), slice(128, 128 + H)

        cleared = sem("cleared")
        dst_idx_ready, res_idx_ready, out_idx_ready = (two(sem, n) for n in ("dst_ir", "res_ir", "out_ir"))
        xd_in, xr_in, x1_out = two(c.pool_dma, "b_xd_in"), two(c.pool_dma, "b_xr_in"), two(c.pool_dma, "b_x1_out")
        turned_ready, hi_ready, lo_ready = two(sem, "turned_ready"), two(sem, "hi_ready"), two(sem, "lo_ready")
        gap_ready, prob_ready, top_ready = two(sem, "gap_ready"), two(sem, "prob_ready"), sem("top_ready")
        col_ready, prob_t_ready, prob_kept = two(sem, "col_ready"), two(sem, "prob_t_ready"), two(sem, "prob_kept")
        keys_ready, group_ready = two(sem, "keys_ready"), two(sem, "group_ready")
        v_ready, pv_ready, carried = two(sem, "v_ready"), two(sem, "pv_ready"), two(sem, "carried")
        sum_ready, mixed_ready = two(sem, "sum_ready"), two(sem, "mixed_ready")
        finish_links = sem("finish_links")
        recip_ready = two(sem, "recip_ready")
        scan_in_ready = two(sem, "scan_in_ready")
        moments_ready, log_ready, rstd_ready = two(sem, "moments_ready"), two(sem, "log_ready"), two(sem, "rstd_ready")
        shift_ready, x1_ready, sq_ready = two(sem, "shift_ready"), two(sem, "x1_ready"), two(sem, "sq_ready")
        summed, summed_sq = two(sem, "summed"), two(sem, "summed_sq")

        AHEAD, BEHIND = 2, 3

        def place(x):
            return (T - 1) - x.num

        with nc.Block() as block:
            @block.gpsimd
            def _(pool):
                g = nc.gpsimd

                def gather_dst(x):
                    p = x.par
                    pool.wait_ge(turned_ready[p], x.turn)
                    settle(pool)
                    g.tensor_copy(dst_idx[p][:, :], s.val_row[:, ds(place(x), 1)]).then_inc(dst_idx_ready[p], 1)
                    pool.wait_ge(dst_idx_ready[p], x.turn + 1)
                    settle(pool)
                    g.indirect_dma_start(xd[p][:, :], None, x_d, bass.IndirectOffsetOnAxis(dst_idx[p][:, :], 0)) \
                        .then_inc(xd_in[p], 16)

                def gather_residual(x):
                    p = x.par
                    pool.wait_ge(mixed_ready[p], x.turn)
                    settle(pool)
                    g.tensor_copy(res_idx[p][:, :], s.first_row[:, ds(place(x), 1)]).then_inc(res_idx_ready[p], 1)
                    pool.wait_ge(res_idx_ready[p], x.turn + 1)
                    settle(pool)
                    g.indirect_dma_start(xr[p][:, :], None, x_d, bass.IndirectOffsetOnAxis(res_idx[p][:, :], 0),
                                         bounds_check=N - 1, oob_is_err=False).then_inc(xr_in[p], 16)

                def scatter(x):
                    p = x.par
                    pool.wait_ge(x1_out[p], 16 * x.turn)
                    settle(pool)
                    g.tensor_copy(out_idx[p][:, :], s.first_row[:, ds(place(x), 1)]).then_inc(out_idx_ready[p], 1)
                    pool.wait_ge(out_idx_ready[p], x.turn + 1)
                    pool.wait_ge(x1_ready[p], x.turn + 1)
                    settle(pool)
                    g.indirect_dma_start(x1_d, bass.IndirectOffsetOnAxis(out_idx[p][:, :], 0), x1[p][:, :], None,
                                         bounds_check=N - 1, oob_is_err=False).then_inc(x1_out[p], 16)

                pool.wait_ge(cleared, 1)
                def body(at):
                    if x := at(2):
                        gather_dst(x)
                    if x := at(-3):
                        scatter(x)
                    if x := at(0):
                        gather_residual(x)
                sweep(pool, body, 2, AHEAD, BEHIND)
                for u in range(2):
                    pool.wait_ge(x1_out[u], 16 * (T // 2))

            @block.tensor
            def _(pe):
                t_ = nc.tensor

                def turn(x):
                    p = x.par
                    pe.wait_ge(xd_in[p], 16 * (x.turn + 1))
                    if not x.is_zero():
                        b = x.before()
                        pe.wait_ge(lo_ready[b.par], b.turn + 1)
                    for k in range(KC):
                        last = t_.transpose(turned_p[:, k * SLOTS:(k + 1) * SLOTS],
                                            xd[p][:, k * 128:(k + 1) * 128], c.ident[0:SLOTS, 0:SLOTS])
                    last.then_inc(turned_ready[p], 1)

                def small(x):
                    p = x.par
                    pe.wait_ge(prob_ready[p], x.turn + 1)
                    pe.wait_ge(prob_kept[p], x.turn)
                    pe.wait_ge(group_ready[p], x.turn)
                    settle(pe)
                    t_.transpose(small_p[p][:, PROB], prob[p][:, :], c.ident[0:H, 0:H]).then_inc(prob_t_ready[p], 1)
                    pe.wait_ge(col_ready[p], x.turn + 1)
                    t_.matmul(small_p[p][:, KEYS], key_col[p][:, :].to_broadcast([SLOTS, SLOTS]),
                              c.ident[0:SLOTS, 0:SLOTS], start=True, stop=True).then_inc(keys_ready[p], 1)

                def values(x):
                    p = x.par
                    pe.wait_ge(hi_ready[p], x.turn + 1)
                    pe.wait_ge(lo_ready[p], x.turn + 1)
                    pe.wait_ge(pv_ready[p], x.turn)
                    product(t_, v_p[p][:, 0:D], xd_hi[p], xd_lo[p], *wv, SLOTS).then_inc(v_ready[p], 1)

                def group_sum(x):
                    p = x.par
                    pe.wait_ge(group_ready[p], x.turn + 1)
                    pe.wait_ge(carried[p], x.turn + 1)
                    pe.wait_ge(mixed_ready[p], x.turn)
                    if not x.is_zero():
                        b = x.before()
                        pe.wait_ge(recip_ready[b.par], b.turn + 1)
                    t_.matmul(acc_p[p][:, 0:D], group[p][:, :], pv[p][:, 0:D], start=True, stop=True)
                    t_.matmul(weight_p[:, 0:H], group[p][:, :], pv[p][:, D:D + H],
                              start=True, stop=True).then_inc(sum_ready[p], 1)

                def body(at):
                    if x := at(1):
                        turn(x)
                        small(x)
                    if x := at(0):
                        values(x)
                    if x := at(-1):
                        group_sum(x)
                sweep(pe, body, 2, AHEAD, BEHIND)

            @block.scalar
            def _(act):
                a = nc.scalar
                a.preload_act_table_set(TABLES)

                def high(x):
                    p = x.par
                    act.wait_ge(turned_ready[p], x.turn + 1)
                    act.wait_ge(v_ready[p], x.turn)
                    a.copy(xd_hi[p][:, :], turned_p[:, 0:KC * SLOTS]).then_inc(hi_ready[p], 1)

                def carry(x):
                    p = x.par
                    act.wait_ge(pv_ready[p], x.turn + 1)
                    if not x.is_zero():
                        b = x.before()
                        act.wait_ge(sum_ready[b.par], b.turn + 1)
                    a.copy(pv[p][0:1, 0:D], acc_p[1 - p][0:1, 0:D])
                    a.copy(pv[p][0:1, D:D + H], weight_p[0:1, 0:H]).then_inc(carried[p], 1)

                def exps(x):
                    p = x.par
                    act.wait_ge(gap_ready[p], x.turn + 1)
                    act.wait_ge(prob_t_ready[p], x.turn)
                    a.activation(prob[p][:, 1:SLOTS], gap[p][:, :], ACT.Exp).then_inc(prob_ready[p], 1)

                def norm(x):
                    p = x.par
                    act.wait_ge(moments_ready[p], x.turn + 1)
                    a.activation(logv[p][:, :], moments[p][:, 1:2], ACT.Ln, bias=c.ln_eps[0:SLOTS, :]) \
                        .then_inc(log_ready[p], 1)
                    act.wait_ge(log_ready[p], x.turn + 1)
                    a.activation(rstd[p][:, :], logv[p][:, :], ACT.Exp, scale=-0.5).then_inc(rstd_ready[p], 1)
                    act.wait_ge(shift_ready[p], x.turn + 1)
                    act.wait_ge(x1_out[p], 16 * x.turn)
                    act.wait_ge(summed[p], x.turn)
                    a.activation(x1[p][:, :], mixed[p][:, :], ACT.Identity, bias=shift[p][:, :],
                                 scale=rstd[p][:, :]).then_inc(x1_ready[p], 1)
                    act.wait_ge(x1_ready[p], x.turn + 1)
                    act.wait_ge(summed_sq[p], x.turn)
                    a.activation(sq[p][:, :], x1[p][:, :], ACT.Square).then_inc(sq_ready[p], 1)

                act.wait_ge(cleared, 1)
                def body(at):
                    if x := at(1):
                        high(x)
                    if x := at(-1):
                        carry(x)
                    if x := at(2):
                        exps(x)
                    if x := at(-2):
                        norm(x)
                sweep(act, body, 2, AHEAD, BEHIND)

            @block.vector
            def _(dve):
                v = nc.vector
                for u in range(2):
                    v.memset(prob[u][:, :], 0.0)
                    v.memset(xr[u][:, :], 0.0)
                v.memset(top[1][:, :], 0.0)
                v.memset(acc_p[1][:, :], 0.0)
                v.memset(weight_p[:, :], 0.0).then_inc(cleared, 1)
                dve.wait_ge(cleared, 1)
                links = Chain(dve, finish_links, 2)

                def maximum(x):
                    p = x.par
                    at_ = ROWS * place(x)
                    if not x.is_zero():
                        dve.wait_ge(top_ready, x.num)
                    dve.wait_ge(gap_ready[p], x.turn)
                    settle(dve)
                    v.tensor_copy(cut_next[p][:, :], e.cut[:, ds(at_ + 1, ROWS)])
                    v.tensor_copy(run_max[p][:, :], e.run_max[:, ds(at_ + 1, ROWS)]).then_inc(scan_in_ready[p], 1)
                    dve.wait_ge(scan_in_ready[p], x.turn + 1)
                    v.tensor_tensor_scan(top[p][:, 1:SLOTS][:, ::-1], cut_next[p][:, ::-1],
                                         run_max[p][:, ::-1], top[1 - p][:, 1:2],
                                         ALU.add, ALU.max).then_inc(top_ready, 1)
                    dve.wait_ge(top_ready, x.num + 1)
                    dve.wait_ge(prob_ready[p], x.turn)
                    settle(dve)
                    v.tensor_tensor(gap[p][:, :], e.aw[:, ds(at_, ROWS)], top[p][:, 1:SLOTS],
                                    ALU.subtract).then_inc(gap_ready[p], 1)
                    dve.wait_ge(keys_ready[p], x.turn)
                    settle(dve)
                    v.tensor_copy(key_col[p][:, :], s.key_out[:, ds(place(x), 1)]).then_inc(col_ready[p], 1)

                def low(x):
                    p = x.par
                    dve.wait_ge(hi_ready[p], x.turn + 1)
                    v.tensor_tensor(xd_lo[p][:, :], turned_p[:, 0:KC * SLOTS], xd_hi[p][:, :].bitcast(F32),
                                    ALU.subtract).then_inc(lo_ready[p], 1)

                def same_group(x):
                    p = x.par
                    dve.wait_ge(keys_ready[p], x.turn + 1)
                    dve.wait_ge(sum_ready[p], x.turn)
                    v.tensor_copy(pv[p][:, D:D + H], small_p[p][:, PROB]).then_inc(prob_kept[p], 1)
                    dve.wait_ge(keys_ready[p], x.turn + 1)
                    settle(dve)
                    v.tensor_scalar(group[p][:, :], small_p[p][:, KEYS], s.key_in[:, ds(place(x), 1)], None,
                                    ALU.is_equal).then_inc(group_ready[p], 1)

                def weigh(x):
                    p = x.par
                    dve.wait_ge(v_ready[p], x.turn + 1)
                    dve.wait_ge(prob_kept[p], x.turn + 1)
                    v.tensor_tensor(pv[p][:, 0:D].rearrange("p (h d) -> p h d", h=H),
                                    v_p[p][:, 0:D].rearrange("p (h d) -> p h d", h=H),
                                    pv[p][:, D:D + H].unsqueeze(2).to_broadcast([SLOTS, H, DH]),
                                    ALU.mult).then_inc(pv_ready[p], 1)

                def finish(x):
                    p = x.par
                    link = links.at(x)
                    dve.wait_ge(sum_ready[p], x.turn + 1)
                    dve.wait_ge(x1_ready[p], x.turn)
                    if not x.is_last():
                        n = x.after()
                        dve.wait_ge(carried[n.par], n.turn + 1)
                    v.reciprocal(recip[p][:, :], weight_p[:, 0:H]).then_inc(recip_ready[p], 1)
                    dve.wait_ge(recip_ready[p], x.turn + 1)
                    link(v.tensor_tensor(mixed[p][:, :].rearrange("p (h d) -> p h d", h=H),
                                         acc_p[p][:, 0:D].rearrange("p (h d) -> p h d", h=H),
                                         recip[p][:, :].unsqueeze(2).to_broadcast([SLOTS, H, DH]), ALU.mult))
                    dve.wait_ge(xr_in[p], 16 * (x.turn + 1))
                    v.tensor_tensor(mixed[p][:, :], mixed[p][:, :], xr[p][:, :], ALU.add).then_inc(mixed_ready[p], 1)
                    dve.wait_ge(mixed_ready[p], x.turn + 1)
                    link(v.bn_stats(stats[p][:, :], mixed[p][:, :]))
                    dve.wait_ge(shift_ready[p], x.turn)
                    settle(dve)
                    v.bn_aggr(moments[p][:, :], stats[p][:, :]).then_inc(moments_ready[p], 1)

                def centre(x):
                    p = x.par
                    dve.wait_ge(rstd_ready[p], x.turn + 1)
                    dve.wait_ge(moments_ready[p], x.turn + 1)
                    v.tensor_scalar(shift[p][:, :], moments[p][:, 0:1], -1.0, rstd[p][:, :], ALU.mult, ALU.mult) \
                        .then_inc(shift_ready[p], 1)

                def sum_up(x):
                    p, b = x.par, x.before()
                    first = s.first[:, ds(place(x), 1)]
                    dve.wait_ge(x1_ready[p], x.turn + 1)
                    if not x.is_zero():
                        dve.wait_ge(summed[b.par], b.turn + 1)
                        dve.wait_ge(summed_sq[b.par], b.turn + 1)
                    settle(dve)
                    v.scalar_tensor_tensor(acc[0][:, :], x1[p][:, :], first, acc[0][:, :],
                                           ALU.mult, ALU.add).then_inc(summed[p], 1)
                    dve.wait_ge(sq_ready[p], x.turn + 1)
                    v.scalar_tensor_tensor(acc[1][:, :], sq[p][:, :], first, acc[1][:, :],
                                           ALU.mult, ALU.add).then_inc(summed_sq[p], 1)

                def body(at):
                    if x := at(-1):
                        weigh(x)
                    if x := at(1):
                        low(x)
                    if x := at(0):
                        same_group(x)
                    if x := at(2):
                        maximum(x)
                    if x := at(-2):
                        finish(x)
                    if x := at(-3):
                        sum_up(x)
                    if x := at(-2):
                        centre(x)
                sweep(dve, body, 2, AHEAD, BEHIND)


def gather_sums(nc, ctx, c, s, x1_d, sums_d):
    P = 4
    with ExitStack() as own:
        semaphores = Semaphores(nc, own)
        def sb(name, shape, dt=F32):
            return own.enter_context(nc.sbuf_tensor(f"g_{name}", shape, dt))

        def sem(name):
            return semaphores.take(f"g_{name}")

        def ring(make, name, *a):
            return [make(f"{name}{u}", *a) for u in range(P)]

        idx = ring(sb, "idx", [SLOTS, 1], U32)
        rows = ring(sb, "rows", [SLOTS, D])
        key_col = ring(sb, "key_col", [SLOTS, 1])
        group = ring(sb, "group", [SLOTS, SLOTS])
        total = ring(sb, "total", [SLOTS, D])
        sum_p = [own.enter_context(nc.psum_tensor(f"g_sum_p{u}", [SLOTS, 512], F32)) for u in range(P)]
        keys_p = [own.enter_context(nc.psum_tensor(f"g_keys_p{u}", [SLOTS, 512], F32)) for u in range(P)]

        cleared = sem("cleared")
        rows_in = ring(c.pool_dma, "g_rows_in")
        idx_ready, col_ready, keys_ready, group_ready, carried, sum_ready, total_ready, total_out = (
            ring(sem, n) for n in ("idx_ready", "col_ready", "keys_ready", "group_ready", "carried",
                                   "sum_ready", "total_ready", "total_out"))
        AHEAD, BEHIND = 4, 1

        def place(x):
            return (T - 1) - x.num

        with nc.Block() as block:
            @block.gpsimd
            def _(pool):
                g = nc.gpsimd

                def body(at):
                    if x := at(3):
                        p = x.par
                        pool.wait_ge(sum_ready[p], x.turn)
                        settle(pool)
                        g.tensor_copy(idx[p][:, :], s.val_row[:, ds(place(x), 1)]).then_inc(idx_ready[p], 1)
                        pool.wait_ge(idx_ready[p], x.turn + 1)
                        settle(pool)
                        g.indirect_dma_start(rows[p][:, :], None, x1_d, bass.IndirectOffsetOnAxis(idx[p][:, :], 0)) \
                            .then_inc(rows_in[p], 16)
                sweep(pool, body, P, AHEAD, BEHIND)

            @block.tensor
            def _(pe):
                t_ = nc.tensor

                def body(at):
                    if x := at(1):
                        p = x.par
                        pe.wait_ge(col_ready[p], x.turn + 1)
                        pe.wait_ge(group_ready[p], x.turn)
                        t_.matmul(keys_p[p][:, 0:SLOTS], key_col[p][:, :].to_broadcast([SLOTS, SLOTS]),
                                  c.ident[0:SLOTS, 0:SLOTS], start=True, stop=True).then_inc(keys_ready[p], 1)
                    if x := at(0):
                        p = x.par
                        pe.wait_ge(group_ready[p], x.turn + 1)
                        pe.wait_ge(carried[p], x.turn + 1)
                        pe.wait_ge(total_ready[p], x.turn)
                        t_.matmul(sum_p[p][:, 0:D], group[p][:, :], rows[p][:, :],
                                  start=True, stop=True).then_inc(sum_ready[p], 1)
                sweep(pe, body, P, AHEAD, BEHIND)

            @block.scalar
            def _(act):
                a = nc.scalar
                act.wait_ge(cleared, 1)

                def body(at):
                    if x := at(0):
                        p = x.par
                        act.wait_ge(rows_in[p], 16 * (x.turn + 1))
                        if not x.is_zero():
                            b = x.before()
                            act.wait_ge(sum_ready[b.par], b.turn + 1)
                        a.copy(rows[p][0:1, :], sum_p[x.before().par][0:1, 0:D]).then_inc(carried[p], 1)
                sweep(act, body, P, AHEAD, BEHIND)

            @block.vector
            def _(dve):
                v = nc.vector
                v.memset(sum_p[P - 1][:, :], 0.0).then_inc(cleared, 1)

                def body(at):
                    if x := at(2):
                        p = x.par
                        dve.wait_ge(keys_ready[p], x.turn)
                        settle(dve)
                        v.tensor_copy(key_col[p][:, :], s.key_out[:, ds(place(x), 1)]).then_inc(col_ready[p], 1)
                    if x := at(1):
                        p = x.par
                        dve.wait_ge(keys_ready[p], x.turn + 1)
                        dve.wait_ge(sum_ready[p], x.turn)
                        settle(dve)
                        v.tensor_scalar(group[p][:, :], keys_p[p][:, 0:SLOTS], s.key_in[:, ds(place(x), 1)], None,
                                        ALU.is_equal).then_inc(group_ready[p], 1)
                    if x := at(-1):
                        p = x.par
                        dve.wait_ge(sum_ready[p], x.turn + 1)
                        dve.wait_ge(total_out[p], 16 * x.turn)
                        if not x.is_last():
                            n = x.after()
                            dve.wait_ge(carried[n.par], n.turn + 1)
                        v.tensor_copy(total[p][:, :], sum_p[p][:, 0:D]).then_inc(total_ready[p], 1)
                sweep(dve, body, P, AHEAD, BEHIND)

            @block.sync
            def _(sp):
                def body(at):
                    if x := at(-1):
                        p = x.par
                        sp.wait_ge(total_ready[p], x.turn + 1)
                        settle(sp)
                        sp.dma_start(sums_d[ds(SLOTS * place(x), SLOTS), :], total[p][:, :]).then_inc(total_out[p], 16)
                sweep(sp, body, P, AHEAD, BEHIND)
                for u in range(P):
                    sp.wait_ge(total_out[u], 16 * (T // P))


def column_variance(v, link, sums_p, mean, square, var, ready):
    link(v.tensor_scalar(mean[:, :], sums_p[:, 0:KC], 1.0 / N, None, ALU.mult))
    link(v.tensor_scalar(var[:, :], sums_p[:, KC:2 * KC], 1.0 / N, None, ALU.mult))
    link(v.tensor_tensor(square[:, :], mean[:, :], mean[:, :], ALU.mult))
    link(v.tensor_tensor(var[:, :], var[:, :], square[:, :], ALU.subtract))
    v.tensor_scalar(var[:, :], var[:, :], 0.0, BN_EPS, ALU.max, ALU.add).then_inc(ready, 1)


def first_norm(nc, ctx, c, acc, g_d, b_d, w_d, bias_d):
    o = Buffers()

    def keep(name, shape, dt=F32):
        return ctx.enter_context(nc.sbuf_tensor(f"n_{name}", shape, dt))

    o.w_hi, o.w_lo = keep("w_hi", [128, KC, D], F32R), keep("w_lo", [128, KC, D], F32R)
    o.shift_w, o.bias = keep("shift_w", [128, D]), keep("bias", [128, D])
    with ExitStack() as own:
        semaphores = Semaphores(nc, own)
        def sb(name, shape, dt=F32):
            return own.enter_context(nc.sbuf_tensor(f"n_{name}", shape, dt))

        def sem(name):
            return semaphores.take(f"n_{name}")
        w = sb("w", [128, KC, D])
        w_scaled = sb("w_scaled", [128, KC, D])
        g_col, b_col, a_col, s_col, var, mean = (sb(n, [128, KC]) for n in ("g_col", "b_col", "a_col", "s_col", "var", "mean"))
        logv = sb("logv", [128, KC])
        bias_row, shift_row = sb("bias_row", [1, D]), sb("shift_row", [1, D])
        sums_p = own.enter_context(nc.psum_tensor("n_sums_p", [128, 512], F32))
        row_p = own.enter_context(nc.psum_tensor("n_row_p", [128, 512], F32))
        wide_p = own.enter_context(nc.psum_tensor("n_wide_p", [128, 512], F32))
        wide2_p = own.enter_context(nc.psum_tensor("n_wide2_p", [128, 512], F32))
        loaded, sums_ready, chain, var_ready, log_ready, rstd_ready, shift_ready, row_ready, row_kept, wide_ready, \
            scaled, high = (sem(n) for n in ("loaded", "sums_ready", "chain", "var_ready", "log_ready", "rstd_ready",
                                             "shift_ready", "row_ready", "row_kept", "wide_ready", "scaled", "high"))
        with nc.Block() as block:
            @block.sync
            def _(sp):
                sp.dma_start(w[:, :, :], w_d.rearrange("(k p) n -> p k n", p=128)).then_inc(loaded, 16)
                sp.dma_start(g_col[:, :], g_d.rearrange("(k p) -> p k", p=128), allow_slow_non_contiguous=True).then_inc(loaded, 16)
                sp.dma_start(b_col[:, :], b_d.rearrange("(k p) -> p k", p=128), allow_slow_non_contiguous=True).then_inc(loaded, 16)
                sp.dma_start(bias_row[:, :], bias_d.rearrange("(a n) -> a n", a=1)).then_inc(loaded, 16)

            @block.tensor
            def _(pe):
                t_ = nc.tensor
                for j in range(2):
                    for k in range(KC):
                        last = t_.matmul(sums_p[:, j * KC + k:j * KC + k + 1], acc[j][:, k * 128:(k + 1) * 128],
                                         c.ones[0:SLOTS, 0:1], start=True, stop=True)
                last.then_inc(sums_ready, 1)
                pe.wait_ge(shift_ready, 1)
                pe.wait_ge(loaded, 64)
                for k in range(KC):
                    last = t_.matmul(row_p[0:1, 0:D], s_col[:, k:k + 1], w[:, k, :], start=(k == 0), stop=(k == KC - 1))
                last.then_inc(row_ready, 1)
                t_.matmul(wide2_p[:, 0:D], c.ones[0:1, :], bias_row[:, :], start=True, stop=True)
                pe.wait_ge(row_kept, 1)
                t_.matmul(wide_p[:, 0:D], c.ones[0:1, :], shift_row[:, :], start=True, stop=True).then_inc(wide_ready, 1)

            @block.scalar
            def _(act):
                a = nc.scalar
                a.preload_act_table_set(TABLES)
                act.wait_ge(var_ready, 1)
                a.activation(logv[:, :], var[:, :], ACT.Ln).then_inc(log_ready, 1)
                act.wait_ge(log_ready, 1)
                a.activation(var[:, :], logv[:, :], ACT.Exp, scale=-0.5).then_inc(rstd_ready, 1)
                act.wait_ge(row_ready, 1)
                a.copy(shift_row[:, :], row_p[0:1, 0:D]).then_inc(row_kept, 1)
                act.wait_ge(scaled, KC)
                a.copy(o.w_hi[:, :, :], w_scaled[:, :, :]).then_inc(high, 1)

            @block.vector
            def _(dve):
                v = nc.vector
                done = [0]

                def link(ins):
                    done[0] += 1
                    ins.then_inc(chain, 1)
                    dve.wait_ge(chain, done[0])

                dve.wait_ge(sums_ready, 1)
                column_variance(v, link, sums_p, mean, a_col, var, var_ready)
                dve.wait_ge(rstd_ready, 1)
                dve.wait_ge(loaded, 64)
                link(v.tensor_tensor(a_col[:, :], var[:, :], g_col[:, :], ALU.mult))
                link(v.tensor_tensor(mean[:, :], mean[:, :], a_col[:, :], ALU.mult))
                v.tensor_tensor(s_col[:, :], b_col[:, :], mean[:, :], ALU.subtract).then_inc(shift_ready, 1)
                for k in range(KC):
                    v.tensor_scalar(w_scaled[:, k, :], w[:, k, :], a_col[:, k:k + 1], None, ALU.mult).then_inc(scaled, 1)
                dve.wait_ge(high, 1)
                v.tensor_tensor(o.w_lo[:, :, :], w_scaled[:, :, :], o.w_hi[:, :, :].bitcast(F32), ALU.subtract)
                dve.wait_ge(wide_ready, 1)
                v.tensor_copy(o.shift_w[:, :], wide_p[:, 0:D])
                v.tensor_copy(o.bias[:, :], wide2_p[:, 0:D])
    return o


def few_node_attention(nc, ctx, c, x1_d, wq_d, wk_d, wv_d, wo_d, proj_d):
    o = Buffers()
    o.first_mix = ctx.enter_context(nc.sbuf_tensor("first_mix", [128, D], F32))
    o.rest_mix = ctx.enter_context(nc.sbuf_tensor("rest_mix", [128, D], F32))
    MC = M // 128
    W1 = DH + 1
    with ExitStack() as own:
        semaphores = Semaphores(nc, own)
        def sb(name, shape, dt=F32):
            return own.enter_context(nc.sbuf_tensor(f"t_{name}", shape, dt))

        def sem(name):
            return semaphores.take(f"t_{name}")

        h = sb("h", [MAXN, D])
        wq, wk, wv, wo = (sb(n, [128, KC, D]) for n in ("wq", "wk", "wv", "wo"))
        proj, proj_t = sb("proj", [128, MC, DH]), sb("proj_t", [DH, M])
        h_t = sb("h_t", [128, KC * MAXN])
        q_t, k_t, q_sq, k_sq = (sb(n, [DH, H * MAXN]) for n in ("q_t", "k_t", "q_sq", "k_sq"))
        half = sb("half", [DH, 1])
        v1 = sb("v1", [MAXN, H, W1])
        qf, kf = sb("qf", [MAXN, H * M]), sb("kf", [MAXN, H * M])
        diag, peak, bias = sb("diag", [MAXN, 2 * H]), sb("peak", [MAXN, 2 * H]), sb("bias", [MAXN, 2 * H])
        peak_t = sb("peak_t", [H, 1])
        qf_t = sb("qf_t", [128, H * MC * MAXN])
        kv = sb("kv", [128, H * MC, W1])
        z = sb("z", [MAXN, H])
        attn, attn_t, out = sb("attn", [MAXN, D]), sb("attn_t", [128, KC * MAXN]), sb("out", [MAXN, D])
        last_row, own_row = sb("last_row", [MAXN, 128]), sb("own_row", [MAXN, 128])
        bank = [own.enter_context(nc.psum_tensor(f"t_bank{i}", [128, 512], F32)) for i in range(8)]

        names = ("loaded h_turned h_kept qkv_ready qkv_kept features_ready q_seen k_ready k_seen peak_turned "
                 "peak_down peak_wide biases q_exp k_exp q_done k_done outer_ready outer_kept mixed_ready "
                 "attn_ready attn_turned attn_kept out_ready out_kept wide_ready chain picks picks_made half_made "
                 "squares").split()
        S = {n: sem(n) for n in names}

        with nc.Block() as block:
            @block.sync
            def _(sp):
                for dst, src in ((h[:, :], x1_d[0:MAXN, :]), (proj[:, :, :], proj_d.rearrange("(c p) d -> p c d", p=128)),
                                 (wq[:, :, :], wq_d.rearrange("(k p) n -> p k n", p=128)),
                                 (wk[:, :, :], wk_d.rearrange("(k p) n -> p k n", p=128)),
                                 (wv[:, :, :], wv_d.rearrange("(k p) n -> p k n", p=128)),
                                 (wo[:, :, :], wo_d.rearrange("(k p) n -> p k n", p=128))):
                    sp.dma_start(dst, src).then_inc(S["loaded"], 16)

            @block.gpsimd
            def _(pool):
                g = nc.gpsimd
                g.affine_select(out=last_row[:, :], in_=c.ones[0:MAXN, :], compare_op=ALU.is_ge, fill=0.0,
                                base=-(MAXN - 1), pattern=[[0, 128]], channel_multiplier=1).then_inc(S["picks"], 1)
                pool.wait_ge(S["picks"], 1)
                g.affine_select(out=own_row[:, :], in_=last_row[:, :], compare_op=ALU.is_gt, fill=0.0,
                                base=-(MAXN - 1), pattern=[[1, 128]], channel_multiplier=0).then_inc(S["picks"], 1)

            @block.tensor
            def _(pe):
                t_ = nc.tensor
                pe.wait_ge(S["loaded"], 96)
                for k in range(KC):
                    t_.transpose(bank[0][:, k * MAXN:(k + 1) * MAXN], h[:, k * 128:(k + 1) * 128], c.ident[0:MAXN, 0:MAXN])
                for m in range(MC):
                    last = t_.transpose(bank[1][0:DH, m * 128:(m + 1) * 128], proj[:, m, :], c.ident[:, :])
                last.then_inc(S["h_turned"], 1)
                pe.wait_ge(S["h_kept"], 1)
                for b, w in ((2, wq), (3, wk)):
                    for a in range(H):
                        for k in range(KC):
                            t_.matmul(bank[b][0:DH, a * MAXN:(a + 1) * MAXN], w[:, k, a * DH:(a + 1) * DH],
                                      h_t[:, k * MAXN:(k + 1) * MAXN], start=(k == 0), stop=(k == KC - 1))
                for k in range(KC):
                    last = t_.matmul(bank[0][0:MAXN, 0:D], h_t[:, k * MAXN:(k + 1) * MAXN], wv[:, k, :],
                                     start=(k == 0), stop=(k == KC - 1))
                last.then_inc(S["qkv_ready"], 1)
                pe.wait_ge(S["qkv_kept"], 1)
                for j, sq in enumerate((q_sq, k_sq)):
                    for a in range(H):
                        t_.matmul(bank[1][0:MAXN, j * H + a:j * H + a + 1], sq[:, a * MAXN:(a + 1) * MAXN], half[:, :],
                                  start=True, stop=True)
                for a in range(H):
                    last = t_.matmul(bank[4 + a // 2][0:MAXN, (a % 2) * M:(a % 2 + 1) * M],
                                     q_t[:, a * MAXN:(a + 1) * MAXN], proj_t[:, :], start=True, stop=True)
                last.then_inc(S["features_ready"], 1)
                pe.wait_ge(S["q_seen"], 1)
                for a in range(H):
                    last = t_.matmul(bank[4 + a // 2][0:MAXN, (a % 2) * M:(a % 2 + 1) * M],
                                     k_t[:, a * MAXN:(a + 1) * MAXN], proj_t[:, :], start=True, stop=True)
                last.then_inc(S["k_ready"], 1)
                pe.wait_ge(S["k_seen"], 1)
                t_.transpose(bank[2][0:H, 0:MAXN], peak[:, H:2 * H], c.ident[0:MAXN, 0:MAXN]).then_inc(S["peak_turned"], 1)
                pe.wait_ge(S["peak_down"], 1)
                t_.matmul(bank[3][0:MAXN, 0:H], peak_t[:, :].to_broadcast([H, MAXN]), c.ident[0:H, 0:H],
                          start=True, stop=True).then_inc(S["peak_wide"], 1)
                pe.wait_ge(S["q_done"], 1)
                for a in range(H):
                    for m in range(MC):
                        i = a * MC + m
                        t_.transpose(bank[i // 8][:, (i % 8) * MAXN:(i % 8 + 1) * MAXN],
                                     qf[:, a * M + m * 128:a * M + (m + 1) * 128], c.ident[0:MAXN, 0:MAXN])
                pe.wait_ge(S["k_done"], 1)
                for a in range(H):
                    for m in range(MC):
                        i = a * MC + m
                        last = t_.matmul(bank[4 + i // 6][:, (i % 6) * W1:(i % 6 + 1) * W1],
                                         kf[:, a * M + m * 128:a * M + (m + 1) * 128], v1[:, a, :],
                                         start=True, stop=True)
                last.then_inc(S["outer_ready"], 1)
                pe.wait_ge(S["outer_kept"], 1)
                for a in range(H):
                    for m in range(MC):
                        i = a * MC + m
                        last = t_.matmul(bank[2 + a // 4][0:MAXN, (a % 4) * W1:(a % 4 + 1) * W1],
                                         qf_t[:, i * MAXN:(i + 1) * MAXN], kv[:, i, :],
                                         start=(m == 0), stop=(m == MC - 1))
                last.then_inc(S["mixed_ready"], 1)
                pe.wait_ge(S["attn_ready"], 1)
                for k in range(KC):
                    last = t_.transpose(bank[0][:, k * MAXN:(k + 1) * MAXN], attn[:, k * 128:(k + 1) * 128],
                                        c.ident[0:MAXN, 0:MAXN])
                last.then_inc(S["attn_turned"], 1)
                pe.wait_ge(S["attn_kept"], 1)
                for k in range(KC):
                    last = t_.matmul(bank[1][0:MAXN, 0:D], attn_t[:, k * MAXN:(k + 1) * MAXN], wo[:, k, :],
                                     start=(k == 0), stop=(k == KC - 1))
                last.then_inc(S["out_ready"], 1)
                pe.wait_ge(S["out_kept"], 1)
                pe.wait_ge(S["picks_made"], 1)
                t_.matmul(bank[4][:, 0:D], own_row[:, :], out[:, :], start=True, stop=True)
                t_.matmul(bank[5][:, 0:D], last_row[:, :], out[:, :], start=True, stop=True).then_inc(S["wide_ready"], 1)

            @block.scalar
            def _(act):
                a_ = nc.scalar
                a_.preload_act_table_set(TABLES)
                act.wait_ge(S["biases"], 1)
                for j, (f, done) in enumerate(((qf, S["q_exp"]), (kf, S["k_exp"]))):
                    for a in range(H):
                        last = a_.activation(f[:, a * M:(a + 1) * M], f[:, a * M:(a + 1) * M], ACT.Exp,
                                             bias=bias[:, j * H + a:j * H + a + 1])
                    last.then_inc(done, 1)

            @block.vector
            def _(dve):
                v = nc.vector
                done = [0]

                def link(ins):
                    done[0] += 1
                    ins.then_inc(S["chain"], 1)
                    dve.wait_ge(S["chain"], done[0])

                v.memset(half[:, :], 0.5)
                v.memset(v1[:, :, :], 1.0).then_inc(S["half_made"], 1)
                dve.wait_ge(S["half_made"], 1)
                dve.wait_ge(S["picks"], 2)
                v.tensor_tensor(own_row[:, :], own_row[:, :], c.ident[0:MAXN, :], ALU.add).then_inc(S["picks_made"], 1)
                dve.wait_ge(S["h_turned"], 1)
                v.tensor_copy(h_t[:, :], bank[0][:, 0:KC * MAXN])
                v.tensor_copy(proj_t[:, :], bank[1][0:DH, 0:M]).then_inc(S["h_kept"], 1)
                dve.wait_ge(S["qkv_ready"], 1)
                v.tensor_scalar(q_t[:, :], bank[2][0:DH, 0:H * MAXN], DH ** -0.25, None, ALU.mult)
                link(v.tensor_scalar(k_t[:, :], bank[3][0:DH, 0:H * MAXN], DH ** -0.25, None, ALU.mult))
                v.tensor_tensor(q_sq[:, :], q_t[:, :], q_t[:, :], ALU.mult)
                v.tensor_tensor(k_sq[:, :], k_t[:, :], k_t[:, :], ALU.mult)
                v.tensor_copy(v1[:, :, 0:DH], bank[0][0:MAXN, 0:D].rearrange("p (h d) -> p h d", h=H)) \
                    .then_inc(S["qkv_kept"], 1)
                dve.wait_ge(S["features_ready"], 1)
                v.tensor_copy(diag[:, :], bank[1][0:MAXN, 0:2 * H])
                for b in range(4):
                    ins = v.tensor_copy(qf[:, b * 512:(b + 1) * 512], bank[4 + b][0:MAXN, :])
                ins.then_inc(S["q_seen"], 1)
                dve.wait_ge(S["q_seen"], 1)
                v.tensor_reduce(peak[:, 0:H], qf[:, :].rearrange("p (h m) -> p h m", h=H), op=ALU.max, axis=AX.X)
                dve.wait_ge(S["k_ready"], 1)
                for b in range(4):
                    ins = v.tensor_copy(kf[:, b * 512:(b + 1) * 512], bank[4 + b][0:MAXN, :])
                link(ins)
                v.tensor_reduce(peak[:, H:2 * H], kf[:, :].rearrange("p (h m) -> p h m", h=H), op=ALU.max,
                                axis=AX.X).then_inc(S["k_seen"], 1)
                dve.wait_ge(S["peak_turned"], 1)
                v.reduce_max(peak_t[:, :], bank[2][0:H, 0:MAXN], AX.X).then_inc(S["peak_down"], 1)
                dve.wait_ge(S["peak_wide"], 1)
                link(v.tensor_copy(peak[:, H:2 * H], bank[3][0:MAXN, 0:H]))
                v.scalar_tensor_tensor(bias[:, :], diag[:, :], -1.0, peak[:, :], ALU.mult, ALU.subtract) \
                    .then_inc(S["biases"], 1)
                dve.wait_ge(S["q_exp"], 1)
                v.tensor_scalar(qf[:, :], qf[:, :], M ** -0.5, KEPS, ALU.mult, ALU.add).then_inc(S["q_done"], 1)
                dve.wait_ge(S["k_exp"], 1)
                v.tensor_scalar(kf[:, :], kf[:, :], M ** -0.5, KEPS, ALU.mult, ALU.add).then_inc(S["k_done"], 1)
                dve.wait_ge(S["outer_ready"], 1)
                for b in range(2):
                    v.tensor_copy(qf_t[:, b * 512:(b + 1) * 512], bank[b][:, :])
                for b in range(3):
                    n = min(6, H * MC - 6 * b)
                    ins = v.tensor_copy(kv[:, 6 * b:6 * b + n, :],
                                        bank[4 + b][:, 0:n * W1].rearrange("p (i w) -> p i w", w=W1))
                ins.then_inc(S["outer_kept"], 1)
                dve.wait_ge(S["mixed_ready"], 1)
                for b in range(2):
                    heads = bank[2 + b][0:MAXN, 0:4 * W1].rearrange("p (h w) -> p h w", w=W1)
                    link(v.tensor_scalar(z[:, 4 * b:4 * b + 4], heads[:, :, DH], KEPS, None, ALU.add))
                    link(v.reciprocal(z[:, 4 * b:4 * b + 4], z[:, 4 * b:4 * b + 4]))
                    ins = v.tensor_tensor(attn[:, b * 256:(b + 1) * 256].rearrange("p (h d) -> p h d", h=4),
                                          heads[:, :, 0:DH],
                                          z[:, 4 * b:4 * b + 4].unsqueeze(2).to_broadcast([MAXN, 4, DH]), ALU.mult)
                ins.then_inc(S["attn_ready"], 1)
                dve.wait_ge(S["attn_turned"], 1)
                v.tensor_copy(attn_t[:, :], bank[0][:, 0:KC * MAXN]).then_inc(S["attn_kept"], 1)
                dve.wait_ge(S["out_ready"], 1)
                v.tensor_copy(out[:, :], bank[1][0:MAXN, 0:D]).then_inc(S["out_kept"], 1)
                dve.wait_ge(S["wide_ready"], 1)
                v.tensor_copy(o.first_mix[:, :], bank[4][:, 0:D])
                v.tensor_copy(o.rest_mix[:, :], bank[5][:, 0:D])
    return o


def convolve(nc, ctx, c, s, n, mix, x1_d, sums_d, y, acc):
    with ExitStack() as own:
        semaphores = Semaphores(nc, own)
        def sb(name, shape, dt=F32):
            return own.enter_context(nc.sbuf_tensor(f"v_{name}", shape, dt))

        def sem(name):
            return semaphores.take(f"v_{name}")

        def two(make, name, *a):
            return [make(f"{name}{u}", *a) for u in range(2)]

        def pb(name, shape):
            return own.enter_context(nc.psum_tensor(f"v_{name}", shape, F32))

        idx = two(sb, "idx", [SLOTS, 1], U32)
        total = two(sb, "total", [SLOTS, D])
        x1 = two(sb, "x1", [ROWS, D])
        hi, lo = two(sb, "hi", [128, KC * ROWS], F32R), two(sb, "lo", [128, KC * ROWS], F32R)
        sq = pb("sq", [ROWS, D])
        turned_p, conv_p = two(pb, "turned_p", [128, 512]), two(pb, "conv_p", [ROWS, 512])

        cleared = sem("cleared")
        links = sem("links")
        total_in = two(c.pool_dma, "v_total_in")
        idx_ready, mean_ready, turned_ready, hi_ready, lo_ready, conv_ready, conv_read, x1_in, based, y_ready, \
            sq_ready, summed, summed_sq = (two(sem, m) for m in (
                "idx_ready", "mean_ready", "turned_ready", "hi_ready", "lo_ready", "conv_ready",
                "conv_read", "x1_in", "based", "y_ready", "sq_ready", "summed", "summed_sq"))
        AHEAD, BEHIND = 2, 2

        with nc.Block() as block:
            @block.gpsimd
            def _(pool):
                g = nc.gpsimd
                pool.wait_ge(cleared, 1)

                def gather(x):
                    p = x.par
                    pool.wait_ge(turned_ready[p], x.turn)
                    g.tensor_copy(idx[p][:, :], s.sum_row[:, ds(x.num, 1)]).then_inc(idx_ready[p], 1)
                    pool.wait_ge(idx_ready[p], x.turn + 1)
                    settle(pool)
                    g.indirect_dma_start(total[p][:, :], None, sums_d, bass.IndirectOffsetOnAxis(idx[p][:, :], 0),
                                         bounds_check=T * SLOTS - 1, oob_is_err=False).then_inc(total_in[p], 16)

                def base(x):
                    p = x.par
                    pool.wait_ge(x1_in[p], 32 * (x.turn + 1))
                    g.tensor_tensor(x1[p][:, :], x1[p][:, :],
                                    (mix.first_mix if x.is_zero() else mix.rest_mix)[0:ROWS, :],
                                    ALU.add).then_inc(based[p], 1)

                def body(at):
                    if x := at(2):
                        gather(x)
                    if x := at(0):
                        base(x)
                sweep(pool, body, 2, AHEAD, BEHIND)

            @block.sync
            def _(sp):
                def body(at):
                    if x := at(1):
                        p = x.par
                        sp.wait_ge(y_ready[p], x.turn)
                        for a, b in ROWS_CUT:
                            sp.dma_start(x1[p][a:b, :], x1_d[ds(ROWS * x.num + a, b - a), :]).then_inc(x1_in[p], 16)
                sweep(sp, body, 2, AHEAD, BEHIND)

            @block.tensor
            def _(pe):
                t_ = nc.tensor

                def turn(x):
                    p = x.par
                    pe.wait_ge(mean_ready[p], x.turn + 1)
                    pe.wait_ge(lo_ready[p], x.turn)
                    for k in range(KC):
                        last = t_.transpose(turned_p[p][:, k * ROWS:(k + 1) * ROWS],
                                            total[p][0:ROWS, k * 128:(k + 1) * 128], c.ident[0:ROWS, 0:ROWS])
                    last.then_inc(turned_ready[p], 1)

                def weights(x):
                    p = x.par
                    pe.wait_ge(hi_ready[p], x.turn + 1)
                    pe.wait_ge(lo_ready[p], x.turn + 1)
                    pe.wait_ge(conv_read[p], x.turn)
                    product(t_, conv_p[p][:, 0:D], hi[p], lo[p], n.w_hi, n.w_lo, ROWS).then_inc(conv_ready[p], 1)

                def body(at):
                    if x := at(1):
                        turn(x)
                    if x := at(0):
                        weights(x)
                sweep(pe, body, 2, AHEAD, BEHIND)

            @block.scalar
            def _(act):
                a = nc.scalar
                a.preload_act_table_set(TABLES)

                def body(at):
                    if x := at(1):
                        p = x.par
                        act.wait_ge(total_in[p], 16 * (x.turn + 1))
                        a.activation(total[p][:, :], total[p][:, :], ACT.Copy, scale=s.inverse[:, ds(x.num, 1)]) \
                            .then_inc(mean_ready[p], 1)
                        act.wait_ge(turned_ready[p], x.turn + 1)
                        act.wait_ge(conv_ready[p], x.turn)
                        a.copy(hi[p][:, :], turned_p[p][:, 0:KC * ROWS]).then_inc(hi_ready[p], 1)
                    if x := at(-1):
                        p = x.par
                        act.wait_ge(y_ready[p], x.turn + 1)
                        if not x.is_zero():
                            b = x.before()
                            act.wait_ge(summed_sq[b.par], b.turn + 1)
                        a.activation(sq[:, :], y[0:ROWS, ds(D * x.num, D)], ACT.Square).then_inc(sq_ready[p], 1)
                sweep(act, body, 2, AHEAD, BEHIND)

            @block.vector
            def _(dve):
                v = nc.vector
                for m in acc:
                    v.memset(m[:, :], 0.0)
                for u in range(2):
                    ins = v.memset(total[u][:, :], 0.0)
                ins.then_inc(cleared, 1)
                dve.wait_ge(cleared, 1)
                chain = Chain(dve, links, 1)

                def add(x):
                    p = x.par
                    link = chain.at(x)
                    dve.wait_ge(conv_ready[p], x.turn + 1)
                    z = y[0:ROWS, ds(D * x.num, D)]
                    v.scalar_tensor_tensor(z, n.shift_w[0:ROWS, :], s.has[:, ds(x.num, 1)],
                                           conv_p[p][:, 0:D], ALU.mult, ALU.add).then_inc(conv_read[p], 1)
                    dve.wait_ge(conv_read[p], x.turn + 1)
                    link(v.tensor_tensor(z, z, n.bias[0:ROWS, :], ALU.add))
                    dve.wait_ge(based[p], x.turn + 1)
                    v.scalar_tensor_tensor(z, z, 0.0, x1[p][:, :], ALU.max, ALU.add).then_inc(y_ready[p], 1)

                def sum_up(x):
                    p, b = x.par, x.before()
                    dve.wait_ge(y_ready[p], x.turn + 1)
                    if not x.is_zero():
                        dve.wait_ge(summed[b.par], b.turn + 1)
                        dve.wait_ge(summed_sq[b.par], b.turn + 1)
                    v.tensor_tensor(acc[0][0:ROWS, :], acc[0][0:ROWS, :], y[0:ROWS, ds(D * x.num, D)],
                                    ALU.add).then_inc(summed[p], 1)
                    dve.wait_ge(sq_ready[p], x.turn + 1)
                    v.tensor_tensor(acc[1][0:ROWS, :], acc[1][0:ROWS, :], sq[:, :], ALU.add).then_inc(summed_sq[p], 1)

                def body(at):
                    if x := at(1):
                        p = x.par
                        dve.wait_ge(hi_ready[p], x.turn + 1)
                        v.tensor_tensor(lo[p][:, :], turned_p[p][:, 0:KC * ROWS], hi[p][:, :].bitcast(F32),
                                        ALU.subtract).then_inc(lo_ready[p], 1)
                    if x := at(0):
                        add(x)
                    if x := at(-1):
                        sum_up(x)
                sweep(dve, body, 2, AHEAD, BEHIND)


def second_norm(nc, ctx, c, acc, g_d, b_d):
    o = Buffers()
    o.gain = ctx.enter_context(nc.sbuf_tensor("gain", [128, D], F32))
    o.offset = ctx.enter_context(nc.sbuf_tensor("offset", [128, D], F32))
    with ExitStack() as own:
        semaphores = Semaphores(nc, own)
        def sb(name, shape, dt=F32):
            return own.enter_context(nc.sbuf_tensor(f"m_{name}", shape, dt))

        def sem(name):
            return semaphores.take(f"m_{name}")
        g_col, b_col, a_col, s_col, var, mean, logv = (sb(m, [128, KC]) for m in (
            "g_col", "b_col", "a_col", "s_col", "var", "mean", "logv"))
        diag = [sb(f"diag{j}", [128, D]) for j in range(2)]
        sums_p, gain_p, offset_p = (own.enter_context(nc.psum_tensor(f"m_{m}", [128, 512], F32))
                                    for m in ("sums_p", "gain_p", "offset_p"))
        loaded, sums_ready, chain, var_ready, log_ready, rstd_ready, diag_ready, wide_ready = (
            sem(m) for m in ("loaded", "sums_ready", "chain", "var_ready", "log_ready", "rstd_ready", "diag_ready",
                             "wide_ready"))
        with nc.Block() as block:
            @block.sync
            def _(sp):
                sp.dma_start(g_col[:, :], g_d.rearrange("(k p) -> p k", p=128), allow_slow_non_contiguous=True).then_inc(loaded, 16)
                sp.dma_start(b_col[:, :], b_d.rearrange("(k p) -> p k", p=128), allow_slow_non_contiguous=True).then_inc(loaded, 16)

            @block.tensor
            def _(pe):
                t_ = nc.tensor
                for j in range(2):
                    for k in range(KC):
                        last = t_.matmul(sums_p[:, j * KC + k:j * KC + k + 1], acc[j][0:ROWS, k * 128:(k + 1) * 128],
                                         c.ones[0:ROWS, 0:1], start=True, stop=True)
                last.then_inc(sums_ready, 1)
                pe.wait_ge(diag_ready, 1)
                t_.matmul(gain_p[:, :], c.ones[:, :], diag[0][:, :], start=True, stop=True)
                t_.matmul(offset_p[:, :], c.ones[:, :], diag[1][:, :], start=True, stop=True).then_inc(wide_ready, 1)

            @block.scalar
            def _(act):
                a = nc.scalar
                a.preload_act_table_set(TABLES)
                act.wait_ge(var_ready, 1)
                a.activation(logv[:, :], var[:, :], ACT.Ln).then_inc(log_ready, 1)
                act.wait_ge(log_ready, 1)
                a.activation(var[:, :], logv[:, :], ACT.Exp, scale=-0.5).then_inc(rstd_ready, 1)

            @block.vector
            def _(dve):
                v = nc.vector
                done = [0]

                def link(ins):
                    done[0] += 1
                    ins.then_inc(chain, 1)
                    dve.wait_ge(chain, done[0])

                dve.wait_ge(sums_ready, 1)
                column_variance(v, link, sums_p, mean, a_col, var, var_ready)
                dve.wait_ge(rstd_ready, 1)
                dve.wait_ge(loaded, 32)
                link(v.tensor_tensor(a_col[:, :], var[:, :], g_col[:, :], ALU.mult))
                link(v.tensor_tensor(mean[:, :], mean[:, :], a_col[:, :], ALU.mult))
                link(v.tensor_tensor(s_col[:, :], b_col[:, :], mean[:, :], ALU.subtract))
                for j, col in enumerate((a_col, s_col)):
                    for k in range(KC):
                        ins = v.tensor_scalar(diag[j][:, k * 128:(k + 1) * 128], c.ident[:, :], col[:, k:k + 1], None,
                                              ALU.mult)
                ins.then_inc(diag_ready, 1)
                dve.wait_ge(wide_ready, 1)
                v.tensor_copy(o.gain[:, :], gain_p[:, :])
                v.tensor_copy(o.offset[:, :], offset_p[:, :])
    return o


def finish_nodes(nc, ctx, c, b, x1_d, y, out_d):
    P = 2
    with ExitStack() as own:
        semaphores = Semaphores(nc, own)
        def sb(name, shape, dt=F32):
            return own.enter_context(nc.sbuf_tensor(f"f_{name}", shape, dt))

        def sem(name):
            return semaphores.take(f"f_{name}")

        def ring(make, name, *a):
            return [make(f"{name}{u}", *a) for u in range(P)]

        x1, out = ring(sb, "x1", [ROWS, D]), ring(sb, "out", [ROWS, D])
        stats, moments = ring(sb, "stats", [ROWS, 6]), ring(sb, "moments", [ROWS, 2])
        logv, rstd, shift = ring(sb, "logv", [ROWS, 1]), ring(sb, "rstd", [ROWS, 1]), ring(sb, "shift", [ROWS, 1])
        x1_in, based, scaled, z_ready, stats_ready, moments_ready, log_ready, rstd_ready, shift_ready, out_ready, \
            stored = (ring(sem, m) for m in (
                "x1_in", "based", "scaled", "z_ready", "stats_ready", "moments_ready", "log_ready", "rstd_ready",
                "shift_ready", "out_ready", "stored"))
        AHEAD, BEHIND = 2, 2
        with nc.Block() as block:
            @block.sync
            def _(sp):
                def body(at):
                    if x := at(2):
                        p = x.par
                        sp.wait_ge(z_ready[p], x.turn)
                        for lo, hi in ROWS_CUT:
                            sp.dma_start(x1[p][lo:hi, :], x1_d[ds(ROWS * x.num + lo, hi - lo), :]).then_inc(x1_in[p], 16)
                    if x := at(-1):
                        p = x.par
                        sp.wait_ge(out_ready[p], x.turn + 1)
                        for lo, hi in ROWS_CUT:
                            sp.dma_start(out_d[ds(ROWS * x.num + lo, hi - lo), :], out[p][lo:hi, :]) \
                                .then_inc(stored[p], 16)
                sweep(sp, body, P, AHEAD, BEHIND)
                for u in range(P):
                    sp.wait_ge(stored[u], 32 * (T // P))

            @block.gpsimd
            def _(pool):
                def body(at):
                    if x := at(1):
                        p = x.par
                        pool.wait_ge(x1_in[p], 32 * (x.turn + 1))
                        nc.gpsimd.tensor_tensor(x1[p][:, :], x1[p][:, :], b.offset[0:ROWS, :], ALU.add) \
                            .then_inc(based[p], 1)
                sweep(pool, body, P, AHEAD, BEHIND)

            @block.scalar
            def _(act):
                a = nc.scalar
                a.preload_act_table_set(TABLES)

                def body(at):
                    if x := at(0):
                        p = x.par
                        act.wait_ge(moments_ready[p], x.turn + 1)
                        a.activation(logv[p][:, :], moments[p][:, 1:2], ACT.Ln, bias=c.ln_eps[0:ROWS, :]) \
                            .then_inc(log_ready[p], 1)
                        act.wait_ge(log_ready[p], x.turn + 1)
                        a.activation(rstd[p][:, :], logv[p][:, :], ACT.Exp, scale=-0.5).then_inc(rstd_ready[p], 1)
                    if x := at(-1):
                        p = x.par
                        act.wait_ge(shift_ready[p], x.turn + 1)
                        act.wait_ge(stored[p], 32 * x.turn)
                        a.activation(out[p][:, :], y[0:ROWS, ds(D * x.num, D)], ACT.Identity, bias=shift[p][:, :],
                                     scale=rstd[p][:, :]).then_inc(out_ready[p], 1)
                sweep(act, body, P, AHEAD, BEHIND)

            @block.vector
            def _(dve):
                v = nc.vector

                def body(at):
                    if x := at(0):
                        p = x.par
                        z = y[0:ROWS, ds(D * x.num, D)]
                        v.tensor_tensor(z, z, b.gain[0:ROWS, :], ALU.mult).then_inc(scaled[p], 1)
                        dve.wait_ge(scaled[p], x.turn + 1)
                        dve.wait_ge(based[p], x.turn + 1)
                        v.tensor_tensor(z, z, x1[p][:, :], ALU.add).then_inc(z_ready[p], 1)
                        dve.wait_ge(z_ready[p], x.turn + 1)
                        settle(dve)
                        v.bn_stats(stats[p][:, :], z).then_inc(stats_ready[p], 1)
                        dve.wait_ge(stats_ready[p], x.turn + 1)
                        dve.wait_ge(shift_ready[p], x.turn)
                        settle(dve)
                        v.bn_aggr(moments[p][:, :], stats[p][:, :]).then_inc(moments_ready[p], 1)
                    if x := at(-1):
                        p = x.par
                        dve.wait_ge(rstd_ready[p], x.turn + 1)
                        dve.wait_ge(out_ready[p], x.turn)
                        v.tensor_scalar(shift[p][:, :], moments[p][:, 0:1], -1.0, rstd[p][:, :], ALU.mult, ALU.mult) \
                            .then_inc(shift_ready[p], 1)
                sweep(dve, body, P, AHEAD, BEHIND)


def resnorm_gnn_pair(nc, x, src, dst, w0, g1, b1, g2, b2, w_conv, b_conv, wq, wk, wv, wo, proj, out):
    x1_d = nc.dram_tensor("x1_rows", (N, D), F32, kind="Internal").ap()
    sums_d = nc.dram_tensor("group_sums", (T * SLOTS, D), F32, kind="Internal").ap()
    with ExitStack() as ctx:
        c = lasting_constants(nc, ctx)
        acc = [ctx.enter_context(nc.sbuf_tensor(f"column_sums{j}", [SLOTS, D], F32)) for j in range(2)]
        by_dst = edge_tables(nc, ctx, "d", True)
        with ExitStack() as first:
            by_src = edge_tables(nc, first, "s", False)
            with ExitStack() as sorting:
                make_constants(nc, sorting, c)
                sort_edges(nc, c, "d", by_dst, dst, src)
                sort_edges(nc, c, "s", by_src, src, dst)
            e = edge_scores(nc, first, c, by_src, x, w0, x1_d, acc)
            attend_edges(nc, first, c, by_src, e, x, w0, x1_d, acc)
        gather_sums(nc, ctx, c, by_dst, x1_d, sums_d)
        mix = few_node_attention(nc, ctx, c, x1_d, wq, wk, wv, wo, proj)
        n = first_norm(nc, ctx, c, acc, g1, b1, w_conv, b_conv)
        y = ctx.enter_context(nc.sbuf_tensor("y", [ROWS, T * D], F32))
        convolve(nc, ctx, c, by_dst, n, mix, x1_d, sums_d, y, acc)
        b = second_norm(nc, ctx, c, acc, g2, b2)
        finish_nodes(nc, ctx, c, b, x1_d, y, out)


_INS = ['x', 'src', 'dst', 'L0_gnn_W', 'L1_gnn_norm1_g', 'L1_gnn_norm1_b', 'L1_gnn_norm2_g', 'L1_gnn_norm2_b',
        'L1_gnn_W_conv', 'L1_gnn_b_conv', 'L1_gnn_Wq', 'L1_gnn_Wk', 'L1_gnn_Wv', 'L1_gnn_Wo', 'L1_gnn_proj']


def kernel(**inputs):
    import numpy as _np
    import concourse.bacc as _bacc
    from concourse import mybir as _mybir
    from concourse.bass_utils import run_bass_kernel_spmd as _run

    nc = _bacc.Bacc("TRN2", target_bir_lowering=False, num_devices=1)
    arrays, args = {}, []
    for name in _INS:
        a = _np.ascontiguousarray(inputs[name])
        arrays[f"in_{name}"] = a
        args.append(nc.dram_tensor(f"in_{name}", a.shape, _mybir.dt.from_np(a.dtype), kind="ExternalInput").ap())
    out = nc.dram_tensor("out", (N, D), _mybir.dt.float32, kind="ExternalOutput").ap()
    resnorm_gnn_pair(nc, *args, out)
    r = _run(nc, [arrays], core_ids=[0])
    return r.results[0]["out"]
```

```python
from contextlib import ExitStack

import concourse.bass as bass
from concourse import mybir

F32 = mybir.dt.float32
F32R = mybir.dt.float32r
BF16 = mybir.dt.bfloat16
I32 = mybir.dt.int32
U32 = mybir.dt.uint32
ALU = mybir.AluOpType
ACT = mybir.ActivationFunctionType
AX = mybir.AxisListType

N = 10000
E = 10000
D = 512
H = 8
DH = D // H
KC = D // 128
ROWS = 125
T = N // ROWS
SLOTS = ROWS + 1
NEVER = 16384
BIG = 1e30
ROUND = 12582912.0
LN_EPS = 1e-5
BN_EPS = 1e-5
KEPS = 1e-6
MAXN = 64
M = 256

ds = bass.ds


class Semaphores:

    def __init__(self, nc, own):
        self.nc, self.own, self.numbers = nc, own, []
        own.callback(self.clear)

    def take(self, name):
        s = self.own.enter_context(self.nc.semaphore(name))
        self.numbers.append(s.num)
        return s

    def clear(self):
        numbers = sorted(self.numbers)
        with self.nc.Block() as block:
            @block.gpsimd
            def _(pool):
                lo = 0
                for k in range(1, len(numbers) + 1):
                    if k == len(numbers) or numbers[k] != numbers[k - 1] + 1:
                        pool.sem_clear(range(numbers[lo], numbers[k - 1] + 1))
                        lo = k


class Buffers:
    pass


def lasting_constants(nc, ctx):
    c = Buffers()
    c.ident = ctx.enter_context(nc.sbuf_tensor("ident", [128, 128], F32))
    c.ones = ctx.enter_context(nc.sbuf_tensor("ones", [128, 128], F32))
    c.ln_eps = ctx.enter_context(nc.sbuf_tensor("ln_eps", [128, 1], F32))
    c.pool_dma = lambda name: ctx.enter_context(nc.semaphore(name))
    return c


def make_constants(nc, ctx, c):

    def sb(name, shape, dt=F32):
        return ctx.enter_context(nc.sbuf_tensor(name, shape, dt))

    c.ramp_i = sb("ramp_i", [128, 128], I32)
    c.ramp = sb("ramp", [128, 128])
    c.row_i = sb("row_i", [128, 1], I32)
    c.row = sb("row", [128, 1])
    c.node_i = sb("node_i", [ROWS, T], I32)
    c.node = sb("node", [ROWS, T])
    c.before = sb("before", [128, 128])
    c.upper = sb("upper", [128, 128])
    c.shift = sb("shift", [SLOTS, SLOTS])
    c.wrap = sb("wrap", [SLOTS, SLOTS])
    c.keep = sb("keep", [SLOTS, SLOTS])
    c.lift = sb("lift", [SLOTS, SLOTS])
    c.zeros = sb("zeros", [128, 512])
    semaphores = Semaphores(nc, ctx)
    made = semaphores.take("constants_made")
    cleared = semaphores.take("constants_cleared")
    ramps = semaphores.take("ramps_made")

    with nc.Block() as block:
        @block.gpsimd
        def _(pool):
            g = nc.gpsimd
            g.iota(c.ramp_i[:, :], [[1, 128]], base=0, channel_multiplier=0).then_inc(ramps, 1)
            g.iota(c.row_i[:, :], [[0, 1]], base=0, channel_multiplier=1).then_inc(ramps, 1)
            g.iota(c.node_i[:, :], [[ROWS, T]], base=0, channel_multiplier=1).then_inc(ramps, 1)
            pool.wait_ge(cleared, 7)
            for mat, size, base in ((c.ident, 128, 0), (c.shift, SLOTS, -1)):
                g.affine_select(out=mat[0:size, 0:size], in_=mat[0:size, 0:size], compare_op=ALU.not_equal,
                                fill=1.0, base=-base, pattern=[[-1, size]], channel_multiplier=1).then_inc(made, 1)
            g.affine_select(out=c.keep[:, :], in_=c.keep[:, :], compare_op=ALU.not_equal, fill=1.0,
                            base=0, pattern=[[-1, SLOTS]], channel_multiplier=1).then_inc(made, 1)
            g.affine_select(out=c.before[:, :], in_=c.ones[:, :], compare_op=ALU.is_gt, fill=0.0,
                            base=0, pattern=[[-1, 128]], channel_multiplier=1).then_inc(made, 1)
            g.affine_select(out=c.upper[:, :], in_=c.ones[:, :], compare_op=ALU.is_gt, fill=0.0,
                            base=0, pattern=[[1, 128]], channel_multiplier=-1).then_inc(made, 1)
            g.affine_select(out=c.wrap[:, :], in_=c.wrap[:, :], compare_op=ALU.not_equal, fill=1.0,
                            base=-(ROWS * 128 + 1), pattern=[[1, SLOTS]], channel_multiplier=128).then_inc(made, 1)
            g.affine_select(out=c.lift[:, :], in_=c.lift[:, :], compare_op=ALU.not_equal, fill=1.0,
                            base=-128, pattern=[[1, SLOTS]], channel_multiplier=128).then_inc(made, 1)

        @block.vector
        def _(dve):
            v = nc.vector
            for mat in (c.ident, c.shift, c.keep, c.wrap, c.lift, c.zeros):
                v.memset(mat[:, :], 0.0).then_inc(cleared, 1)
            v.memset(c.ones[:, :], 1.0).then_inc(cleared, 1)
            v.memset(c.ln_eps[:, :], LN_EPS)
            dve.wait_ge(ramps, 3)
            v.tensor_copy(c.ramp[:, :], c.ramp_i[:, :])
            v.tensor_copy(c.row[:, :], c.row_i[:, :])
            v.tensor_copy(c.node[:, :], c.node_i[:, :])
            dve.wait_ge(made, 7)
            v.memset(c.keep[0:1, 0:1], 0.0)
            v.memset(c.shift[0:1, 0:2], 0.0)


def pairs(eng, body):
    body(0)
    with eng.Fori(1, T // 2) as i:
        body(i)


def divide(v, dve, link, out, x, rows):
    link(v.tensor_scalar(out[0:rows, :], x[0:rows, :], -62.0, 1.0 / ROWS, ALU.add, ALU.mult))
    link(v.tensor_scalar(out[0:rows, :], out[0:rows, :], ROUND, None, ALU.add))
    link(v.tensor_scalar(out[0:rows, :], out[0:rows, :], -ROUND, None, ALU.add))


def edge_tables(nc, ctx, tag, brief):
    o = Buffers()

    def keep(name, shape, dt=F32):
        return ctx.enter_context(nc.sbuf_tensor(f"{tag}_{name}", shape, dt))

    def only_full(*a):
        return None if brief else keep(*a)

    o.key_row = only_full("key_row", [SLOTS, T], U32)
    o.val_row = keep("val_row", [SLOTS, T], U32)
    o.first_row = only_full("first_row", [SLOTS, T], U32)
    o.first = only_full("first", [SLOTS, T])
    o.key_in = keep("key_in", [SLOTS, T])
    o.key_out = keep("key_out", [SLOTS, T])
    o.cut = only_full("cut", [SLOTS, T])
    o.empty = only_full("empty", [ROWS, T])
    o.empty_row = only_full("empty_row", [SLOTS, T], U32)
    o.has = keep("has", [ROWS, T])
    o.inverse = keep("inverse", [SLOTS, T])
    o.sum_row = keep("sum_row", [SLOTS, T], U32)
    return o


def sort_buffers(nc, own, semaphores, tag, o, key_d, val_d):
    j = Buffers()
    j.o, j.key_d, j.val_d = o, key_d, val_d

    def sb(name, shape, dt=F32):
        return own.enter_context(nc.sbuf_tensor(f"{tag}_{name}", shape, dt))

    def pb(name, rows):
        return [own.enter_context(nc.psum_tensor(f"{tag}_{name}{u}", [rows, 512], F32)) for u in range(2)]

    def sem(name):
        return semaphores.take(f"{tag}_{name}")

    def two(make, name, *a):
        return [make(f"{name}{u}", *a) for u in range(2)]

    j.key_i = sb("key_i", [ROWS, T], I32)
    j.val_i = sb("val_i", [ROWS, T], I32)
    j.digits = sb("digits", [ROWS, T, 2])
    j.key, j.key_tile, j.key_slot, j.key1, j.val1, j.rank, j.start, j.pos, j.pos_tile, j.pos_slot, j.node_cnt, \
        j.empty = (sb(m, [ROWS, T]) for m in (
            "key", "key_tile", "key_slot", "key1", "val1", "rank", "start", "pos", "pos_tile", "pos_slot",
            "node_cnt", "no_edge"))
    j.slot_hot, j.tile_hot = two(sb, "slot_hot", [ROWS, ROWS], BF16), two(sb, "tile_hot", [ROWS, T], BF16)
    j.counts = sb("counts", [ROWS, T, T])
    j.summed = sb("summed", [ROWS, T, T])
    j.base = sb("base", [ROWS, 1])
    j.column = two(sb, "column", [ROWS, 2])
    j.slot_hot_t = two(sb, "slot_hot_t", [ROWS, ROWS])
    j.junk, j.junk2 = two(sb, "junk", [ROWS, ROWS]), two(sb, "junk2", [ROWS, T])
    j.out_hot = two(sb, "out_hot", [ROWS, SLOTS])
    j.place_hot = two(sb, "place_hot", [ROWS, T])
    j.payload = two(sb, "payload", [ROWS, 2, T])
    j.ks = sb("ks", [SLOTS, T + 2])
    j.vs, j.same, j.tmp = sb("vs", [SLOTS, T]), sb("same", [SLOTS, T]), sb("tmp", [SLOTS, T])
    j.tmp_i = sb("tmp_i", [SLOTS, T], I32)

    j.rows_p = pb("rows_p", SLOTS)
    j.look = pb("look", SLOTS)
    j.hist, j.sorted_p, j.edge_p = j.look, j.look[0], j.rows_p[0]

    j.loaded, j.chain, j.digits_ready, j.base_asked, j.base_ready, j.starts_ready, j.pos_ready, j.sorted_ready, \
        j.sorted_kept, j.edges_ready = (sem(m) for m in (
            "loaded", "chain", "digits_ready", "base_asked", "base_ready", "starts_ready", "pos_ready",
            "sorted_ready", "sorted_kept", "edges_ready"))
    j.hot_ready, j.hist_ready, j.hist_kept, j.column_ready, j.rows_ready, j.hot_t_ready, j.ranked, \
        j.look_ready, j.looked, j.placed, j.payload_ready, j.payload_used = (two(sem, m) for m in (
            "hot_ready", "hist_ready", "hist_kept", "column_ready", "rows_ready", "hot_t_ready",
            "ranked", "look_ready", "looked", "placed", "payload_ready", "payload_used"))
    return j


def sort_edges(nc, c, jobs):
    with ExitStack() as own:
        semaphores = Semaphores(nc, own)
        jobs = [sort_buffers(nc, own, semaphores, *job) for job in jobs]
        lanes = [(j, u) for j in jobs for u in range(2)]

        with nc.Block() as block:
            @block.sync
            def _(sp):
                for j in jobs:
                    sp.dma_start(j.key_i[:, :], j.key_d.rearrange("(p t) -> p t", t=T)).then_inc(j.loaded, 16)
                    sp.dma_start(j.val_i[:, :], j.val_d.rearrange("(p t) -> p t", t=T)).then_inc(j.loaded, 16)

            @block.vector
            def _(dve):
                v = nc.vector

                def linked(j):
                    def link(ins):
                        j.links = j.links + 1
                        ins.then_inc(j.chain, 1)
                        dve.wait_ge(j.chain, j.links)
                    return link

                for j in jobs:
                    j.links, j.link = 0, linked(j)

                for j in jobs:
                    link = j.link
                    dve.wait_ge(j.loaded, 32)
                    v.tensor_copy(j.key[:, :], j.key_i[:, :])
                    link(v.tensor_copy(j.val1[:, :], j.val_i[:, :]))
                    v.tensor_scalar(j.key1[:, :], j.key[:, :], 1.0, None, ALU.add)
                    link(v.tensor_scalar(j.val1[:, :], j.val1[:, :], 1.0, None, ALU.add))
                    divide(v, dve, link, j.key_tile, j.key, ROWS)
                    link(v.scalar_tensor_tensor(j.key_slot[:, :], j.key_tile[:, :], -float(ROWS), j.key[:, :],
                                                ALU.mult, ALU.add))
                    v.tensor_copy(j.digits[:, :, 0], j.key[:, :])
                    v.tensor_copy(j.digits[:, :, 1], j.key_slot[:, :]).then_inc(j.digits_ready, 1)

                for j in jobs:
                    dve.wait_ge(j.digits_ready, 1)

                def one_hot(i):
                    for j, u in lanes:
                        dve.wait_ge(j.hist_ready[u], i)
                        v.tensor_scalar(j.slot_hot[u][:, :], c.ramp[0:ROWS, 0:ROWS],
                                        j.key_slot[:, ds(2 * i + u, 1)], None, ALU.is_equal)
                        v.tensor_scalar(j.tile_hot[u][:, :], c.ramp[0:ROWS, 0:T],
                                        j.key_tile[:, ds(2 * i + u, 1)], None,
                                        ALU.is_equal).then_inc(j.hot_ready[u], 1)
                pairs(dve, one_hot)

                for j in jobs:
                    for u in range(2):
                        dve.wait_ge(j.hist_kept[u], T // 2)
                    counts, summed = (m[:, :, :].rearrange("p a t -> p (a t)") for m in (j.counts, j.summed))
                    j.link(v.tensor_tensor_scan(summed, counts, counts, 0.0, ALU.add, ALU.bypass))
                    v.memset(j.ks[:, :], 0.0).then_inc(j.base_asked, 1)
                for j in jobs:
                    link = j.link
                    counts, summed = (m[:, :, :].rearrange("p a t -> p (a t)") for m in (j.counts, j.summed))
                    dve.wait_ge(j.base_ready, 1)
                    link(v.tensor_copy(j.base[:, :], j.edge_p[0:ROWS, 0:1]))
                    link(v.tensor_scalar(j.node_cnt[:, :], j.summed[:, :, T - 1], j.base[:, :], None, ALU.add))
                    v.scalar_tensor_tensor(counts, summed, j.base[:, :], counts,
                                           ALU.add, ALU.subtract).then_inc(j.starts_ready, 1)

                def place_edges(i):
                    for j, u in lanes:
                        dve.wait_ge(j.rows_ready[u], i + 1)
                        dve.wait_ge(j.look_ready[u], i)
                        v.tensor_scalar(j.slot_hot_t[u][:, :], j.rows_p[u][0:ROWS, ROWS:2 * ROWS], c.row[0:ROWS, :],
                                        None, ALU.is_equal).then_inc(j.hot_t_ready[u], 1)
                        dve.wait_ge(j.ranked[u], i)
                        v.scalar_tensor_tensor(j.junk[u][:, :], j.rows_p[u][0:ROWS, 0:ROWS],
                                               j.digits[:, ds(2 * i + u, 1), 0:1].rearrange("p a b -> p (a b)"),
                                               c.before[0:ROWS, 0:ROWS], ALU.is_equal, ALU.mult,
                                               accum_out=j.rank[:, ds(2 * i + u, 1)]).then_inc(j.ranked[u], 1)
                    for j, u in lanes:
                        dve.wait_ge(j.looked[u], i)
                        dve.wait_ge(j.look_ready[u], i + 1)
                        v.scalar_tensor_tensor(j.junk2[u][:, :], c.ramp[0:ROWS, 0:T],
                                               j.key_tile[:, ds(2 * i + u, 1)], j.look[u][0:ROWS, 0:T],
                                               ALU.is_equal, ALU.mult,
                                               accum_out=j.start[:, ds(2 * i + u, 1)]).then_inc(j.looked[u], 1)
                pairs(dve, place_edges)
                for j in jobs:
                    link = j.link
                    for u in range(2):
                        dve.wait_ge(j.looked[u], T // 2)
                        dve.wait_ge(j.ranked[u], T // 2)
                    link(v.tensor_tensor(j.pos[:, :], j.start[:, :], j.rank[:, :], ALU.add))
                    divide(v, dve, link, j.pos_tile, j.pos, ROWS)
                    link(v.scalar_tensor_tensor(j.pos_slot[:, :], j.pos_tile[:, :], -float(ROWS), j.pos[:, :],
                                                ALU.mult, ALU.add))
                    v.tensor_scalar(j.pos_slot[:, :], j.pos_slot[:, :], 1.0, None, ALU.add).then_inc(j.pos_ready, 1)
                for j in jobs:
                    dve.wait_ge(j.pos_ready, 1)

                def permute(i):
                    for j, u in lanes:
                        dve.wait_ge(j.payload_used[u], i)
                        v.tensor_scalar(j.out_hot[u][:, :], c.ramp[0:ROWS, 0:SLOTS], j.pos_slot[:, ds(2 * i + u, 1)],
                                        None, ALU.is_equal)
                        dve.wait_ge(j.payload_ready[u], i)
                        v.tensor_scalar(j.place_hot[u][:, :], c.ramp[0:ROWS, 0:T], j.pos_tile[:, ds(2 * i + u, 1)],
                                        None, ALU.is_equal).then_inc(j.placed[u], 1)
                pairs(dve, permute)

                for j in jobs:
                    link, o = j.link, j.o
                    dve.wait_ge(j.starts_ready, 1)
                    link(v.tensor_tensor(j.node_cnt[:, :], j.node_cnt[:, :], j.counts[:, :, 0], ALU.subtract))
                    link(v.tensor_scalar(o.has[:, :], j.node_cnt[:, :], 1.0, None, ALU.min))
                    link(v.tensor_scalar(j.empty[:, :], o.has[:, :], -1.0, 1.0, ALU.mult, ALU.add))
                    link(v.tensor_scalar(j.tmp[0:ROWS, :], j.node_cnt[:, :], 1.0, None, ALU.max))
                    link(v.memset(o.inverse[:, :], 0.0))
                    link(v.reciprocal(j.tmp[0:ROWS, :], j.tmp[0:ROWS, :]))
                    link(v.tensor_tensor(o.inverse[0:ROWS, :], j.tmp[0:ROWS, :], o.has[:, :], ALU.mult))
                    link(v.memset(j.tmp_i[:, :], NEVER))
                    if o.empty_row is not None:
                        v.tensor_copy(o.empty[:, :], j.empty[:, :])
                        link(v.scalar_tensor_tensor(j.tmp_i[0:ROWS, :], o.has[:, :], float(NEVER), c.node[:, :],
                                                    ALU.mult, ALU.add))
                        link(v.tensor_copy(o.empty_row[:, :], j.tmp_i[:, :]))
                    link(v.tensor_copy(j.start[:, :], j.counts[:, :, 0]))
                    divide(v, dve, link, j.rank, j.start, ROWS)
                    link(v.scalar_tensor_tensor(j.start[:, :], j.start[:, :], 1.0, j.rank[:, :], ALU.add, ALU.add))
                    link(v.scalar_tensor_tensor(j.start[:, :], j.empty[:, :], float(NEVER), j.start[:, :],
                                                ALU.mult, ALU.add))
                    link(v.tensor_copy(j.tmp_i[0:ROWS, :], j.start[:, :]))
                    link(v.tensor_copy(o.sum_row[:, :], j.tmp_i[:, :]))

                for j in jobs:
                    dve.wait_ge(j.sorted_ready, 1)
                    v.memset(j.ks[:, 0:1], -1.0)
                    v.memset(j.ks[:, T + 1:T + 2], -2.0)
                    v.tensor_copy(j.ks[:, 1:T + 1], j.sorted_p[:, 0:T]).then_inc(j.sorted_kept, 1)
                for j in jobs:
                    link, o = j.link, j.o
                    link(v.tensor_copy(j.vs[:, :], j.sorted_p[:, T:2 * T]))
                    link(v.tensor_scalar(j.tmp[:, :], j.vs[:, :], -1.0, 0.0, ALU.add, ALU.max))
                    link(v.tensor_copy(j.tmp_i[:, :], j.tmp[:, :]))
                    link(v.tensor_copy(o.val_row[:, :], j.tmp_i[:, :]))
                    dve.wait_ge(j.sorted_kept, 1)
                    link(v.tensor_scalar(j.tmp[:, :], j.ks[:, 1:T + 1], -1.0, 0.0, ALU.add, ALU.max))
                    link(v.tensor_copy(j.tmp_i[:, :], j.tmp[:, :]))
                    if o.key_row is not None:
                        link(v.tensor_copy(o.key_row[:, :], j.tmp_i[:, :]))
                    dve.wait_ge(j.edges_ready, 1)
                    v.tensor_copy(o.key_in[:, :], j.edge_p[:, T:2 * T])
                    v.tensor_copy(o.key_out[:, :], j.edge_p[:, 2 * T:3 * T])
                    if o.first is not None:
                        link(v.tensor_tensor(j.same[:, :], j.ks[:, 1:T + 1], j.edge_p[:, 0:T], ALU.is_equal))
                        v.tensor_scalar(o.first[:, :], j.same[:, :], -1.0, 1.0, ALU.mult, ALU.add)
                        v.tensor_scalar(o.cut[:, :], j.same[:, :], -1.0, BIG, ALU.add, ALU.mult)
                        link(v.scalar_tensor_tensor(j.tmp_i[:, :], j.same[:, :], float(NEVER), j.tmp[:, :],
                                                    ALU.mult, ALU.add))
                        v.tensor_copy(o.first_row[:, :], j.tmp_i[:, :])

            @block.scalar
            def _(act):
                for j in jobs:
                    act.wait_ge(j.digits_ready, 1)

                def keep_counts(i):
                    for j, u in lanes:
                        act.wait_ge(j.hist_ready[u], i + 1)
                        nc.scalar.activation(j.counts[:, :, ds(2 * i + u, 1)].rearrange("p a b -> p (a b)"),
                                             j.hist[u][0:ROWS, 0:T], ACT.Copy).then_inc(j.hist_kept[u], 1)
                pairs(act, keep_counts)

                def take_column(i):
                    for j, u in lanes:
                        act.wait_ge(j.rows_ready[u], i)
                        nc.scalar.activation(j.column[u][:, :], j.digits[:, ds(2 * i + u, 1), :]
                                             .rearrange("p a b -> p (a b)"), ACT.Copy).then_inc(j.column_ready[u], 1)
                pairs(act, take_column)

                def fill_places(i):
                    for j, u in lanes:
                        act.wait_ge(j.payload_used[u], i)
                        act.wait_ge(j.placed[u], i + 1)
                        for at, val in ((0, j.key1), (1, j.val1)):
                            last = nc.scalar.activation(j.payload[u][:, at, :], j.place_hot[u][:, :], ACT.Copy,
                                                        scale=val[:, ds(2 * i + u, 1)])
                        last.then_inc(j.payload_ready[u], 1)
                pairs(act, fill_places)

            @block.tensor
            def _(pe):
                t_ = nc.tensor

                def count(i):
                    for j, u in lanes:
                        pe.wait_ge(j.hist_kept[u], i)
                        pe.wait_ge(j.hot_ready[u], i + 1)
                        t_.matmul(j.hist[u][0:ROWS, 0:T], j.slot_hot[u][:, :], j.tile_hot[u][:, :],
                                  start=True, stop=True).then_inc(j.hist_ready[u], 1)
                pairs(pe, count)
                for j in jobs:
                    pe.wait_ge(j.base_asked, 1)
                    t_.matmul(j.edge_p[0:ROWS, 0:1], c.upper[0:ROWS, 0:ROWS],
                              j.summed[:, T - 1, T - 1:T], start=True, stop=True).then_inc(j.base_ready, 1)
                for j in jobs:
                    pe.wait_ge(j.starts_ready, 1)

                def look_up(i):
                    for j, u in lanes:
                        pe.wait_ge(j.column_ready[u], i + 1)
                        pe.wait_ge(j.ranked[u], i)
                        pe.wait_ge(j.hot_t_ready[u], i)
                        t_.matmul(j.rows_p[u][0:ROWS, 0:ROWS], j.column[u][:, 0:1].to_broadcast([ROWS, ROWS]),
                                  c.ident[0:ROWS, 0:ROWS], start=True, stop=True)
                        t_.matmul(j.rows_p[u][0:ROWS, ROWS:2 * ROWS], j.column[u][:, 1:2].to_broadcast([ROWS, ROWS]),
                                  c.ident[0:ROWS, 0:ROWS], start=True, stop=True).then_inc(j.rows_ready[u], 1)
                    for j, u in lanes:
                        pe.wait_ge(j.looked[u], i)
                        pe.wait_ge(j.hot_t_ready[u], i + 1)
                        t_.matmul(j.look[u][0:ROWS, 0:T], j.slot_hot_t[u][:, :],
                                  j.counts[:, :, ds(2 * i + u, 1)].rearrange("p a b -> p (a b)"),
                                  start=True, stop=True).then_inc(j.look_ready[u], 1)
                pairs(pe, look_up)
                for j in jobs:
                    for u in range(2):
                        pe.wait_ge(j.looked[u], T // 2)
                    t_.matmul(j.sorted_p[:, 0:2 * T], c.zeros[:, 0:SLOTS], c.zeros[:, 0:2 * T], start=True, stop=False)

                def gather_permuted(i):
                    for j, u in lanes:
                        pe.wait_ge(j.payload_ready[u], i + 1)
                        t_.matmul(j.sorted_p[:, 0:2 * T], j.out_hot[u][:, :],
                                  j.payload[u][:, :, :].rearrange("p a b -> p (a b)"),
                                  start=False, stop=False).then_inc(j.payload_used[u], 1)
                pairs(pe, gather_permuted)
                for j in jobs:
                    t_.matmul(j.sorted_p[:, 0:2 * T], c.zeros[:, 0:SLOTS], c.zeros[:, 0:2 * T],
                              start=False, stop=True).then_inc(j.sorted_ready, 1)
                for j in jobs:
                    ks = j.ks
                    pe.wait_ge(j.sorted_kept, 1)
                    for at, mats in ((0, ((c.shift, 1), (c.wrap, 0))), (T, ((c.keep, 1), (c.lift, 2))),
                                     (2 * T, ((c.keep, 1), (c.lift, 1)))):
                        for k, (mat, first) in enumerate(mats):
                            last = t_.matmul(j.edge_p[:, at:at + T], mat[:, :], ks[:, first:first + T],
                                             start=(k == 0), stop=(k == 1))
                    last.then_inc(j.edges_ready, 1)


def settle(eng):
    eng.nop(nofuse=True)


class Tile:

    def __init__(self, period, i, c):
        self.period, self.i, self.c = period, i, c
        self.par = c % period
        self.turn = i + c // period
        self.num = period * i + c

    def before(self, n=1):
        return Tile(self.period, self.i, self.c - n)

    def after(self):
        return Tile(self.period, self.i, self.c + 1)

    def is_last(self):
        return isinstance(self.i, int) and self.num == T - 1

    def is_zero(self):
        return isinstance(self.i, int) and self.num == 0


def sweep(eng, body, period, ahead, behind):
    lo = 1 - (-behind // period)
    hi = (T - ahead) // period

    def fixed(s):
        def at(k):
            return Tile(period, 0, s + k) if 0 <= s + k < T else None
        body(at)

    for s in range(-ahead, lo * period):
        fixed(s)
    with eng.Fori(lo, hi) as i:
        for c in range(period):
            body(lambda k, c=c: Tile(period, i, c + k))
    for s in range(hi * period, T + behind):
        fixed(s)


class Chain:

    def __init__(self, eng, sem, each):
        self.eng, self.sem, self.each = eng, sem, each

    def at(self, x):
        k = [0]

        def link(ins):
            k[0] += 1
            ins.then_inc(self.sem, 1)
            self.eng.wait_ge(self.sem, self.each * x.num + k[0])
        return link


ROWS_CUT = ((0, 112), (112, ROWS))
TABLES = "natural_log_exp_and_others"


def split_weights(nc, ctx, semaphores, name, w_d, lo_col, hi_col):
    n = hi_col - lo_col
    hi = ctx.enter_context(nc.sbuf_tensor(f"{name}_hi", [128, KC, n], F32R))
    lo = ctx.enter_context(nc.sbuf_tensor(f"{name}_lo", [128, KC, n], F32R))
    with nc.sbuf_tensor(f"{name}_raw", [128, KC, n], F32) as raw, \
            nc.Block() as block:
        loaded, high = semaphores.take(f"{name}_loaded"), semaphores.take(f"{name}_high")

        @block.sync
        def _(sp):
            sp.dma_start(raw[:, :, :], w_d.rearrange("(k p) n -> p k n", p=128)[:, :, lo_col:hi_col]) \
                .then_inc(loaded, 16)

        @block.scalar
        def _(act):
            act.wait_ge(loaded, 16)
            nc.scalar.copy(hi[:, :, :], raw[:, :, :]).then_inc(high, 1)

        @block.vector
        def _(dve):
            dve.wait_ge(high, 1)
            nc.vector.tensor_tensor(lo[:, :, :], raw[:, :, :], hi[:, :, :].bitcast(F32), ALU.subtract)
    return hi, lo


def product(t, out, x_hi, x_lo, w_hi, w_lo, rows):
    for k in range(KC):
        xh = x_hi[:, k * rows:(k + 1) * rows]
        t.matmul(out, xh, w_hi[:, k, :], start=(k == 0), stop=False)
        t.matmul(out, xh, w_lo[:, k, :], start=False, stop=False)
        last = t.matmul(out, x_lo[:, k * rows:(k + 1) * rows], w_hi[:, k, :], start=False, stop=(k == KC - 1))
    return last


def edge_scores(nc, ctx, c, s, x_d, w_d, x1_d):
    o = Buffers()
    o.aw = ctx.enter_context(nc.sbuf_tensor("aw_all", [H, E], F32))
    o.cut = ctx.enter_context(nc.sbuf_tensor("cut_all", [H, E + 1], BF16))
    o.run_max = ctx.enter_context(nc.sbuf_tensor("run_max", [H, E + 1], F32))
    with ExitStack() as own:
        semaphores = Semaphores(nc, own)
        def sb(name, shape, dt=F32):
            return own.enter_context(nc.sbuf_tensor(f"a_{name}", shape, dt))

        def pb(name, shape):
            return own.enter_context(nc.psum_tensor(f"a_{name}", shape, F32))

        def sem(name):
            return semaphores.take(f"a_{name}")

        def two(make, name, *a):
            return [make(f"{name}{u}", *a) for u in range(2)]

        wq = split_weights(nc, own, semaphores, "wq", w_d, 0, D)
        wk = split_weights(nc, own, semaphores, "wk", w_d, D, 2 * D)

        src_idx, dst_idx = two(sb, "src_idx", [SLOTS, 1], U32), two(sb, "dst_idx", [SLOTS, 1], U32)
        empty_idx = two(sb, "empty_idx", [SLOTS, 1], U32)
        xs, xd = two(sb, "xs", [SLOTS, D]), two(sb, "xd", [SLOTS, D])
        xs_hi, xs_lo = two(sb, "xs_hi", [128, KC * SLOTS], F32R), two(sb, "xs_lo", [128, KC * SLOTS], F32R)
        xd_hi, xd_lo = two(sb, "xd_hi", [128, KC * SLOTS], F32R), two(sb, "xd_lo", [128, KC * SLOTS], F32R)
        q = two(sb, "q", [SLOTS, D])
        qk = two(sb, "qk", [SLOTS, D])
        aw_col, cut_col = two(sb, "aw_col", [SLOTS, H]), two(sb, "cut_col", [SLOTS, H])
        xn = two(sb, "xn", [ROWS, D])
        x1n = two(sb, "x1n", [SLOTS, D])
        stats, moments = two(sb, "stats", [ROWS, 6]), two(sb, "moments", [ROWS, 2])
        logv, rstd, shift = two(sb, "logv", [ROWS, 1]), two(sb, "rstd", [ROWS, 1]), two(sb, "shift", [ROWS, 1])

        turned_s, turned_d = pb("turned_s", [128, 512]), pb("turned_d", [128, 512])
        q_p, k_p = two(pb, "q_p", [SLOTS, 512]), two(pb, "k_p", [SLOTS, 512])
        score_p = two(pb, "score_p", [H, 512])

        cleared = sem("cleared")
        idx_ready = two(sem, "idx_ready")
        xs_in, xd_in = two(c.pool_dma, "a_xs_in"), two(c.pool_dma, "a_xd_in")
        turned_s_ready, turned_d_ready = two(sem, "turned_s_ready"), two(sem, "turned_d_ready")
        hi_s_ready, hi_d_ready = two(sem, "hi_s_ready"), two(sem, "hi_d_ready")
        lo_s_ready, lo_d_ready = two(sem, "lo_s_ready"), two(sem, "lo_d_ready")
        q_ready, k_ready, q_kept = two(sem, "q_ready"), two(sem, "k_ready"), two(sem, "q_kept")
        prod_ready, aw_ready = two(sem, "prod_ready"), two(sem, "aw_ready")
        score_ready, scanned = two(sem, "score_ready"), two(sem, "scanned")
        xn_in, stats_ready, moments_ready = two(sem, "xn_in"), two(sem, "stats_ready"), two(sem, "moments_ready")
        log_ready, rstd_ready, shift_ready = two(sem, "log_ready"), two(sem, "rstd_ready"), two(sem, "shift_ready")
        x1n_ready = two(sem, "x1n_ready")
        cut_kept = sem("cut_kept")
        empty_idx_ready, x1n_out = two(sem, "empty_idx_ready"), two(c.pool_dma, "a_x1n_out")

        AHEAD, BEHIND = 2, 2
        with nc.Block() as block:
            @block.sync
            def _(sp):
                def load_nodes(x):
                    sp.wait_ge(x1n_ready[x.par], x.turn)
                    sp.wait_ge(stats_ready[x.par], x.turn)
                    for a, b in ROWS_CUT:
                        sp.dma_start(xn[x.par][a:b, :], x_d[ds(ROWS * x.num + a, b - a), :]) \
                            .then_inc(xn_in[x.par], 16)

                def body(at):
                    if x := at(2):
                        load_nodes(x)
                sweep(sp, body, 2, AHEAD, BEHIND)

            @block.gpsimd
            def _(pool):
                g = nc.gpsimd

                def gather(x):
                    p = x.par
                    pool.wait_ge(turned_s_ready[p], x.turn)
                    pool.wait_ge(turned_d_ready[p], x.turn)
                    g.tensor_copy(src_idx[p][:, :], s.key_row[:, ds(x.num, 1)])
                    g.tensor_copy(dst_idx[p][:, :], s.val_row[:, ds(x.num, 1)]).then_inc(idx_ready[p], 1)
                    pool.wait_ge(idx_ready[p], x.turn + 1)
                    settle(pool)
                    g.indirect_dma_start(xs[p][:, :], None, x_d, bass.IndirectOffsetOnAxis(src_idx[p][:, :], 0)) \
                        .then_inc(xs_in[p], 16)
                    settle(pool)
                    g.indirect_dma_start(xd[p][:, :], None, x_d, bass.IndirectOffsetOnAxis(dst_idx[p][:, :], 0)) \
                        .then_inc(xd_in[p], 16)

                def scatter_empty(x):
                    p = x.par
                    pool.wait_ge(x1n_out[p], 16 * x.turn)
                    g.tensor_copy(empty_idx[p][:, :], s.empty_row[:, ds(x.num, 1)]).then_inc(empty_idx_ready[p], 1)
                    pool.wait_ge(empty_idx_ready[p], x.turn + 1)
                    pool.wait_ge(x1n_ready[p], x.turn + 1)
                    settle(pool)
                    g.indirect_dma_start(x1_d, bass.IndirectOffsetOnAxis(empty_idx[p][:, :], 0), x1n[p][:, :], None,
                                         bounds_check=N - 1, oob_is_err=False).then_inc(x1n_out[p], 16)

                pool.wait_ge(cleared, 1)
                def body(at):
                    if x := at(2):
                        gather(x)
                    if x := at(-1):
                        scatter_empty(x)
                sweep(pool, body, 2, AHEAD, BEHIND)
                for u in range(2):
                    pool.wait_ge(x1n_out[u], 16 * (T // 2))

            @block.tensor
            def _(pe):
                t_ = nc.tensor

                def turn(x, x_in, rows, out, lo_ready, ready):
                    p = x.par
                    pe.wait_ge(x_in[p], 16 * (x.turn + 1))
                    if not x.is_zero():
                        b = x.before()
                        pe.wait_ge(lo_ready[b.par], b.turn + 1)
                    for k in range(KC):
                        last = t_.transpose(out[:, k * SLOTS:(k + 1) * SLOTS],
                                            rows[p][:, k * 128:(k + 1) * 128], c.ident[0:SLOTS, 0:SLOTS])
                    last.then_inc(ready[p], 1)

                def query(x):
                    p = x.par
                    pe.wait_ge(hi_s_ready[p], x.turn + 1)
                    pe.wait_ge(lo_s_ready[p], x.turn + 1)
                    pe.wait_ge(q_kept[p], x.turn)
                    product(t_, q_p[p][:, 0:D], xs_hi[p], xs_lo[p], *wq, SLOTS).then_inc(q_ready[p], 1)

                def keys(x):
                    p = x.par
                    pe.wait_ge(hi_d_ready[p], x.turn + 1)
                    pe.wait_ge(lo_d_ready[p], x.turn + 1)
                    pe.wait_ge(prod_ready[p], x.turn)
                    product(t_, k_p[p][:, 0:D], xd_hi[p], xd_lo[p], *wk, SLOTS).then_inc(k_ready[p], 1)

                def scores(x):
                    p = x.par
                    pe.wait_ge(aw_ready[p], x.turn + 1)
                    pe.wait_ge(scanned[p], x.turn)
                    t_.transpose(score_p[p][:, 0:SLOTS], aw_col[p][:, :], c.ident[0:SLOTS, 0:SLOTS])
                    t_.transpose(score_p[p][:, SLOTS:2 * SLOTS], cut_col[p][:, :], c.ident[0:SLOTS, 0:SLOTS]) \
                        .then_inc(score_ready[p], 1)

                def body(at):
                    if x := at(0):
                        query(x)
                    if x := at(1):
                        turn(x, xs_in, xs, turned_s, lo_s_ready, turned_s_ready)
                    if x := at(0):
                        keys(x)
                    if x := at(-1):
                        scores(x)
                    if x := at(1):
                        turn(x, xd_in, xd, turned_d, lo_d_ready, turned_d_ready)
                sweep(pe, body, 2, AHEAD, BEHIND)

            @block.scalar
            def _(act):
                a = nc.scalar
                a.preload_act_table_set(TABLES)

                def high(x, turned_ready, turned, used, hi, ready):
                    p = x.par
                    act.wait_ge(turned_ready[p], x.turn + 1)
                    act.wait_ge(used[p], x.turn)
                    a.copy(hi[p][:, :], turned[:, 0:KC * SLOTS]).then_inc(ready[p], 1)

                def deviation(x):
                    p = x.par
                    act.wait_ge(moments_ready[p], x.turn + 1)
                    a.activation(logv[p][:, :], moments[p][:, 1:2], ACT.Ln, bias=c.ln_eps[0:ROWS, :]) \
                        .then_inc(log_ready[p], 1)
                    act.wait_ge(log_ready[p], x.turn + 1)
                    a.activation(rstd[p][:, :], logv[p][:, :], ACT.Exp, scale=-0.5).then_inc(rstd_ready[p], 1)

                def normalise(x):
                    p = x.par
                    act.wait_ge(shift_ready[p], x.turn + 1)
                    act.wait_ge(x1n_out[p], 16 * x.turn)
                    a.activation(x1n[p][0:ROWS, :], xn[p][:, :], ACT.Identity, bias=shift[p][:, :],
                                 scale=rstd[p][:, :]).then_inc(x1n_ready[p], 1)

                def keep_q(x):
                    p = x.par
                    act.wait_ge(q_ready[p], x.turn + 1)
                    act.wait_ge(prod_ready[p], x.turn)
                    a.mul(q[p][:, :], q_p[p][:, 0:D], DH ** -0.5).then_inc(q_kept[p], 1)

                act.wait_ge(cleared, 1)
                def body(at):
                    if x := at(0):
                        keep_q(x)
                    if x := at(1):
                        high(x, turned_s_ready, turned_s, q_ready, xs_hi, hi_s_ready)
                    if x := at(-1):
                        normalise(x)
                    if x := at(0):
                        deviation(x)
                    if x := at(1):
                        high(x, turned_d_ready, turned_d, k_ready, xd_hi, hi_d_ready)
                sweep(act, body, 2, AHEAD, BEHIND)

            @block.vector
            def _(dve):
                v = nc.vector
                v.memset(o.cut[:, E:E + 1], -BIG)
                v.memset(o.run_max[:, 0:1], -BIG)
                for u in range(2):
                    v.memset(x1n[u][:, :], 0.0)
                v.memset(score_p[0][:, 0:1], 0.0).then_inc(cleared, 1)
                dve.wait_ge(cleared, 1)

                def low(x, hi_ready, turned, hi, lo, ready):
                    p = x.par
                    dve.wait_ge(hi_ready[p], x.turn + 1)
                    v.tensor_tensor(lo[p][:, :], turned[:, 0:KC * SLOTS], hi[p][:, :].bitcast(F32),
                                    ALU.subtract).then_inc(ready[p], 1)

                def measure(x):
                    p = x.par
                    dve.wait_ge(xn_in[p], 32 * (x.turn + 1))
                    dve.wait_ge(rstd_ready[p], x.turn)
                    v.bn_stats(stats[p][:, :], xn[p][:, :]).then_inc(stats_ready[p], 1)
                    dve.wait_ge(stats_ready[p], x.turn + 1)
                    settle(dve)
                    v.bn_aggr(moments[p][:, :], stats[p][:, :]).then_inc(moments_ready[p], 1)

                def centre(x):
                    p = x.par
                    dve.wait_ge(rstd_ready[p], x.turn + 1)
                    dve.wait_ge(moments_ready[p], x.turn + 1)
                    v.tensor_scalar(shift[p][:, :], moments[p][:, 0:1], -1.0, rstd[p][:, :], ALU.mult, ALU.mult) \
                        .then_inc(shift_ready[p], 1)

                def scan(x):
                    p = x.par
                    dve.wait_ge(score_ready[p], x.turn + 1)
                    v.tensor_copy(o.aw[:, ds(ROWS * x.num, ROWS)], score_p[p][:, 1:SLOTS])
                    v.tensor_copy(o.cut[:, ds(ROWS * x.num, ROWS)], score_p[p][:, SLOTS + 1:2 * SLOTS]) \
                        .then_inc(cut_kept, 1)
                    dve.wait_ge(cut_kept, x.num + 1)
                    if not x.is_zero():
                        b = x.before()
                        dve.wait_ge(scanned[b.par], b.turn + 1)
                    v.tensor_tensor_scan(o.run_max[:, ds(ROWS * x.num + 1, ROWS)], o.cut[:, ds(ROWS * x.num, ROWS)],
                                         score_p[p][:, 1:SLOTS], o.run_max[:, ds(ROWS * x.num, 1)],
                                         ALU.add, ALU.max).then_inc(scanned[p], 1)

                def score(x):
                    p = x.par
                    dve.wait_ge(score_ready[p], x.turn)
                    v.tensor_copy(cut_col[p][:, :], s.cut[:, ds(x.num, 1)].to_broadcast([SLOTS, H]))
                    dve.wait_ge(q_kept[p], x.turn + 1)
                    dve.wait_ge(k_ready[p], x.turn + 1)
                    dve.wait_ge(aw_ready[p], x.turn)
                    v.tensor_tensor(qk[p][:, :], q[p][:, :], k_p[p][:, 0:D], ALU.mult).then_inc(prod_ready[p], 1)
                    dve.wait_ge(prod_ready[p], x.turn + 1)
                    v.tensor_reduce(aw_col[p][:, :], qk[p][:, :].rearrange("p (h d) -> p h d", h=H),
                                    op=ALU.add, axis=AX.X).then_inc(aw_ready[p], 1)

                def body(at):
                    if x := at(1):
                        low(x, hi_s_ready, turned_s, xs_hi, xs_lo, lo_s_ready)
                    if x := at(0):
                        measure(x)
                    if x := at(-2):
                        scan(x)
                    if x := at(0):
                        score(x)
                    if x := at(1):
                        low(x, hi_d_ready, turned_d, xd_hi, xd_lo, lo_d_ready)
                    if x := at(0):
                        centre(x)
                sweep(dve, body, 2, AHEAD, BEHIND)
    return o


def attend_edges(nc, ctx, c, s, e, x_d, w_d, x1_d):
    with ExitStack() as own:
        semaphores = Semaphores(nc, own)
        def sb(name, shape, dt=F32):
            return own.enter_context(nc.sbuf_tensor(f"b_{name}", shape, dt))

        def pb(name, shape):
            return own.enter_context(nc.psum_tensor(f"b_{name}", shape, F32))

        def sem(name):
            return semaphores.take(f"b_{name}")

        def two(make, name, *a):
            return [make(f"{name}{u}", *a) for u in range(2)]

        wv = split_weights(nc, own, semaphores, "wv", w_d, 2 * D, 3 * D)

        dst_idx, res_idx, out_idx = (two(sb, n, [SLOTS, 1], U32) for n in ("dst_idx", "res_idx", "out_idx"))
        xd, xr = two(sb, "xd", [SLOTS, D]), two(sb, "xr", [SLOTS, D])
        xd_hi, xd_lo = two(sb, "xd_hi", [128, KC * SLOTS], F32R), two(sb, "xd_lo", [128, KC * SLOTS], F32R)
        top = two(sb, "top", [H, SLOTS])
        gap = two(sb, "gap", [H, ROWS])
        cut_next, run_max = two(sb, "cut_next", [H, ROWS]), two(sb, "run_max", [H, ROWS])
        prob = two(sb, "prob", [H, SLOTS])
        key_col = two(sb, "key_col", [SLOTS, 1])
        group = two(sb, "group", [SLOTS, SLOTS])
        pv = two(sb, "pv", [SLOTS, D + H])
        recip = two(sb, "recip", [SLOTS, H])
        mixed = two(sb, "mixed", [SLOTS, D])
        x1 = two(sb, "x1", [SLOTS, D])
        stats, moments = two(sb, "stats", [SLOTS, 6]), two(sb, "moments", [SLOTS, 2])
        logv, rstd, shift = two(sb, "logv", [SLOTS, 1]), two(sb, "rstd", [SLOTS, 1]), two(sb, "shift", [SLOTS, 1])

        turned_p = pb("turned_p", [128, 512])
        v_p, acc_p = two(pb, "v_p", [SLOTS, 512]), two(pb, "acc_p", [SLOTS, 512])
        small_p = two(pb, "small_p", [SLOTS, 512])
        weight_p = pb("weight_p", [SLOTS, 512])
        KEYS, PROB = slice(0, SLOTS), slice(128, 128 + H)

        cleared = sem("cleared")
        dst_idx_ready, res_idx_ready, out_idx_ready = (two(sem, n) for n in ("dst_ir", "res_ir", "out_ir"))
        xd_in, xr_in, x1_out = two(c.pool_dma, "b_xd_in"), two(c.pool_dma, "b_xr_in"), two(c.pool_dma, "b_x1_out")
        turned_ready, hi_ready, lo_ready = two(sem, "turned_ready"), two(sem, "hi_ready"), two(sem, "lo_ready")
        gap_ready, prob_ready, top_ready = two(sem, "gap_ready"), two(sem, "prob_ready"), sem("top_ready")
        col_ready, prob_t_ready, prob_kept = two(sem, "col_ready"), two(sem, "prob_t_ready"), two(sem, "prob_kept")
        keys_ready, group_ready = two(sem, "keys_ready"), two(sem, "group_ready")
        v_ready, pv_ready, carried = two(sem, "v_ready"), two(sem, "pv_ready"), two(sem, "carried")
        sum_ready, mixed_ready = two(sem, "sum_ready"), two(sem, "mixed_ready")
        finish_links = sem("finish_links")
        recip_ready = two(sem, "recip_ready")
        scan_in_ready = two(sem, "scan_in_ready")
        moments_ready, log_ready, rstd_ready = two(sem, "moments_ready"), two(sem, "log_ready"), two(sem, "rstd_ready")
        shift_ready, x1_ready = two(sem, "shift_ready"), two(sem, "x1_ready")

        AHEAD, BEHIND = 2, 3

        def place(x):
            return (T - 1) - x.num

        with nc.Block() as block:
            @block.gpsimd
            def _(pool):
                g = nc.gpsimd

                def gather_dst(x):
                    p = x.par
                    pool.wait_ge(turned_ready[p], x.turn)
                    settle(pool)
                    g.tensor_copy(dst_idx[p][:, :], s.val_row[:, ds(place(x), 1)]).then_inc(dst_idx_ready[p], 1)
                    pool.wait_ge(dst_idx_ready[p], x.turn + 1)
                    settle(pool)
                    g.indirect_dma_start(xd[p][:, :], None, x_d, bass.IndirectOffsetOnAxis(dst_idx[p][:, :], 0)) \
                        .then_inc(xd_in[p], 16)

                def gather_residual(x):
                    p = x.par
                    pool.wait_ge(mixed_ready[p], x.turn)
                    settle(pool)
                    g.tensor_copy(res_idx[p][:, :], s.first_row[:, ds(place(x), 1)]).then_inc(res_idx_ready[p], 1)
                    pool.wait_ge(res_idx_ready[p], x.turn + 1)
                    settle(pool)
                    g.indirect_dma_start(xr[p][:, :], None, x_d, bass.IndirectOffsetOnAxis(res_idx[p][:, :], 0),
                                         bounds_check=N - 1, oob_is_err=False).then_inc(xr_in[p], 16)

                def scatter(x):
                    p = x.par
                    pool.wait_ge(x1_out[p], 16 * x.turn)
                    settle(pool)
                    g.tensor_copy(out_idx[p][:, :], s.first_row[:, ds(place(x), 1)]).then_inc(out_idx_ready[p], 1)
                    pool.wait_ge(out_idx_ready[p], x.turn + 1)
                    pool.wait_ge(x1_ready[p], x.turn + 1)
                    settle(pool)
                    g.indirect_dma_start(x1_d, bass.IndirectOffsetOnAxis(out_idx[p][:, :], 0), x1[p][:, :], None,
                                         bounds_check=N - 1, oob_is_err=False).then_inc(x1_out[p], 16)

                pool.wait_ge(cleared, 1)
                def body(at):
                    if x := at(2):
                        gather_dst(x)
                    if x := at(-3):
                        scatter(x)
                    if x := at(0):
                        gather_residual(x)
                sweep(pool, body, 2, AHEAD, BEHIND)
                for u in range(2):
                    pool.wait_ge(x1_out[u], 16 * (T // 2))

            @block.tensor
            def _(pe):
                t_ = nc.tensor

                def turn(x):
                    p = x.par
                    pe.wait_ge(xd_in[p], 16 * (x.turn + 1))
                    if not x.is_zero():
                        b = x.before()
                        pe.wait_ge(lo_ready[b.par], b.turn + 1)
                    for k in range(KC):
                        last = t_.transpose(turned_p[:, k * SLOTS:(k + 1) * SLOTS],
                                            xd[p][:, k * 128:(k + 1) * 128], c.ident[0:SLOTS, 0:SLOTS])
                    last.then_inc(turned_ready[p], 1)

                def small(x):
                    p = x.par
                    pe.wait_ge(prob_ready[p], x.turn + 1)
                    pe.wait_ge(prob_kept[p], x.turn)
                    pe.wait_ge(group_ready[p], x.turn)
                    settle(pe)
                    t_.transpose(small_p[p][:, PROB], prob[p][:, :], c.ident[0:H, 0:H]).then_inc(prob_t_ready[p], 1)
                    pe.wait_ge(col_ready[p], x.turn + 1)
                    t_.matmul(small_p[p][:, KEYS], key_col[p][:, :].to_broadcast([SLOTS, SLOTS]),
                              c.ident[0:SLOTS, 0:SLOTS], start=True, stop=True).then_inc(keys_ready[p], 1)

                def values(x):
                    p = x.par
                    pe.wait_ge(hi_ready[p], x.turn + 1)
                    pe.wait_ge(lo_ready[p], x.turn + 1)
                    pe.wait_ge(pv_ready[p], x.turn)
                    product(t_, v_p[p][:, 0:D], xd_hi[p], xd_lo[p], *wv, SLOTS).then_inc(v_ready[p], 1)

                def group_sum(x):
                    p = x.par
                    pe.wait_ge(group_ready[p], x.turn + 1)
                    pe.wait_ge(carried[p], x.turn + 1)
                    pe.wait_ge(mixed_ready[p], x.turn)
                    if not x.is_zero():
                        b = x.before()
                        pe.wait_ge(recip_ready[b.par], b.turn + 1)
                    t_.matmul(acc_p[p][:, 0:D], group[p][:, :], pv[p][:, 0:D], start=True, stop=True)
                    t_.matmul(weight_p[:, 0:H], group[p][:, :], pv[p][:, D:D + H],
                              start=True, stop=True).then_inc(sum_ready[p], 1)

                def body(at):
                    if x := at(1):
                        turn(x)
                        small(x)
                    if x := at(0):
                        values(x)
                    if x := at(-1):
                        group_sum(x)
                sweep(pe, body, 2, AHEAD, BEHIND)

            @block.scalar
            def _(act):
                a = nc.scalar
                a.preload_act_table_set(TABLES)

                def high(x):
                    p = x.par
                    act.wait_ge(turned_ready[p], x.turn + 1)
                    act.wait_ge(v_ready[p], x.turn)
                    a.copy(xd_hi[p][:, :], turned_p[:, 0:KC * SLOTS]).then_inc(hi_ready[p], 1)

                def carry(x):
                    p = x.par
                    act.wait_ge(pv_ready[p], x.turn + 1)
                    if not x.is_zero():
                        b = x.before()
                        act.wait_ge(sum_ready[b.par], b.turn + 1)
                    a.copy(pv[p][0:1, 0:D], acc_p[1 - p][0:1, 0:D])
                    a.copy(pv[p][0:1, D:D + H], weight_p[0:1, 0:H]).then_inc(carried[p], 1)

                def exps(x):
                    p = x.par
                    act.wait_ge(gap_ready[p], x.turn + 1)
                    act.wait_ge(prob_t_ready[p], x.turn)
                    a.activation(prob[p][:, 1:SLOTS], gap[p][:, :], ACT.Exp).then_inc(prob_ready[p], 1)

                def norm(x):
                    p = x.par
                    act.wait_ge(moments_ready[p], x.turn + 1)
                    a.activation(logv[p][:, :], moments[p][:, 1:2], ACT.Ln, bias=c.ln_eps[0:SLOTS, :]) \
                        .then_inc(log_ready[p], 1)
                    act.wait_ge(log_ready[p], x.turn + 1)
                    a.activation(rstd[p][:, :], logv[p][:, :], ACT.Exp, scale=-0.5).then_inc(rstd_ready[p], 1)
                    act.wait_ge(shift_ready[p], x.turn + 1)
                    act.wait_ge(x1_out[p], 16 * x.turn)
                    a.activation(x1[p][:, :], mixed[p][:, :], ACT.Identity, bias=shift[p][:, :],
                                 scale=rstd[p][:, :]).then_inc(x1_ready[p], 1)

                act.wait_ge(cleared, 1)
                def body(at):
                    if x := at(1):
                        high(x)
                    if x := at(-1):
                        carry(x)
                    if x := at(2):
                        exps(x)
                    if x := at(-2):
                        norm(x)
                sweep(act, body, 2, AHEAD, BEHIND)

            @block.vector
            def _(dve):
                v = nc.vector
                for u in range(2):
                    v.memset(prob[u][:, :], 0.0)
                    v.memset(xr[u][:, :], 0.0)
                v.memset(top[1][:, :], 0.0)
                v.memset(acc_p[1][:, :], 0.0)
                v.memset(weight_p[:, :], 0.0).then_inc(cleared, 1)
                dve.wait_ge(cleared, 1)
                links = Chain(dve, finish_links, 2)

                def maximum(x):
                    p = x.par
                    at_ = ROWS * place(x)
                    if not x.is_zero():
                        dve.wait_ge(top_ready, x.num)
                    dve.wait_ge(gap_ready[p], x.turn)
                    settle(dve)
                    v.tensor_copy(cut_next[p][:, :], e.cut[:, ds(at_ + 1, ROWS)])
                    v.tensor_copy(run_max[p][:, :], e.run_max[:, ds(at_ + 1, ROWS)]).then_inc(scan_in_ready[p], 1)
                    dve.wait_ge(scan_in_ready[p], x.turn + 1)
                    v.tensor_tensor_scan(top[p][:, 1:SLOTS][:, ::-1], cut_next[p][:, ::-1],
                                         run_max[p][:, ::-1], top[1 - p][:, 1:2],
                                         ALU.add, ALU.max).then_inc(top_ready, 1)
                    dve.wait_ge(top_ready, x.num + 1)
                    dve.wait_ge(prob_ready[p], x.turn)
                    settle(dve)
                    v.tensor_tensor(gap[p][:, :], e.aw[:, ds(at_, ROWS)], top[p][:, 1:SLOTS],
                                    ALU.subtract).then_inc(gap_ready[p], 1)
                    dve.wait_ge(keys_ready[p], x.turn)
                    settle(dve)
                    v.tensor_copy(key_col[p][:, :], s.key_out[:, ds(place(x), 1)]).then_inc(col_ready[p], 1)

                def low(x):
                    p = x.par
                    dve.wait_ge(hi_ready[p], x.turn + 1)
                    v.tensor_tensor(xd_lo[p][:, :], turned_p[:, 0:KC * SLOTS], xd_hi[p][:, :].bitcast(F32),
                                    ALU.subtract).then_inc(lo_ready[p], 1)

                def same_group(x):
                    p = x.par
                    dve.wait_ge(keys_ready[p], x.turn + 1)
                    dve.wait_ge(sum_ready[p], x.turn)
                    v.tensor_copy(pv[p][:, D:D + H], small_p[p][:, PROB]).then_inc(prob_kept[p], 1)
                    dve.wait_ge(keys_ready[p], x.turn + 1)
                    settle(dve)
                    v.tensor_scalar(group[p][:, :], small_p[p][:, KEYS], s.key_in[:, ds(place(x), 1)], None,
                                    ALU.is_equal).then_inc(group_ready[p], 1)

                def weigh(x):
                    p = x.par
                    dve.wait_ge(v_ready[p], x.turn + 1)
                    dve.wait_ge(prob_kept[p], x.turn + 1)
                    v.tensor_tensor(pv[p][:, 0:D].rearrange("p (h d) -> p h d", h=H),
                                    v_p[p][:, 0:D].rearrange("p (h d) -> p h d", h=H),
                                    pv[p][:, D:D + H].unsqueeze(2).to_broadcast([SLOTS, H, DH]),
                                    ALU.mult).then_inc(pv_ready[p], 1)

                def finish(x):
                    p = x.par
                    link = links.at(x)
                    dve.wait_ge(sum_ready[p], x.turn + 1)
                    dve.wait_ge(x1_ready[p], x.turn)
                    if not x.is_last():
                        n = x.after()
                        dve.wait_ge(carried[n.par], n.turn + 1)
                    v.reciprocal(recip[p][:, :], weight_p[:, 0:H]).then_inc(recip_ready[p], 1)
                    dve.wait_ge(recip_ready[p], x.turn + 1)
                    link(v.tensor_tensor(mixed[p][:, :].rearrange("p (h d) -> p h d", h=H),
                                         acc_p[p][:, 0:D].rearrange("p (h d) -> p h d", h=H),
                                         recip[p][:, :].unsqueeze(2).to_broadcast([SLOTS, H, DH]), ALU.mult))
                    dve.wait_ge(xr_in[p], 16 * (x.turn + 1))
                    v.tensor_tensor(mixed[p][:, :], mixed[p][:, :], xr[p][:, :], ALU.add).then_inc(mixed_ready[p], 1)
                    dve.wait_ge(mixed_ready[p], x.turn + 1)
                    link(v.bn_stats(stats[p][:, :], mixed[p][:, :]))
                    dve.wait_ge(shift_ready[p], x.turn)
                    settle(dve)
                    v.bn_aggr(moments[p][:, :], stats[p][:, :]).then_inc(moments_ready[p], 1)

                def centre(x):
                    p = x.par
                    dve.wait_ge(rstd_ready[p], x.turn + 1)
                    dve.wait_ge(moments_ready[p], x.turn + 1)
                    v.tensor_scalar(shift[p][:, :], moments[p][:, 0:1], -1.0, rstd[p][:, :], ALU.mult, ALU.mult) \
                        .then_inc(shift_ready[p], 1)

                def body(at):
                    if x := at(-1):
                        weigh(x)
                    if x := at(1):
                        low(x)
                    if x := at(0):
                        same_group(x)
                    if x := at(2):
                        maximum(x)
                    if x := at(-2):
                        finish(x)
                    if x := at(-2):
                        centre(x)
                sweep(dve, body, 2, AHEAD, BEHIND)


def gather_sums(nc, ctx, c, s, x1_d, sums_d, acc):
    P = 4
    with ExitStack() as own:
        semaphores = Semaphores(nc, own)
        def sb(name, shape, dt=F32):
            return own.enter_context(nc.sbuf_tensor(f"g_{name}", shape, dt))

        def sem(name):
            return semaphores.take(f"g_{name}")

        def ring(make, name, *a):
            return [make(f"{name}{u}", *a) for u in range(P)]

        idx = ring(sb, "idx", [SLOTS, 1], U32)
        rows = ring(sb, "rows", [SLOTS, D])
        key_col = ring(sb, "key_col", [SLOTS, 1])
        group = ring(sb, "group", [SLOTS, SLOTS])
        total = ring(sb, "total", [SLOTS, D])
        nodes, sq = ring(sb, "nodes", [ROWS, D]), ring(sb, "sq", [ROWS, D])
        sum_p = [own.enter_context(nc.psum_tensor(f"g_sum_p{u}", [SLOTS, 512], F32)) for u in range(P)]
        keys_p = [own.enter_context(nc.psum_tensor(f"g_keys_p{u}", [SLOTS, 512], F32)) for u in range(P)]

        cleared = sem("cleared")
        rows_in = ring(c.pool_dma, "g_rows_in")
        idx_ready, col_ready, keys_ready, group_ready, carried, sum_ready, total_ready, total_out = (
            ring(sem, n) for n in ("idx_ready", "col_ready", "keys_ready", "group_ready", "carried",
                                   "sum_ready", "total_ready", "total_out"))
        nodes_in, sq_ready, summed, summed_sq = (ring(sem, n) for n in ("nodes_in", "sq_ready", "summed",
                                                                        "summed_sq"))
        AHEAD, BEHIND = 4, 1

        def place(x):
            return (T - 1) - x.num

        with nc.Block() as block:
            @block.gpsimd
            def _(pool):
                g = nc.gpsimd

                def body(at):
                    if x := at(3):
                        p = x.par
                        pool.wait_ge(sum_ready[p], x.turn)
                        settle(pool)
                        g.tensor_copy(idx[p][:, :], s.val_row[:, ds(place(x), 1)]).then_inc(idx_ready[p], 1)
                        pool.wait_ge(idx_ready[p], x.turn + 1)
                        settle(pool)
                        g.indirect_dma_start(rows[p][:, :], None, x1_d, bass.IndirectOffsetOnAxis(idx[p][:, :], 0)) \
                            .then_inc(rows_in[p], 16)
                sweep(pool, body, P, AHEAD, BEHIND)

            @block.tensor
            def _(pe):
                t_ = nc.tensor

                def body(at):
                    if x := at(1):
                        p = x.par
                        pe.wait_ge(col_ready[p], x.turn + 1)
                        pe.wait_ge(group_ready[p], x.turn)
                        t_.matmul(keys_p[p][:, 0:SLOTS], key_col[p][:, :].to_broadcast([SLOTS, SLOTS]),
                                  c.ident[0:SLOTS, 0:SLOTS], start=True, stop=True).then_inc(keys_ready[p], 1)
                    if x := at(0):
                        p = x.par
                        pe.wait_ge(group_ready[p], x.turn + 1)
                        pe.wait_ge(carried[p], x.turn + 1)
                        pe.wait_ge(total_ready[p], x.turn)
                        t_.matmul(sum_p[p][:, 0:D], group[p][:, :], rows[p][:, :],
                                  start=True, stop=True).then_inc(sum_ready[p], 1)
                sweep(pe, body, P, AHEAD, BEHIND)

            @block.scalar
            def _(act):
                a = nc.scalar
                act.wait_ge(cleared, 1)

                def body(at):
                    if x := at(0):
                        p = x.par
                        act.wait_ge(rows_in[p], 16 * (x.turn + 1))
                        if not x.is_zero():
                            b = x.before()
                            act.wait_ge(sum_ready[b.par], b.turn + 1)
                        a.copy(rows[p][0:1, :], sum_p[x.before().par][0:1, 0:D]).then_inc(carried[p], 1)
                        act.wait_ge(nodes_in[p], 32 * (x.turn + 1))
                        act.wait_ge(summed_sq[p], x.turn)
                        a.activation(sq[p][:, :], nodes[p][:, :], ACT.Square).then_inc(sq_ready[p], 1)
                sweep(act, body, P, AHEAD, BEHIND)

            @block.vector
            def _(dve):
                v = nc.vector
                for m in acc:
                    v.memset(m[:, :], 0.0)
                v.memset(sum_p[P - 1][:, :], 0.0).then_inc(cleared, 1)
                dve.wait_ge(cleared, 1)

                def body(at):
                    if x := at(2):
                        p = x.par
                        dve.wait_ge(keys_ready[p], x.turn)
                        settle(dve)
                        v.tensor_copy(key_col[p][:, :], s.key_out[:, ds(place(x), 1)]).then_inc(col_ready[p], 1)
                    if x := at(1):
                        p = x.par
                        dve.wait_ge(keys_ready[p], x.turn + 1)
                        dve.wait_ge(sum_ready[p], x.turn)
                        settle(dve)
                        v.tensor_scalar(group[p][:, :], keys_p[p][:, 0:SLOTS], s.key_in[:, ds(place(x), 1)], None,
                                        ALU.is_equal).then_inc(group_ready[p], 1)
                    if x := at(-1):
                        p = x.par
                        dve.wait_ge(sum_ready[p], x.turn + 1)
                        dve.wait_ge(total_out[p], 16 * x.turn)
                        if not x.is_last():
                            n = x.after()
                            dve.wait_ge(carried[n.par], n.turn + 1)
                        v.tensor_copy(total[p][:, :], sum_p[p][:, 0:D]).then_inc(total_ready[p], 1)
                        dve.wait_ge(nodes_in[p], 32 * (x.turn + 1))
                        if not x.is_zero():
                            b = x.before()
                            dve.wait_ge(summed[b.par], b.turn + 1)
                            dve.wait_ge(summed_sq[b.par], b.turn + 1)
                        v.tensor_tensor(acc[0][0:ROWS, :], acc[0][0:ROWS, :], nodes[p][:, :],
                                        ALU.add).then_inc(summed[p], 1)
                        dve.wait_ge(sq_ready[p], x.turn + 1)
                        v.tensor_tensor(acc[1][0:ROWS, :], acc[1][0:ROWS, :], sq[p][:, :],
                                        ALU.add).then_inc(summed_sq[p], 1)
                sweep(dve, body, P, AHEAD, BEHIND)

            @block.sync
            def _(sp):
                def body(at):
                    if x := at(2):
                        p = x.par
                        sp.wait_ge(summed[p], x.turn)
                        sp.wait_ge(sq_ready[p], x.turn)
                        for lo, hi in ROWS_CUT:
                            sp.dma_start(nodes[p][lo:hi, :], x1_d[ds(ROWS * x.num + lo, hi - lo), :]) \
                                .then_inc(nodes_in[p], 16)
                    if x := at(-1):
                        p = x.par
                        sp.wait_ge(total_ready[p], x.turn + 1)
                        settle(sp)
                        sp.dma_start(sums_d[ds(SLOTS * place(x), SLOTS), :], total[p][:, :]).then_inc(total_out[p], 16)
                sweep(sp, body, P, AHEAD, BEHIND)
                for u in range(P):
                    sp.wait_ge(total_out[u], 16 * (T // P))


def column_variance(v, link, sums_p, mean, square, var, ready):
    link(v.tensor_scalar(mean[:, :], sums_p[:, 0:KC], 1.0 / N, None, ALU.mult))
    link(v.tensor_scalar(var[:, :], sums_p[:, KC:2 * KC], 1.0 / N, None, ALU.mult))
    link(v.tensor_tensor(square[:, :], mean[:, :], mean[:, :], ALU.mult))
    link(v.tensor_tensor(var[:, :], var[:, :], square[:, :], ALU.subtract))
    v.tensor_scalar(var[:, :], var[:, :], 0.0, BN_EPS, ALU.max, ALU.add).then_inc(ready, 1)


def first_norm(nc, ctx, c, acc, g_d, b_d, w_d, bias_d):
    o = Buffers()

    def keep(name, shape, dt=F32):
        return ctx.enter_context(nc.sbuf_tensor(f"n_{name}", shape, dt))

    o.w_hi, o.w_lo = keep("w_hi", [128, KC, D], F32R), keep("w_lo", [128, KC, D], F32R)
    o.shift_w, o.bias = keep("shift_w", [128, D]), keep("bias", [128, D])
    with ExitStack() as own:
        semaphores = Semaphores(nc, own)
        def sb(name, shape, dt=F32):
            return own.enter_context(nc.sbuf_tensor(f"n_{name}", shape, dt))

        def sem(name):
            return semaphores.take(f"n_{name}")
        w = sb("w", [128, KC, D])
        w_scaled = sb("w_scaled", [128, KC, D])
        g_col, b_col, a_col, s_col, var, mean = (sb(n, [128, KC]) for n in ("g_col", "b_col", "a_col", "s_col", "var", "mean"))
        logv = sb("logv", [128, KC])
        bias_row, shift_row = sb("bias_row", [1, D]), sb("shift_row", [1, D])
        sums_p = own.enter_context(nc.psum_tensor("n_sums_p", [128, 512], F32))
        row_p = own.enter_context(nc.psum_tensor("n_row_p", [128, 512], F32))
        wide_p = own.enter_context(nc.psum_tensor("n_wide_p", [128, 512], F32))
        wide2_p = own.enter_context(nc.psum_tensor("n_wide2_p", [128, 512], F32))
        loaded, sums_ready, chain, var_ready, log_ready, rstd_ready, shift_ready, row_ready, row_kept, wide_ready, \
            scaled, high = (sem(n) for n in ("loaded", "sums_ready", "chain", "var_ready", "log_ready", "rstd_ready",
                                             "shift_ready", "row_ready", "row_kept", "wide_ready", "scaled", "high"))
        with nc.Block() as block:
            @block.sync
            def _(sp):
                sp.dma_start(w[:, :, :], w_d.rearrange("(k p) n -> p k n", p=128)).then_inc(loaded, 16)
                sp.dma_start(g_col[:, :], g_d.rearrange("(k p) -> p k", p=128), allow_slow_non_contiguous=True).then_inc(loaded, 16)
                sp.dma_start(b_col[:, :], b_d.rearrange("(k p) -> p k", p=128), allow_slow_non_contiguous=True).then_inc(loaded, 16)
                sp.dma_start(bias_row[:, :], bias_d.rearrange("(a n) -> a n", a=1)).then_inc(loaded, 16)

            @block.tensor
            def _(pe):
                t_ = nc.tensor
                for j in range(2):
                    for k in range(KC):
                        last = t_.matmul(sums_p[:, j * KC + k:j * KC + k + 1], acc[j][:, k * 128:(k + 1) * 128],
                                         c.ones[0:SLOTS, 0:1], start=True, stop=True)
                last.then_inc(sums_ready, 1)
                pe.wait_ge(shift_ready, 1)
                pe.wait_ge(loaded, 64)
                for k in range(KC):
                    last = t_.matmul(row_p[0:1, 0:D], s_col[:, k:k + 1], w[:, k, :], start=(k == 0), stop=(k == KC - 1))
                last.then_inc(row_ready, 1)
                t_.matmul(wide2_p[:, 0:D], c.ones[0:1, :], bias_row[:, :], start=True, stop=True)
                pe.wait_ge(row_kept, 1)
                t_.matmul(wide_p[:, 0:D], c.ones[0:1, :], shift_row[:, :], start=True, stop=True).then_inc(wide_ready, 1)

            @block.scalar
            def _(act):
                a = nc.scalar
                a.preload_act_table_set(TABLES)
                act.wait_ge(var_ready, 1)
                a.activation(logv[:, :], var[:, :], ACT.Ln).then_inc(log_ready, 1)
                act.wait_ge(log_ready, 1)
                a.activation(var[:, :], logv[:, :], ACT.Exp, scale=-0.5).then_inc(rstd_ready, 1)
                act.wait_ge(row_ready, 1)
                a.copy(shift_row[:, :], row_p[0:1, 0:D]).then_inc(row_kept, 1)
                act.wait_ge(scaled, KC)
                a.copy(o.w_hi[:, :, :], w_scaled[:, :, :]).then_inc(high, 1)

            @block.vector
            def _(dve):
                v = nc.vector
                done = [0]

                def link(ins):
                    done[0] += 1
                    ins.then_inc(chain, 1)
                    dve.wait_ge(chain, done[0])

                dve.wait_ge(sums_ready, 1)
                column_variance(v, link, sums_p, mean, a_col, var, var_ready)
                dve.wait_ge(rstd_ready, 1)
                dve.wait_ge(loaded, 64)
                link(v.tensor_tensor(a_col[:, :], var[:, :], g_col[:, :], ALU.mult))
                link(v.tensor_tensor(mean[:, :], mean[:, :], a_col[:, :], ALU.mult))
                v.tensor_tensor(s_col[:, :], b_col[:, :], mean[:, :], ALU.subtract).then_inc(shift_ready, 1)
                for k in range(KC):
                    v.tensor_scalar(w_scaled[:, k, :], w[:, k, :], a_col[:, k:k + 1], None, ALU.mult).then_inc(scaled, 1)
                dve.wait_ge(high, 1)
                v.tensor_tensor(o.w_lo[:, :, :], w_scaled[:, :, :], o.w_hi[:, :, :].bitcast(F32), ALU.subtract)
                dve.wait_ge(wide_ready, 1)
                v.tensor_copy(o.shift_w[:, :], wide_p[:, 0:D])
                v.tensor_copy(o.bias[:, :], wide2_p[:, 0:D])
    return o


def few_node_attention(nc, ctx, c, x1_d, wq_d, wk_d, wv_d, wo_d, proj_d):
    o = Buffers()
    o.first_mix = ctx.enter_context(nc.sbuf_tensor("first_mix", [128, D], F32))
    o.rest_mix = ctx.enter_context(nc.sbuf_tensor("rest_mix", [128, D], F32))
    MC = M // 128
    W1 = DH + 1
    with ExitStack() as own:
        semaphores = Semaphores(nc, own)
        def sb(name, shape, dt=F32):
            return own.enter_context(nc.sbuf_tensor(f"t_{name}", shape, dt))

        def sem(name):
            return semaphores.take(f"t_{name}")

        h = sb("h", [MAXN, D])
        wq, wk, wv, wo = (sb(n, [128, KC, D]) for n in ("wq", "wk", "wv", "wo"))
        proj, proj_t = sb("proj", [128, MC, DH]), sb("proj_t", [DH, M])
        h_t = sb("h_t", [128, KC * MAXN])
        q_t, k_t, q_sq, k_sq = (sb(n, [DH, H * MAXN]) for n in ("q_t", "k_t", "q_sq", "k_sq"))
        half = sb("half", [DH, 1])
        v1 = sb("v1", [MAXN, H, W1])
        qf, kf = sb("qf", [MAXN, H * M]), sb("kf", [MAXN, H * M])
        diag, peak, bias = sb("diag", [MAXN, 2 * H]), sb("peak", [MAXN, 2 * H]), sb("bias", [MAXN, 2 * H])
        peak_t = sb("peak_t", [H, 1])
        qf_t = sb("qf_t", [128, H * MC * MAXN])
        kv = sb("kv", [128, H * MC, W1])
        z = sb("z", [MAXN, H])
        attn, attn_t, out = sb("attn", [MAXN, D]), sb("attn_t", [128, KC * MAXN]), sb("out", [MAXN, D])
        last_row, own_row = sb("last_row", [MAXN, 128]), sb("own_row", [MAXN, 128])
        bank = [own.enter_context(nc.psum_tensor(f"t_bank{i}", [128, 512], F32)) for i in range(8)]

        names = ("loaded h_turned h_kept qkv_ready qkv_kept features_ready q_seen k_ready k_seen peak_turned "
                 "peak_down peak_wide biases q_exp k_exp q_done k_done outer_ready outer_kept mixed_ready "
                 "attn_ready attn_turned attn_kept out_ready out_kept wide_ready chain picks picks_made half_made "
                 "squares").split()
        S = {n: sem(n) for n in names}

        with nc.Block() as block:
            @block.sync
            def _(sp):
                for dst, src in ((h[:, :], x1_d[0:MAXN, :]), (proj[:, :, :], proj_d.rearrange("(c p) d -> p c d", p=128)),
                                 (wq[:, :, :], wq_d.rearrange("(k p) n -> p k n", p=128)),
                                 (wk[:, :, :], wk_d.rearrange("(k p) n -> p k n", p=128)),
                                 (wv[:, :, :], wv_d.rearrange("(k p) n -> p k n", p=128)),
                                 (wo[:, :, :], wo_d.rearrange("(k p) n -> p k n", p=128))):
                    sp.dma_start(dst, src).then_inc(S["loaded"], 16)

            @block.gpsimd
            def _(pool):
                g = nc.gpsimd
                g.affine_select(out=last_row[:, :], in_=c.ones[0:MAXN, :], compare_op=ALU.is_ge, fill=0.0,
                                base=-(MAXN - 1), pattern=[[0, 128]], channel_multiplier=1).then_inc(S["picks"], 1)
                pool.wait_ge(S["picks"], 1)
                g.affine_select(out=own_row[:, :], in_=last_row[:, :], compare_op=ALU.is_gt, fill=0.0,
                                base=-(MAXN - 1), pattern=[[1, 128]], channel_multiplier=0).then_inc(S["picks"], 1)

            @block.tensor
            def _(pe):
                t_ = nc.tensor
                pe.wait_ge(S["loaded"], 96)
                for k in range(KC):
                    t_.transpose(bank[0][:, k * MAXN:(k + 1) * MAXN], h[:, k * 128:(k + 1) * 128], c.ident[0:MAXN, 0:MAXN])
                for m in range(MC):
                    last = t_.transpose(bank[1][0:DH, m * 128:(m + 1) * 128], proj[:, m, :], c.ident[:, :])
                last.then_inc(S["h_turned"], 1)
                pe.wait_ge(S["h_kept"], 1)
                for b, w in ((2, wq), (3, wk)):
                    for a in range(H):
                        for k in range(KC):
                            t_.matmul(bank[b][0:DH, a * MAXN:(a + 1) * MAXN], w[:, k, a * DH:(a + 1) * DH],
                                      h_t[:, k * MAXN:(k + 1) * MAXN], start=(k == 0), stop=(k == KC - 1))
                for k in range(KC):
                    last = t_.matmul(bank[0][0:MAXN, 0:D], h_t[:, k * MAXN:(k + 1) * MAXN], wv[:, k, :],
                                     start=(k == 0), stop=(k == KC - 1))
                last.then_inc(S["qkv_ready"], 1)
                pe.wait_ge(S["qkv_kept"], 1)
                for j, sq in enumerate((q_sq, k_sq)):
                    for a in range(H):
                        t_.matmul(bank[1][0:MAXN, j * H + a:j * H + a + 1], sq[:, a * MAXN:(a + 1) * MAXN], half[:, :],
                                  start=True, stop=True)
                for a in range(H):
                    last = t_.matmul(bank[4 + a // 2][0:MAXN, (a % 2) * M:(a % 2 + 1) * M],
                                     q_t[:, a * MAXN:(a + 1) * MAXN], proj_t[:, :], start=True, stop=True)
                last.then_inc(S["features_ready"], 1)
                pe.wait_ge(S["q_seen"], 1)
                for a in range(H):
                    last = t_.matmul(bank[4 + a // 2][0:MAXN, (a % 2) * M:(a % 2 + 1) * M],
                                     k_t[:, a * MAXN:(a + 1) * MAXN], proj_t[:, :], start=True, stop=True)
                last.then_inc(S["k_ready"], 1)
                pe.wait_ge(S["k_seen"], 1)
                t_.transpose(bank[2][0:H, 0:MAXN], peak[:, H:2 * H], c.ident[0:MAXN, 0:MAXN]).then_inc(S["peak_turned"], 1)
                pe.wait_ge(S["peak_down"], 1)
                t_.matmul(bank[3][0:MAXN, 0:H], peak_t[:, :].to_broadcast([H, MAXN]), c.ident[0:H, 0:H],
                          start=True, stop=True).then_inc(S["peak_wide"], 1)
                pe.wait_ge(S["q_done"], 1)
                for a in range(H):
                    for m in range(MC):
                        i = a * MC + m
                        t_.transpose(bank[i // 8][:, (i % 8) * MAXN:(i % 8 + 1) * MAXN],
                                     qf[:, a * M + m * 128:a * M + (m + 1) * 128], c.ident[0:MAXN, 0:MAXN])
                pe.wait_ge(S["k_done"], 1)
                for a in range(H):
                    for m in range(MC):
                        i = a * MC + m
                        last = t_.matmul(bank[4 + i // 6][:, (i % 6) * W1:(i % 6 + 1) * W1],
                                         kf[:, a * M + m * 128:a * M + (m + 1) * 128], v1[:, a, :],
                                         start=True, stop=True)
                last.then_inc(S["outer_ready"], 1)
                pe.wait_ge(S["outer_kept"], 1)
                for a in range(H):
                    for m in range(MC):
                        i = a * MC + m
                        last = t_.matmul(bank[2 + a // 4][0:MAXN, (a % 4) * W1:(a % 4 + 1) * W1],
                                         qf_t[:, i * MAXN:(i + 1) * MAXN], kv[:, i, :],
                                         start=(m == 0), stop=(m == MC - 1))
                last.then_inc(S["mixed_ready"], 1)
                pe.wait_ge(S["attn_ready"], 1)
                for k in range(KC):
                    last = t_.transpose(bank[0][:, k * MAXN:(k + 1) * MAXN], attn[:, k * 128:(k + 1) * 128],
                                        c.ident[0:MAXN, 0:MAXN])
                last.then_inc(S["attn_turned"], 1)
                pe.wait_ge(S["attn_kept"], 1)
                for k in range(KC):
                    last = t_.matmul(bank[1][0:MAXN, 0:D], attn_t[:, k * MAXN:(k + 1) * MAXN], wo[:, k, :],
                                     start=(k == 0), stop=(k == KC - 1))
                last.then_inc(S["out_ready"], 1)
                pe.wait_ge(S["out_kept"], 1)
                pe.wait_ge(S["picks_made"], 1)
                t_.matmul(bank[4][:, 0:D], own_row[:, :], out[:, :], start=True, stop=True)
                t_.matmul(bank[5][:, 0:D], last_row[:, :], out[:, :], start=True, stop=True).then_inc(S["wide_ready"], 1)

            @block.scalar
            def _(act):
                a_ = nc.scalar
                a_.preload_act_table_set(TABLES)
                act.wait_ge(S["biases"], 1)
                for j, (f, done) in enumerate(((qf, S["q_exp"]), (kf, S["k_exp"]))):
                    for a in range(H):
                        last = a_.activation(f[:, a * M:(a + 1) * M], f[:, a * M:(a + 1) * M], ACT.Exp,
                                             bias=bias[:, j * H + a:j * H + a + 1])
                    last.then_inc(done, 1)

            @block.vector
            def _(dve):
                v = nc.vector
                done = [0]

                def link(ins):
                    done[0] += 1
                    ins.then_inc(S["chain"], 1)
                    dve.wait_ge(S["chain"], done[0])

                v.memset(half[:, :], 0.5)
                v.memset(v1[:, :, :], 1.0).then_inc(S["half_made"], 1)
                dve.wait_ge(S["half_made"], 1)
                dve.wait_ge(S["picks"], 2)
                v.tensor_tensor(own_row[:, :], own_row[:, :], c.ident[0:MAXN, :], ALU.add).then_inc(S["picks_made"], 1)
                dve.wait_ge(S["h_turned"], 1)
                v.tensor_copy(h_t[:, :], bank[0][:, 0:KC * MAXN])
                v.tensor_copy(proj_t[:, :], bank[1][0:DH, 0:M]).then_inc(S["h_kept"], 1)
                dve.wait_ge(S["qkv_ready"], 1)
                v.tensor_scalar(q_t[:, :], bank[2][0:DH, 0:H * MAXN], DH ** -0.25, None, ALU.mult)
                link(v.tensor_scalar(k_t[:, :], bank[3][0:DH, 0:H * MAXN], DH ** -0.25, None, ALU.mult))
                v.tensor_tensor(q_sq[:, :], q_t[:, :], q_t[:, :], ALU.mult)
                v.tensor_tensor(k_sq[:, :], k_t[:, :], k_t[:, :], ALU.mult)
                v.tensor_copy(v1[:, :, 0:DH], bank[0][0:MAXN, 0:D].rearrange("p (h d) -> p h d", h=H)) \
                    .then_inc(S["qkv_kept"], 1)
                dve.wait_ge(S["features_ready"], 1)
                v.tensor_copy(diag[:, :], bank[1][0:MAXN, 0:2 * H])
                for b in range(4):
                    ins = v.tensor_copy(qf[:, b * 512:(b + 1) * 512], bank[4 + b][0:MAXN, :])
                ins.then_inc(S["q_seen"], 1)
                dve.wait_ge(S["q_seen"], 1)
                v.tensor_reduce(peak[:, 0:H], qf[:, :].rearrange("p (h m) -> p h m", h=H), op=ALU.max, axis=AX.X)
                dve.wait_ge(S["k_ready"], 1)
                for b in range(4):
                    ins = v.tensor_copy(kf[:, b * 512:(b + 1) * 512], bank[4 + b][0:MAXN, :])
                link(ins)
                v.tensor_reduce(peak[:, H:2 * H], kf[:, :].rearrange("p (h m) -> p h m", h=H), op=ALU.max,
                                axis=AX.X).then_inc(S["k_seen"], 1)
                dve.wait_ge(S["peak_turned"], 1)
                v.reduce_max(peak_t[:, :], bank[2][0:H, 0:MAXN], AX.X).then_inc(S["peak_down"], 1)
                dve.wait_ge(S["peak_wide"], 1)
                link(v.tensor_copy(peak[:, H:2 * H], bank[3][0:MAXN, 0:H]))
                v.scalar_tensor_tensor(bias[:, :], diag[:, :], -1.0, peak[:, :], ALU.mult, ALU.subtract) \
                    .then_inc(S["biases"], 1)
                dve.wait_ge(S["q_exp"], 1)
                v.tensor_scalar(qf[:, :], qf[:, :], M ** -0.5, KEPS, ALU.mult, ALU.add).then_inc(S["q_done"], 1)
                dve.wait_ge(S["k_exp"], 1)
                v.tensor_scalar(kf[:, :], kf[:, :], M ** -0.5, KEPS, ALU.mult, ALU.add).then_inc(S["k_done"], 1)
                dve.wait_ge(S["outer_ready"], 1)
                for b in range(2):
                    v.tensor_copy(qf_t[:, b * 512:(b + 1) * 512], bank[b][:, :])
                for b in range(3):
                    n = min(6, H * MC - 6 * b)
                    ins = v.tensor_copy(kv[:, 6 * b:6 * b + n, :],
                                        bank[4 + b][:, 0:n * W1].rearrange("p (i w) -> p i w", w=W1))
                ins.then_inc(S["outer_kept"], 1)
                dve.wait_ge(S["mixed_ready"], 1)
                for b in range(2):
                    heads = bank[2 + b][0:MAXN, 0:4 * W1].rearrange("p (h w) -> p h w", w=W1)
                    link(v.tensor_scalar(z[:, 4 * b:4 * b + 4], heads[:, :, DH], KEPS, None, ALU.add))
                    link(v.reciprocal(z[:, 4 * b:4 * b + 4], z[:, 4 * b:4 * b + 4]))
                    ins = v.tensor_tensor(attn[:, b * 256:(b + 1) * 256].rearrange("p (h d) -> p h d", h=4),
                                          heads[:, :, 0:DH],
                                          z[:, 4 * b:4 * b + 4].unsqueeze(2).to_broadcast([MAXN, 4, DH]), ALU.mult)
                ins.then_inc(S["attn_ready"], 1)
                dve.wait_ge(S["attn_turned"], 1)
                v.tensor_copy(attn_t[:, :], bank[0][:, 0:KC * MAXN]).then_inc(S["attn_kept"], 1)
                dve.wait_ge(S["out_ready"], 1)
                v.tensor_copy(out[:, :], bank[1][0:MAXN, 0:D]).then_inc(S["out_kept"], 1)
                dve.wait_ge(S["wide_ready"], 1)
                v.tensor_copy(o.first_mix[:, :], bank[4][:, 0:D])
                v.tensor_copy(o.rest_mix[:, :], bank[5][:, 0:D])
    return o


def convolve(nc, ctx, c, s, n, mix, x1_d, sums_d, y, acc):
    with ExitStack() as own:
        semaphores = Semaphores(nc, own)
        def sb(name, shape, dt=F32):
            return own.enter_context(nc.sbuf_tensor(f"v_{name}", shape, dt))

        def sem(name):
            return semaphores.take(f"v_{name}")

        def two(make, name, *a):
            return [make(f"{name}{u}", *a) for u in range(2)]

        def pb(name, shape):
            return own.enter_context(nc.psum_tensor(f"v_{name}", shape, F32))

        idx = two(sb, "idx", [SLOTS, 1], U32)
        total = two(sb, "total", [SLOTS, D])
        x1 = two(sb, "x1", [ROWS, D])
        hi, lo = two(sb, "hi", [128, KC * ROWS], F32R), two(sb, "lo", [128, KC * ROWS], F32R)
        sq = pb("sq", [ROWS, D])
        turned_p, conv_p = two(pb, "turned_p", [128, 512]), two(pb, "conv_p", [ROWS, 512])

        cleared = sem("cleared")
        links = sem("links")
        total_in = two(c.pool_dma, "v_total_in")
        idx_ready, mean_ready, turned_ready, hi_ready, lo_ready, conv_ready, conv_read, x1_in, based, y_ready, \
            sq_ready, summed, summed_sq = (two(sem, m) for m in (
                "idx_ready", "mean_ready", "turned_ready", "hi_ready", "lo_ready", "conv_ready",
                "conv_read", "x1_in", "based", "y_ready", "sq_ready", "summed", "summed_sq"))
        AHEAD, BEHIND = 2, 2

        with nc.Block() as block:
            @block.gpsimd
            def _(pool):
                g = nc.gpsimd
                pool.wait_ge(cleared, 1)

                def gather(x):
                    p = x.par
                    pool.wait_ge(turned_ready[p], x.turn)
                    g.tensor_copy(idx[p][:, :], s.sum_row[:, ds(x.num, 1)]).then_inc(idx_ready[p], 1)
                    pool.wait_ge(idx_ready[p], x.turn + 1)
                    settle(pool)
                    g.indirect_dma_start(total[p][:, :], None, sums_d, bass.IndirectOffsetOnAxis(idx[p][:, :], 0),
                                         bounds_check=T * SLOTS - 1, oob_is_err=False).then_inc(total_in[p], 16)

                def base(x):
                    p = x.par
                    pool.wait_ge(x1_in[p], 32 * (x.turn + 1))
                    g.tensor_tensor(x1[p][:, :], x1[p][:, :],
                                    (mix.first_mix if x.is_zero() else mix.rest_mix)[0:ROWS, :],
                                    ALU.add).then_inc(based[p], 1)

                def body(at):
                    if x := at(2):
                        gather(x)
                    if x := at(0):
                        base(x)
                sweep(pool, body, 2, AHEAD, BEHIND)

            @block.sync
            def _(sp):
                def body(at):
                    if x := at(1):
                        p = x.par
                        sp.wait_ge(y_ready[p], x.turn)
                        for a, b in ROWS_CUT:
                            sp.dma_start(x1[p][a:b, :], x1_d[ds(ROWS * x.num + a, b - a), :]).then_inc(x1_in[p], 16)
                sweep(sp, body, 2, AHEAD, BEHIND)

            @block.tensor
            def _(pe):
                t_ = nc.tensor

                def turn(x):
                    p = x.par
                    pe.wait_ge(mean_ready[p], x.turn + 1)
                    pe.wait_ge(lo_ready[p], x.turn)
                    for k in range(KC):
                        last = t_.transpose(turned_p[p][:, k * ROWS:(k + 1) * ROWS],
                                            total[p][0:ROWS, k * 128:(k + 1) * 128], c.ident[0:ROWS, 0:ROWS])
                    last.then_inc(turned_ready[p], 1)

                def weights(x):
                    p = x.par
                    pe.wait_ge(hi_ready[p], x.turn + 1)
                    pe.wait_ge(lo_ready[p], x.turn + 1)
                    pe.wait_ge(conv_read[p], x.turn)
                    product(t_, conv_p[p][:, 0:D], hi[p], lo[p], n.w_hi, n.w_lo, ROWS).then_inc(conv_ready[p], 1)

                def body(at):
                    if x := at(1):
                        turn(x)
                    if x := at(0):
                        weights(x)
                sweep(pe, body, 2, AHEAD, BEHIND)

            @block.scalar
            def _(act):
                a = nc.scalar
                a.preload_act_table_set(TABLES)

                def body(at):
                    if x := at(1):
                        p = x.par
                        act.wait_ge(total_in[p], 16 * (x.turn + 1))
                        a.activation(total[p][:, :], total[p][:, :], ACT.Copy, scale=s.inverse[:, ds(x.num, 1)]) \
                            .then_inc(mean_ready[p], 1)
                        act.wait_ge(turned_ready[p], x.turn + 1)
                        act.wait_ge(conv_ready[p], x.turn)
                        a.copy(hi[p][:, :], turned_p[p][:, 0:KC * ROWS]).then_inc(hi_ready[p], 1)
                    if x := at(-1):
                        p = x.par
                        act.wait_ge(y_ready[p], x.turn + 1)
                        if not x.is_zero():
                            b = x.before()
                            act.wait_ge(summed_sq[b.par], b.turn + 1)
                        a.activation(sq[:, :], y[0:ROWS, ds(D * x.num, D)], ACT.Square).then_inc(sq_ready[p], 1)
                sweep(act, body, 2, AHEAD, BEHIND)

            @block.vector
            def _(dve):
                v = nc.vector
                for m in acc:
                    v.memset(m[:, :], 0.0)
                for u in range(2):
                    ins = v.memset(total[u][:, :], 0.0)
                ins.then_inc(cleared, 1)
                dve.wait_ge(cleared, 1)
                chain = Chain(dve, links, 1)

                def add(x):
                    p = x.par
                    link = chain.at(x)
                    dve.wait_ge(conv_ready[p], x.turn + 1)
                    z = y[0:ROWS, ds(D * x.num, D)]
                    v.scalar_tensor_tensor(z, n.shift_w[0:ROWS, :], s.has[:, ds(x.num, 1)],
                                           conv_p[p][:, 0:D], ALU.mult, ALU.add).then_inc(conv_read[p], 1)
                    dve.wait_ge(conv_read[p], x.turn + 1)
                    link(v.tensor_tensor(z, z, n.bias[0:ROWS, :], ALU.add))
                    dve.wait_ge(based[p], x.turn + 1)
                    v.scalar_tensor_tensor(z, z, 0.0, x1[p][:, :], ALU.max, ALU.add).then_inc(y_ready[p], 1)

                def sum_up(x):
                    p, b = x.par, x.before()
                    dve.wait_ge(y_ready[p], x.turn + 1)
                    if not x.is_zero():
                        dve.wait_ge(summed[b.par], b.turn + 1)
                        dve.wait_ge(summed_sq[b.par], b.turn + 1)
                    v.tensor_tensor(acc[0][0:ROWS, :], acc[0][0:ROWS, :], y[0:ROWS, ds(D * x.num, D)],
                                    ALU.add).then_inc(summed[p], 1)
                    dve.wait_ge(sq_ready[p], x.turn + 1)
                    v.tensor_tensor(acc[1][0:ROWS, :], acc[1][0:ROWS, :], sq[:, :], ALU.add).then_inc(summed_sq[p], 1)

                def body(at):
                    if x := at(1):
                        p = x.par
                        dve.wait_ge(hi_ready[p], x.turn + 1)
                        v.tensor_tensor(lo[p][:, :], turned_p[p][:, 0:KC * ROWS], hi[p][:, :].bitcast(F32),
                                        ALU.subtract).then_inc(lo_ready[p], 1)
                    if x := at(0):
                        add(x)
                    if x := at(-1):
                        sum_up(x)
                sweep(dve, body, 2, AHEAD, BEHIND)


def second_norm(nc, ctx, c, acc, g_d, b_d):
    o = Buffers()
    o.gain = ctx.enter_context(nc.sbuf_tensor("gain", [128, D], F32))
    o.offset = ctx.enter_context(nc.sbuf_tensor("offset", [128, D], F32))
    with ExitStack() as own:
        semaphores = Semaphores(nc, own)
        def sb(name, shape, dt=F32):
            return own.enter_context(nc.sbuf_tensor(f"m_{name}", shape, dt))

        def sem(name):
            return semaphores.take(f"m_{name}")
        g_col, b_col, a_col, s_col, var, mean, logv = (sb(m, [128, KC]) for m in (
            "g_col", "b_col", "a_col", "s_col", "var", "mean", "logv"))
        diag = [sb(f"diag{j}", [128, D]) for j in range(2)]
        sums_p, gain_p, offset_p = (own.enter_context(nc.psum_tensor(f"m_{m}", [128, 512], F32))
                                    for m in ("sums_p", "gain_p", "offset_p"))
        loaded, sums_ready, chain, var_ready, log_ready, rstd_ready, diag_ready, wide_ready = (
            sem(m) for m in ("loaded", "sums_ready", "chain", "var_ready", "log_ready", "rstd_ready", "diag_ready",
                             "wide_ready"))
        with nc.Block() as block:
            @block.sync
            def _(sp):
                sp.dma_start(g_col[:, :], g_d.rearrange("(k p) -> p k", p=128), allow_slow_non_contiguous=True).then_inc(loaded, 16)
                sp.dma_start(b_col[:, :], b_d.rearrange("(k p) -> p k", p=128), allow_slow_non_contiguous=True).then_inc(loaded, 16)

            @block.tensor
            def _(pe):
                t_ = nc.tensor
                for j in range(2):
                    for k in range(KC):
                        last = t_.matmul(sums_p[:, j * KC + k:j * KC + k + 1], acc[j][0:ROWS, k * 128:(k + 1) * 128],
                                         c.ones[0:ROWS, 0:1], start=True, stop=True)
                last.then_inc(sums_ready, 1)
                pe.wait_ge(diag_ready, 1)
                t_.matmul(gain_p[:, :], c.ones[:, :], diag[0][:, :], start=True, stop=True)
                t_.matmul(offset_p[:, :], c.ones[:, :], diag[1][:, :], start=True, stop=True).then_inc(wide_ready, 1)

            @block.scalar
            def _(act):
                a = nc.scalar
                a.preload_act_table_set(TABLES)
                act.wait_ge(var_ready, 1)
                a.activation(logv[:, :], var[:, :], ACT.Ln).then_inc(log_ready, 1)
                act.wait_ge(log_ready, 1)
                a.activation(var[:, :], logv[:, :], ACT.Exp, scale=-0.5).then_inc(rstd_ready, 1)

            @block.vector
            def _(dve):
                v = nc.vector
                done = [0]

                def link(ins):
                    done[0] += 1
                    ins.then_inc(chain, 1)
                    dve.wait_ge(chain, done[0])

                dve.wait_ge(sums_ready, 1)
                column_variance(v, link, sums_p, mean, a_col, var, var_ready)
                dve.wait_ge(rstd_ready, 1)
                dve.wait_ge(loaded, 32)
                link(v.tensor_tensor(a_col[:, :], var[:, :], g_col[:, :], ALU.mult))
                link(v.tensor_tensor(mean[:, :], mean[:, :], a_col[:, :], ALU.mult))
                link(v.tensor_tensor(s_col[:, :], b_col[:, :], mean[:, :], ALU.subtract))
                for j, col in enumerate((a_col, s_col)):
                    for k in range(KC):
                        ins = v.tensor_scalar(diag[j][:, k * 128:(k + 1) * 128], c.ident[:, :], col[:, k:k + 1], None,
                                              ALU.mult)
                ins.then_inc(diag_ready, 1)
                dve.wait_ge(wide_ready, 1)
                v.tensor_copy(o.gain[:, :], gain_p[:, :])
                v.tensor_copy(o.offset[:, :], offset_p[:, :])
    return o


def finish_nodes(nc, ctx, c, b, x1_d, y, out_d):
    P = 2
    with ExitStack() as own:
        semaphores = Semaphores(nc, own)
        def sb(name, shape, dt=F32):
            return own.enter_context(nc.sbuf_tensor(f"f_{name}", shape, dt))

        def sem(name):
            return semaphores.take(f"f_{name}")

        def ring(make, name, *a):
            return [make(f"{name}{u}", *a) for u in range(P)]

        x1, out = ring(sb, "x1", [ROWS, D]), ring(sb, "out", [ROWS, D])
        stats, moments = ring(sb, "stats", [ROWS, 6]), ring(sb, "moments", [ROWS, 2])
        logv, rstd, shift = ring(sb, "logv", [ROWS, 1]), ring(sb, "rstd", [ROWS, 1]), ring(sb, "shift", [ROWS, 1])
        x1_in, based, scaled, z_ready, stats_ready, moments_ready, log_ready, rstd_ready, shift_ready, out_ready, \
            stored = (ring(sem, m) for m in (
                "x1_in", "based", "scaled", "z_ready", "stats_ready", "moments_ready", "log_ready", "rstd_ready",
                "shift_ready", "out_ready", "stored"))
        AHEAD, BEHIND = 2, 2
        with nc.Block() as block:
            @block.sync
            def _(sp):
                def body(at):
                    if x := at(2):
                        p = x.par
                        sp.wait_ge(z_ready[p], x.turn)
                        for lo, hi in ROWS_CUT:
                            sp.dma_start(x1[p][lo:hi, :], x1_d[ds(ROWS * x.num + lo, hi - lo), :]).then_inc(x1_in[p], 16)
                    if x := at(-1):
                        p = x.par
                        sp.wait_ge(out_ready[p], x.turn + 1)
                        for lo, hi in ROWS_CUT:
                            sp.dma_start(out_d[ds(ROWS * x.num + lo, hi - lo), :], out[p][lo:hi, :]) \
                                .then_inc(stored[p], 16)
                sweep(sp, body, P, AHEAD, BEHIND)
                for u in range(P):
                    sp.wait_ge(stored[u], 32 * (T // P))

            @block.gpsimd
            def _(pool):
                def body(at):
                    if x := at(1):
                        p = x.par
                        pool.wait_ge(x1_in[p], 32 * (x.turn + 1))
                        nc.gpsimd.tensor_tensor(x1[p][:, :], x1[p][:, :], b.offset[0:ROWS, :], ALU.add) \
                            .then_inc(based[p], 1)
                sweep(pool, body, P, AHEAD, BEHIND)

            @block.scalar
            def _(act):
                a = nc.scalar
                a.preload_act_table_set(TABLES)

                def body(at):
                    if x := at(0):
                        p = x.par
                        act.wait_ge(moments_ready[p], x.turn + 1)
                        a.activation(logv[p][:, :], moments[p][:, 1:2], ACT.Ln, bias=c.ln_eps[0:ROWS, :]) \
                            .then_inc(log_ready[p], 1)
                        act.wait_ge(log_ready[p], x.turn + 1)
                        a.activation(rstd[p][:, :], logv[p][:, :], ACT.Exp, scale=-0.5).then_inc(rstd_ready[p], 1)
                    if x := at(-1):
                        p = x.par
                        act.wait_ge(shift_ready[p], x.turn + 1)
                        act.wait_ge(stored[p], 32 * x.turn)
                        a.activation(out[p][:, :], y[0:ROWS, ds(D * x.num, D)], ACT.Identity, bias=shift[p][:, :],
                                     scale=rstd[p][:, :]).then_inc(out_ready[p], 1)
                sweep(act, body, P, AHEAD, BEHIND)

            @block.vector
            def _(dve):
                v = nc.vector

                def body(at):
                    if x := at(0):
                        p = x.par
                        z = y[0:ROWS, ds(D * x.num, D)]
                        v.tensor_tensor(z, z, b.gain[0:ROWS, :], ALU.mult).then_inc(scaled[p], 1)
                        dve.wait_ge(scaled[p], x.turn + 1)
                        dve.wait_ge(based[p], x.turn + 1)
                        v.tensor_tensor(z, z, x1[p][:, :], ALU.add).then_inc(z_ready[p], 1)
                        dve.wait_ge(z_ready[p], x.turn + 1)
                        settle(dve)
                        v.bn_stats(stats[p][:, :], z).then_inc(stats_ready[p], 1)
                        dve.wait_ge(stats_ready[p], x.turn + 1)
                        dve.wait_ge(shift_ready[p], x.turn)
                        settle(dve)
                        v.bn_aggr(moments[p][:, :], stats[p][:, :]).then_inc(moments_ready[p], 1)
                    if x := at(-1):
                        p = x.par
                        dve.wait_ge(rstd_ready[p], x.turn + 1)
                        dve.wait_ge(out_ready[p], x.turn)
                        v.tensor_scalar(shift[p][:, :], moments[p][:, 0:1], -1.0, rstd[p][:, :], ALU.mult, ALU.mult) \
                            .then_inc(shift_ready[p], 1)
                sweep(dve, body, P, AHEAD, BEHIND)


def resnorm_gnn_pair(nc, x, src, dst, w0, g1, b1, g2, b2, w_conv, b_conv, wq, wk, wv, wo, proj, out):
    x1_d = nc.dram_tensor("x1_rows", (N, D), F32, kind="Internal").ap()
    sums_d = nc.dram_tensor("group_sums", (T * SLOTS, D), F32, kind="Internal").ap()
    with ExitStack() as ctx:
        c = lasting_constants(nc, ctx)
        acc = [ctx.enter_context(nc.sbuf_tensor(f"column_sums{j}", [SLOTS, D], F32)) for j in range(2)]
        by_dst = edge_tables(nc, ctx, "d", True)
        with ExitStack() as first:
            by_src = edge_tables(nc, first, "s", False)
            with ExitStack() as sorting:
                make_constants(nc, sorting, c)
                sort_edges(nc, c, (("s", by_src, src, dst), ("d", by_dst, dst, src)))
            e = edge_scores(nc, first, c, by_src, x, w0, x1_d)
            attend_edges(nc, first, c, by_src, e, x, w0, x1_d)
        gather_sums(nc, ctx, c, by_dst, x1_d, sums_d, acc)
        mix = few_node_attention(nc, ctx, c, x1_d, wq, wk, wv, wo, proj)
        n = first_norm(nc, ctx, c, acc, g1, b1, w_conv, b_conv)
        y = ctx.enter_context(nc.sbuf_tensor("y", [ROWS, T * D], F32))
        convolve(nc, ctx, c, by_dst, n, mix, x1_d, sums_d, y, acc)
        b = second_norm(nc, ctx, c, acc, g2, b2)
        finish_nodes(nc, ctx, c, b, x1_d, y, out)


_INS = ['x', 'src', 'dst', 'L0_gnn_W', 'L1_gnn_norm1_g', 'L1_gnn_norm1_b', 'L1_gnn_norm2_g', 'L1_gnn_norm2_b',
        'L1_gnn_W_conv', 'L1_gnn_b_conv', 'L1_gnn_Wq', 'L1_gnn_Wk', 'L1_gnn_Wv', 'L1_gnn_Wo', 'L1_gnn_proj']


def kernel(**inputs):
    import numpy as _np
    import concourse.bacc as _bacc
    from concourse import mybir as _mybir
    from concourse.bass_utils import run_bass_kernel_spmd as _run

    nc = _bacc.Bacc("TRN2", target_bir_lowering=False, num_devices=1)
    arrays, args = {}, []
    for name in _INS:
        a = _np.ascontiguousarray(inputs[name])
        arrays[f"in_{name}"] = a
        args.append(nc.dram_tensor(f"in_{name}", a.shape, _mybir.dt.from_np(a.dtype), kind="ExternalInput").ap())
    out = nc.dram_tensor("out", (N, D), _mybir.dt.float32, kind="ExternalOutput").ap()
    resnorm_gnn_pair(nc, *args, out)
    r = _run(nc, [arrays], core_ids=[0])
    return r.results[0]["out"]
```

```python
from contextlib import ExitStack

import concourse.bass as bass
from concourse import mybir

F32 = mybir.dt.float32
F32R = mybir.dt.float32r
BF16 = mybir.dt.bfloat16
I32 = mybir.dt.int32
U32 = mybir.dt.uint32
ALU = mybir.AluOpType
ACT = mybir.ActivationFunctionType
AX = mybir.AxisListType

N = 10000
E = 10000
D = 512
H = 8
DH = D // H
KC = D // 128
ROWS = 125
T = N // ROWS
SLOTS = ROWS + 1
NEVER = 16384
BIG = 1e30
ROUND = 12582912.0
LN_EPS = 1e-5
BN_EPS = 1e-5
KEPS = 1e-6
MAXN = 64
M = 256

ds = bass.ds


class Semaphores:

    def __init__(self, nc, own):
        self.nc, self.own, self.numbers = nc, own, []
        own.callback(self.clear)

    def take(self, name):
        s = self.own.enter_context(self.nc.semaphore(name))
        self.numbers.append(s.num)
        return s

    def clear(self):
        numbers = sorted(self.numbers)
        with self.nc.Block() as block:
            @block.gpsimd
            def _(pool):
                lo = 0
                for k in range(1, len(numbers) + 1):
                    if k == len(numbers) or numbers[k] != numbers[k - 1] + 1:
                        pool.sem_clear(range(numbers[lo], numbers[k - 1] + 1))
                        lo = k


class Buffers:
    pass


def lasting_constants(nc, ctx):
    c = Buffers()
    c.ident = ctx.enter_context(nc.sbuf_tensor("ident", [128, 128], F32))
    c.ones = ctx.enter_context(nc.sbuf_tensor("ones", [128, 128], F32))
    c.ln_eps = ctx.enter_context(nc.sbuf_tensor("ln_eps", [128, 1], F32))
    c.pool_dma = lambda name: ctx.enter_context(nc.semaphore(name))
    return c


def make_constants(nc, ctx, c):

    def sb(name, shape, dt=F32):
        return ctx.enter_context(nc.sbuf_tensor(name, shape, dt))

    c.ramp_i = sb("ramp_i", [128, 128], I32)
    c.ramp = sb("ramp", [128, 128])
    c.row_i = sb("row_i", [128, 1], I32)
    c.row = sb("row", [128, 1])
    c.node_i = sb("node_i", [ROWS, T], I32)
    c.node = sb("node", [ROWS, T])
    c.before = sb("before", [128, 128])
    c.upper = sb("upper", [128, 128])
    c.shift = sb("shift", [SLOTS, SLOTS])
    c.wrap = sb("wrap", [SLOTS, SLOTS])
    c.keep = sb("keep", [SLOTS, SLOTS])
    c.lift = sb("lift", [SLOTS, SLOTS])
    c.zeros = sb("zeros", [128, 512])
    semaphores = Semaphores(nc, ctx)
    made = semaphores.take("constants_made")
    cleared = semaphores.take("constants_cleared")
    ramps = semaphores.take("ramps_made")

    with nc.Block() as block:
        @block.gpsimd
        def _(pool):
            g = nc.gpsimd
            g.iota(c.ramp_i[:, :], [[1, 128]], base=0, channel_multiplier=0).then_inc(ramps, 1)
            g.iota(c.row_i[:, :], [[0, 1]], base=0, channel_multiplier=1).then_inc(ramps, 1)
            g.iota(c.node_i[:, :], [[ROWS, T]], base=0, channel_multiplier=1).then_inc(ramps, 1)
            pool.wait_ge(cleared, 7)
            for mat, size, base in ((c.ident, 128, 0), (c.shift, SLOTS, -1)):
                g.affine_select(out=mat[0:size, 0:size], in_=mat[0:size, 0:size], compare_op=ALU.not_equal,
                                fill=1.0, base=-base, pattern=[[-1, size]], channel_multiplier=1).then_inc(made, 1)
            g.affine_select(out=c.keep[:, :], in_=c.keep[:, :], compare_op=ALU.not_equal, fill=1.0,
                            base=0, pattern=[[-1, SLOTS]], channel_multiplier=1).then_inc(made, 1)
            g.affine_select(out=c.before[:, :], in_=c.ones[:, :], compare_op=ALU.is_gt, fill=0.0,
                            base=0, pattern=[[-1, 128]], channel_multiplier=1).then_inc(made, 1)
            g.affine_select(out=c.upper[:, :], in_=c.ones[:, :], compare_op=ALU.is_gt, fill=0.0,
                            base=0, pattern=[[1, 128]], channel_multiplier=-1).then_inc(made, 1)
            g.affine_select(out=c.wrap[:, :], in_=c.wrap[:, :], compare_op=ALU.not_equal, fill=1.0,
                            base=-(ROWS * 128 + 1), pattern=[[1, SLOTS]], channel_multiplier=128).then_inc(made, 1)
            g.affine_select(out=c.lift[:, :], in_=c.lift[:, :], compare_op=ALU.not_equal, fill=1.0,
                            base=-128, pattern=[[1, SLOTS]], channel_multiplier=128).then_inc(made, 1)

        @block.vector
        def _(dve):
            v = nc.vector
            for mat in (c.ident, c.shift, c.keep, c.wrap, c.lift, c.zeros):
                v.memset(mat[:, :], 0.0).then_inc(cleared, 1)
            v.memset(c.ones[:, :], 1.0).then_inc(cleared, 1)
            v.memset(c.ln_eps[:, :], LN_EPS)
            dve.wait_ge(ramps, 3)
            v.tensor_copy(c.ramp[:, :], c.ramp_i[:, :])
            v.tensor_copy(c.row[:, :], c.row_i[:, :])
            v.tensor_copy(c.node[:, :], c.node_i[:, :])
            dve.wait_ge(made, 7)
            v.memset(c.keep[0:1, 0:1], 0.0)
            v.memset(c.shift[0:1, 0:2], 0.0)


def pairs(eng, body):
    assert (T // 2 - 1) % 3 == 0
    body(0)
    with eng.Fori(0, (T // 2 - 1) // 3) as i:
        for k in range(3):
            body(3 * i + (1 + k))


def divide(v, dve, link, out, x, rows):
    link(v.tensor_scalar(out[0:rows, :], x[0:rows, :], -62.0, 1.0 / ROWS, ALU.add, ALU.mult))
    link(v.tensor_scalar(out[0:rows, :], out[0:rows, :], ROUND, None, ALU.add))
    link(v.tensor_scalar(out[0:rows, :], out[0:rows, :], -ROUND, None, ALU.add))


def edge_tables(nc, ctx, tag, brief):
    o = Buffers()

    def keep(name, shape, dt=F32):
        return ctx.enter_context(nc.sbuf_tensor(f"{tag}_{name}", shape, dt))

    def only_full(*a):
        return None if brief else keep(*a)

    o.key_row = only_full("key_row", [SLOTS, T], U32)
    o.val_row = keep("val_row", [SLOTS, T], U32)
    o.first_row = only_full("first_row", [SLOTS, T], U32)
    o.first = only_full("first", [SLOTS, T])
    o.key_in = keep("key_in", [SLOTS, T])
    o.key_out = keep("key_out", [SLOTS, T])
    o.cut = only_full("cut", [SLOTS, T])
    o.empty = only_full("empty", [ROWS, T])
    o.empty_row = only_full("empty_row", [SLOTS, T], U32)
    o.has = keep("has", [ROWS, T])
    o.inverse = keep("inverse", [SLOTS, T])
    o.sum_row = keep("sum_row", [SLOTS, T], U32)
    return o


def sort_buffers(nc, own, semaphores, tag, o, key_d, val_d):
    j = Buffers()
    j.o, j.key_d, j.val_d = o, key_d, val_d

    def sb(name, shape, dt=F32):
        return own.enter_context(nc.sbuf_tensor(f"{tag}_{name}", shape, dt))

    def pb(name, rows):
        return [own.enter_context(nc.psum_tensor(f"{tag}_{name}{u}", [rows, 512], F32)) for u in range(2)]

    def sem(name):
        return semaphores.take(f"{tag}_{name}")

    def two(make, name, *a):
        return [make(f"{name}{u}", *a) for u in range(2)]

    j.key_i = sb("key_i", [ROWS, T], I32)
    j.val_i = sb("val_i", [ROWS, T], I32)
    j.digits = sb("digits", [ROWS, T, 2])
    j.key, j.key_tile, j.key_slot, j.key1, j.val1, j.rank, j.start, j.pos, j.pos_tile, j.pos_slot, j.node_cnt, \
        j.empty = (sb(m, [ROWS, T]) for m in (
            "key", "key_tile", "key_slot", "key1", "val1", "rank", "start", "pos", "pos_tile", "pos_slot",
            "node_cnt", "no_edge"))
    j.slot_hot, j.tile_hot = two(sb, "slot_hot", [ROWS, ROWS], BF16), two(sb, "tile_hot", [ROWS, T], BF16)
    j.counts = sb("counts", [ROWS, T, T])
    j.summed = sb("summed", [ROWS, T, T])
    j.base = sb("base", [ROWS, 1])
    j.column = two(sb, "column", [ROWS, 2])
    j.slot_hot_t = two(sb, "slot_hot_t", [ROWS, ROWS])
    j.junk, j.junk2 = two(sb, "junk", [ROWS, ROWS]), two(sb, "junk2", [ROWS, T])
    j.out_hot = two(sb, "out_hot", [ROWS, SLOTS])
    j.place_hot = two(sb, "place_hot", [ROWS, T])
    j.payload = two(sb, "payload", [ROWS, 2, T])
    j.ks = sb("ks", [SLOTS, T + 2])
    j.vs, j.same, j.tmp = sb("vs", [SLOTS, T]), sb("same", [SLOTS, T]), sb("tmp", [SLOTS, T])
    j.tmp_i = sb("tmp_i", [SLOTS, T], I32)

    j.rows_p = pb("rows_p", SLOTS)
    j.look = pb("look", SLOTS)
    j.hist, j.sorted_p, j.edge_p = j.look, j.look[0], j.rows_p[0]

    j.loaded, j.chain, j.digits_ready, j.base_asked, j.base_ready, j.starts_ready, j.pos_ready, j.sorted_ready, \
        j.sorted_kept, j.edges_ready = (sem(m) for m in (
            "loaded", "chain", "digits_ready", "base_asked", "base_ready", "starts_ready", "pos_ready",
            "sorted_ready", "sorted_kept", "edges_ready"))
    j.hot_ready, j.hist_ready, j.hist_kept, j.column_ready, j.rows_ready, j.hot_t_ready, j.ranked, \
        j.look_ready, j.looked, j.placed, j.payload_ready, j.payload_used = (two(sem, m) for m in (
            "hot_ready", "hist_ready", "hist_kept", "column_ready", "rows_ready", "hot_t_ready",
            "ranked", "look_ready", "looked", "placed", "payload_ready", "payload_used"))
    return j


def sort_edges(nc, c, jobs):
    with ExitStack() as own:
        semaphores = Semaphores(nc, own)
        jobs = [sort_buffers(nc, own, semaphores, *job) for job in jobs]
        lanes = [(j, u) for j in jobs for u in range(2)]

        with nc.Block() as block:
            @block.sync
            def _(sp):
                for j in jobs:
                    sp.dma_start(j.key_i[:, :], j.key_d.rearrange("(p t) -> p t", t=T)).then_inc(j.loaded, 16)
                    sp.dma_start(j.val_i[:, :], j.val_d.rearrange("(p t) -> p t", t=T)).then_inc(j.loaded, 16)

            @block.vector
            def _(dve):
                v = nc.vector

                def linked(j):
                    def link(ins):
                        j.links = j.links + 1
                        ins.then_inc(j.chain, 1)
                        dve.wait_ge(j.chain, j.links)
                    return link

                for j in jobs:
                    j.links, j.link = 0, linked(j)

                for j in jobs:
                    link = j.link
                    dve.wait_ge(j.loaded, 32)
                    v.tensor_copy(j.key[:, :], j.key_i[:, :])
                    link(v.tensor_copy(j.val1[:, :], j.val_i[:, :]))
                    v.tensor_scalar(j.key1[:, :], j.key[:, :], 1.0, None, ALU.add)
                    link(v.tensor_scalar(j.val1[:, :], j.val1[:, :], 1.0, None, ALU.add))
                    divide(v, dve, link, j.key_tile, j.key, ROWS)
                    link(v.scalar_tensor_tensor(j.key_slot[:, :], j.key_tile[:, :], -float(ROWS), j.key[:, :],
                                                ALU.mult, ALU.add))
                    v.tensor_copy(j.digits[:, :, 0], j.key[:, :])
                    v.tensor_copy(j.digits[:, :, 1], j.key_slot[:, :]).then_inc(j.digits_ready, 1)

                for j in jobs:
                    dve.wait_ge(j.digits_ready, 1)

                def one_hot(i):
                    for j, u in lanes:
                        dve.wait_ge(j.hist_ready[u], i)
                        v.tensor_scalar(j.slot_hot[u][:, :], c.ramp[0:ROWS, 0:ROWS],
                                        j.key_slot[:, ds(2 * i + u, 1)], None, ALU.is_equal)
                        v.tensor_scalar(j.tile_hot[u][:, :], c.ramp[0:ROWS, 0:T],
                                        j.key_tile[:, ds(2 * i + u, 1)], None,
                                        ALU.is_equal).then_inc(j.hot_ready[u], 1)
                pairs(dve, one_hot)

                for j in jobs:
                    for u in range(2):
                        dve.wait_ge(j.hist_kept[u], T // 2)
                    counts, summed = (m[:, :, :].rearrange("p a t -> p (a t)") for m in (j.counts, j.summed))
                    j.link(v.tensor_tensor_scan(summed, counts, counts, 0.0, ALU.add, ALU.bypass))
                    v.memset(j.ks[:, :], 0.0).then_inc(j.base_asked, 1)
                for j in jobs:
                    link = j.link
                    counts, summed = (m[:, :, :].rearrange("p a t -> p (a t)") for m in (j.counts, j.summed))
                    dve.wait_ge(j.base_ready, 1)
                    link(v.tensor_copy(j.base[:, :], j.edge_p[0:ROWS, 0:1]))
                    link(v.tensor_scalar(j.node_cnt[:, :], j.summed[:, :, T - 1], j.base[:, :], None, ALU.add))
                    v.scalar_tensor_tensor(counts, summed, j.base[:, :], counts,
                                           ALU.add, ALU.subtract).then_inc(j.starts_ready, 1)

                def place_edges(i):
                    for j, u in lanes:
                        dve.wait_ge(j.rows_ready[u], i + 1)
                        dve.wait_ge(j.look_ready[u], i)
                        v.tensor_scalar(j.slot_hot_t[u][:, :], j.rows_p[u][0:ROWS, ROWS:2 * ROWS], c.row[0:ROWS, :],
                                        None, ALU.is_equal).then_inc(j.hot_t_ready[u], 1)
                        dve.wait_ge(j.ranked[u], i)
                        v.scalar_tensor_tensor(j.junk[u][:, :], j.rows_p[u][0:ROWS, 0:ROWS],
                                               j.digits[:, ds(2 * i + u, 1), 0:1].rearrange("p a b -> p (a b)"),
                                               c.before[0:ROWS, 0:ROWS], ALU.is_equal, ALU.mult,
                                               accum_out=j.rank[:, ds(2 * i + u, 1)]).then_inc(j.ranked[u], 1)
                    for j, u in lanes:
                        dve.wait_ge(j.looked[u], i)
                        dve.wait_ge(j.look_ready[u], i + 1)
                        v.scalar_tensor_tensor(j.junk2[u][:, :], c.ramp[0:ROWS, 0:T],
                                               j.key_tile[:, ds(2 * i + u, 1)], j.look[u][0:ROWS, 0:T],
                                               ALU.is_equal, ALU.mult,
                                               accum_out=j.start[:, ds(2 * i + u, 1)]).then_inc(j.looked[u], 1)
                pairs(dve, place_edges)
                for j in jobs:
                    link = j.link
                    for u in range(2):
                        dve.wait_ge(j.looked[u], T // 2)
                        dve.wait_ge(j.ranked[u], T // 2)
                    link(v.tensor_tensor(j.pos[:, :], j.start[:, :], j.rank[:, :], ALU.add))
                    divide(v, dve, link, j.pos_tile, j.pos, ROWS)
                    link(v.scalar_tensor_tensor(j.pos_slot[:, :], j.pos_tile[:, :], -float(ROWS), j.pos[:, :],
                                                ALU.mult, ALU.add))
                    v.tensor_scalar(j.pos_slot[:, :], j.pos_slot[:, :], 1.0, None, ALU.add).then_inc(j.pos_ready, 1)
                for j in jobs:
                    dve.wait_ge(j.pos_ready, 1)

                def permute(i):
                    for j, u in lanes:
                        dve.wait_ge(j.payload_used[u], i)
                        v.tensor_scalar(j.out_hot[u][:, :], c.ramp[0:ROWS, 0:SLOTS], j.pos_slot[:, ds(2 * i + u, 1)],
                                        None, ALU.is_equal)
                        dve.wait_ge(j.payload_ready[u], i)
                        v.tensor_scalar(j.place_hot[u][:, :], c.ramp[0:ROWS, 0:T], j.pos_tile[:, ds(2 * i + u, 1)],
                                        None, ALU.is_equal).then_inc(j.placed[u], 1)
                pairs(dve, permute)

                for j in jobs:
                    link, o = j.link, j.o
                    dve.wait_ge(j.starts_ready, 1)
                    link(v.tensor_tensor(j.node_cnt[:, :], j.node_cnt[:, :], j.counts[:, :, 0], ALU.subtract))
                    link(v.tensor_scalar(o.has[:, :], j.node_cnt[:, :], 1.0, None, ALU.min))
                    link(v.tensor_scalar(j.empty[:, :], o.has[:, :], -1.0, 1.0, ALU.mult, ALU.add))
                    link(v.tensor_scalar(j.tmp[0:ROWS, :], j.node_cnt[:, :], 1.0, None, ALU.max))
                    link(v.memset(o.inverse[:, :], 0.0))
                    link(v.reciprocal(j.tmp[0:ROWS, :], j.tmp[0:ROWS, :]))
                    link(v.tensor_tensor(o.inverse[0:ROWS, :], j.tmp[0:ROWS, :], o.has[:, :], ALU.mult))
                    link(v.memset(j.tmp_i[:, :], NEVER))
                    if o.empty_row is not None:
                        v.tensor_copy(o.empty[:, :], j.empty[:, :])
                        link(v.scalar_tensor_tensor(j.tmp_i[0:ROWS, :], o.has[:, :], float(NEVER), c.node[:, :],
                                                    ALU.mult, ALU.add))
                        link(v.tensor_copy(o.empty_row[:, :], j.tmp_i[:, :]))
                    link(v.tensor_copy(j.start[:, :], j.counts[:, :, 0]))
                    divide(v, dve, link, j.rank, j.start, ROWS)
                    link(v.scalar_tensor_tensor(j.start[:, :], j.start[:, :], 1.0, j.rank[:, :], ALU.add, ALU.add))
                    link(v.scalar_tensor_tensor(j.start[:, :], j.empty[:, :], float(NEVER), j.start[:, :],
                                                ALU.mult, ALU.add))
                    link(v.tensor_copy(j.tmp_i[0:ROWS, :], j.start[:, :]))
                    link(v.tensor_copy(o.sum_row[:, :], j.tmp_i[:, :]))

                for j in jobs:
                    dve.wait_ge(j.sorted_ready, 1)
                    v.memset(j.ks[:, 0:1], -1.0)
                    v.memset(j.ks[:, T + 1:T + 2], -2.0)
                    v.tensor_copy(j.ks[:, 1:T + 1], j.sorted_p[:, 0:T]).then_inc(j.sorted_kept, 1)
                for j in jobs:
                    link, o = j.link, j.o
                    link(v.tensor_copy(j.vs[:, :], j.sorted_p[:, T:2 * T]))
                    link(v.tensor_scalar(j.tmp[:, :], j.vs[:, :], -1.0, 0.0, ALU.add, ALU.max))
                    link(v.tensor_copy(j.tmp_i[:, :], j.tmp[:, :]))
                    link(v.tensor_copy(o.val_row[:, :], j.tmp_i[:, :]))
                    dve.wait_ge(j.sorted_kept, 1)
                    link(v.tensor_scalar(j.tmp[:, :], j.ks[:, 1:T + 1], -1.0, 0.0, ALU.add, ALU.max))
                    link(v.tensor_copy(j.tmp_i[:, :], j.tmp[:, :]))
                    if o.key_row is not None:
                        link(v.tensor_copy(o.key_row[:, :], j.tmp_i[:, :]))
                    dve.wait_ge(j.edges_ready, 1)
                    v.tensor_copy(o.key_in[:, :], j.edge_p[:, T:2 * T])
                    v.tensor_copy(o.key_out[:, :], j.edge_p[:, 2 * T:3 * T])
                    if o.first is not None:
                        link(v.tensor_tensor(j.same[:, :], j.ks[:, 1:T + 1], j.edge_p[:, 0:T], ALU.is_equal))
                        v.tensor_scalar(o.first[:, :], j.same[:, :], -1.0, 1.0, ALU.mult, ALU.add)
                        v.tensor_scalar(o.cut[:, :], j.same[:, :], -1.0, BIG, ALU.add, ALU.mult)
                        link(v.scalar_tensor_tensor(j.tmp_i[:, :], j.same[:, :], float(NEVER), j.tmp[:, :],
                                                    ALU.mult, ALU.add))
                        v.tensor_copy(o.first_row[:, :], j.tmp_i[:, :])

            @block.scalar
            def _(act):
                for j in jobs:
                    act.wait_ge(j.digits_ready, 1)

                def keep_counts(i):
                    for j, u in lanes:
                        act.wait_ge(j.hist_ready[u], i + 1)
                        nc.scalar.activation(j.counts[:, :, ds(2 * i + u, 1)].rearrange("p a b -> p (a b)"),
                                             j.hist[u][0:ROWS, 0:T], ACT.Copy).then_inc(j.hist_kept[u], 1)
                pairs(act, keep_counts)

                def take_column(i):
                    for j, u in lanes:
                        act.wait_ge(j.rows_ready[u], i)
                        nc.scalar.activation(j.column[u][:, :], j.digits[:, ds(2 * i + u, 1), :]
                                             .rearrange("p a b -> p (a b)"), ACT.Copy).then_inc(j.column_ready[u], 1)
                pairs(act, take_column)

                def fill_places(i):
                    for j, u in lanes:
                        act.wait_ge(j.payload_used[u], i)
                        act.wait_ge(j.placed[u], i + 1)
                        for at, val in ((0, j.key1), (1, j.val1)):
                            last = nc.scalar.activation(j.payload[u][:, at, :], j.place_hot[u][:, :], ACT.Copy,
                                                        scale=val[:, ds(2 * i + u, 1)])
                        last.then_inc(j.payload_ready[u], 1)
                pairs(act, fill_places)

            @block.tensor
            def _(pe):
                t_ = nc.tensor

                def count(i):
                    for j, u in lanes:
                        pe.wait_ge(j.hist_kept[u], i)
                        pe.wait_ge(j.hot_ready[u], i + 1)
                        t_.matmul(j.hist[u][0:ROWS, 0:T], j.slot_hot[u][:, :], j.tile_hot[u][:, :],
                                  start=True, stop=True).then_inc(j.hist_ready[u], 1)
                pairs(pe, count)
                for j in jobs:
                    pe.wait_ge(j.base_asked, 1)
                    t_.matmul(j.edge_p[0:ROWS, 0:1], c.upper[0:ROWS, 0:ROWS],
                              j.summed[:, T - 1, T - 1:T], start=True, stop=True).then_inc(j.base_ready, 1)
                for j in jobs:
                    pe.wait_ge(j.starts_ready, 1)

                def look_up(i):
                    for j, u in lanes:
                        pe.wait_ge(j.column_ready[u], i + 1)
                        pe.wait_ge(j.ranked[u], i)
                        pe.wait_ge(j.hot_t_ready[u], i)
                        t_.matmul(j.rows_p[u][0:ROWS, 0:ROWS], j.column[u][:, 0:1].to_broadcast([ROWS, ROWS]),
                                  c.ident[0:ROWS, 0:ROWS], start=True, stop=True)
                        t_.matmul(j.rows_p[u][0:ROWS, ROWS:2 * ROWS], j.column[u][:, 1:2].to_broadcast([ROWS, ROWS]),
                                  c.ident[0:ROWS, 0:ROWS], start=True, stop=True).then_inc(j.rows_ready[u], 1)
                    for j, u in lanes:
                        pe.wait_ge(j.looked[u], i)
                        pe.wait_ge(j.hot_t_ready[u], i + 1)
                        t_.matmul(j.look[u][0:ROWS, 0:T], j.slot_hot_t[u][:, :],
                                  j.counts[:, :, ds(2 * i + u, 1)].rearrange("p a b -> p (a b)"),
                                  start=True, stop=True).then_inc(j.look_ready[u], 1)
                pairs(pe, look_up)
                for j in jobs:
                    for u in range(2):
                        pe.wait_ge(j.looked[u], T // 2)
                    t_.matmul(j.sorted_p[:, 0:2 * T], c.zeros[:, 0:SLOTS], c.zeros[:, 0:2 * T], start=True, stop=False)

                def gather_permuted(i):
                    for j, u in lanes:
                        pe.wait_ge(j.payload_ready[u], i + 1)
                        t_.matmul(j.sorted_p[:, 0:2 * T], j.out_hot[u][:, :],
                                  j.payload[u][:, :, :].rearrange("p a b -> p (a b)"),
                                  start=False, stop=False).then_inc(j.payload_used[u], 1)
                pairs(pe, gather_permuted)
                for j in jobs:
                    t_.matmul(j.sorted_p[:, 0:2 * T], c.zeros[:, 0:SLOTS], c.zeros[:, 0:2 * T],
                              start=False, stop=True).then_inc(j.sorted_ready, 1)
                for j in jobs:
                    ks = j.ks
                    pe.wait_ge(j.sorted_kept, 1)
                    for at, mats in ((0, ((c.shift, 1), (c.wrap, 0))), (T, ((c.keep, 1), (c.lift, 2))),
                                     (2 * T, ((c.keep, 1), (c.lift, 1)))):
                        for k, (mat, first) in enumerate(mats):
                            last = t_.matmul(j.edge_p[:, at:at + T], mat[:, :], ks[:, first:first + T],
                                             start=(k == 0), stop=(k == 1))
                    last.then_inc(j.edges_ready, 1)


def settle(eng):
    eng.nop(nofuse=True)


class Tile:

    def __init__(self, period, i, c, ring=None):
        self.period, self.i, self.c, self.ring = period, i, c, ring or period
        self.par = c % self.ring
        self.turn = i * (period // self.ring) + c // self.ring
        self.buf = c % period
        self.lap = i + c // period
        self.num = period * i + c

    def before(self, n=1):
        return Tile(self.period, self.i, self.c - n, self.ring)

    def after(self):
        return Tile(self.period, self.i, self.c + 1, self.ring)

    def again(self):
        return not isinstance(self.i, int) or self.num >= self.period

    def is_last(self):
        return isinstance(self.i, int) and self.num == T - 1

    def is_zero(self):
        return isinstance(self.i, int) and self.num == 0


def sweep(eng, body, period, ahead, behind, ring=None):
    lo = 1 - (-behind // period)
    hi = (T - ahead) // period

    def fixed(s):
        def at(k):
            return Tile(period, 0, s + k, ring) if 0 <= s + k < T else None
        body(at)

    for s in range(-ahead, lo * period):
        fixed(s)
    with eng.Fori(lo, hi) as i:
        for c in range(period):
            body(lambda k, c=c: Tile(period, i, c + k, ring))
    for s in range(hi * period, T + behind):
        fixed(s)


ROWS_CUT = ((0, 112), (112, ROWS))
TABLES = "natural_log_exp_and_others"


class SplitWeights:

    def __init__(self, nc, ctx, semaphores, name, w_d, lo_col, hi_col):
        n = hi_col - lo_col
        self.nc, self.from_d = nc, w_d.rearrange("(k p) n -> p k n", p=128)[:, :, lo_col:hi_col]
        self.hi = ctx.enter_context(nc.sbuf_tensor(f"{name}_hi", [128, KC, n], F32R))
        self.lo = ctx.enter_context(nc.sbuf_tensor(f"{name}_lo", [128, KC, n], F32R))
        self.raw = ctx.enter_context(nc.sbuf_tensor(f"{name}_raw", [128, KC, n], F32))
        self.loaded, self.high, self.split = (semaphores.take(f"{name}_{m}") for m in ("loaded", "high", "split"))

    def load(self, sp):
        sp.dma_start(self.raw[:, :, :], self.from_d).then_inc(self.loaded, 16)

    def act(self, act):
        act.wait_ge(self.loaded, 16)
        self.nc.scalar.copy(self.hi[:, :, :], self.raw[:, :, :]).then_inc(self.high, 1)

    def dve(self, dve):
        dve.wait_ge(self.high, 1)
        self.nc.vector.tensor_tensor(self.lo[:, :, :], self.raw[:, :, :], self.hi[:, :, :].bitcast(F32),
                                     ALU.subtract).then_inc(self.split, 1)

    def pe(self, pe):
        pe.wait_ge(self.split, 1)


def product(t, out, x_hi, x_lo, w_hi, w_lo, rows, chunks=range(KC)):
    for k in chunks:
        xh = x_hi[:, k * rows:(k + 1) * rows]
        t.matmul(out, xh, w_hi[:, k, :], start=(k == 0), stop=False)
        t.matmul(out, xh, w_lo[:, k, :], start=False, stop=False)
        last = t.matmul(out, x_lo[:, k * rows:(k + 1) * rows], w_hi[:, k, :], start=False, stop=(k == KC - 1))
    return last


def edge_scores(nc, ctx, c, s, x_d, w_d, x1_d, own_d, other_d, acc):
    o = Buffers()
    o.aw = ctx.enter_context(nc.sbuf_tensor("aw_all", [H, E], F32))
    o.cut = ctx.enter_context(nc.sbuf_tensor("cut_all", [H, E + 1], BF16))
    o.run_max = ctx.enter_context(nc.sbuf_tensor("run_max", [H, E + 1], F32))
    with ExitStack() as own:
        semaphores = Semaphores(nc, own)
        def sb(name, shape, dt=F32):
            return own.enter_context(nc.sbuf_tensor(f"a_{name}", shape, dt))

        def pb(name, shape):
            return own.enter_context(nc.psum_tensor(f"a_{name}", shape, F32))

        def sem(name):
            return semaphores.take(f"a_{name}")

        def two(make, name, *a):
            return [make(f"{name}{u}", *a) for u in range(2)]

        wq = SplitWeights(nc, own, semaphores, "wq", w_d, 0, D)
        wk = SplitWeights(nc, own, semaphores, "wk", w_d, D, 2 * D)

        P = 4

        def four(make, name, *a):
            return [make(f"{name}{u}", *a) for u in range(P)]

        src_idx, dst_idx = four(sb, "src_idx", [SLOTS, 1], U32), four(sb, "dst_idx", [SLOTS, 1], U32)
        empty_idx = two(sb, "empty_idx", [SLOTS, 1], U32)
        xs, xd = four(sb, "xs", [SLOTS, D]), four(sb, "xd", [SLOTS, D])
        xs_hi, xs_lo = two(sb, "xs_hi", [128, KC * SLOTS], F32R), two(sb, "xs_lo", [128, KC * SLOTS], F32R)
        xd_hi, xd_lo = two(sb, "xd_hi", [128, KC * SLOTS], F32R), two(sb, "xd_lo", [128, KC * SLOTS], F32R)
        q = two(sb, "q", [SLOTS, D])
        qk = two(sb, "qk", [SLOTS, D])
        aw_col, cut_col = two(sb, "aw_col", [SLOTS, H]), two(sb, "cut_col", [SLOTS, H])
        xn = two(sb, "xn", [ROWS, D])
        x1n = two(sb, "x1n", [SLOTS, D])
        sq = sb("sq", [ROWS, D])
        stats, moments = two(sb, "stats", [ROWS, 6]), two(sb, "moments", [ROWS, 2])
        logv, rstd, shift = two(sb, "logv", [ROWS, 1]), two(sb, "rstd", [ROWS, 1]), two(sb, "shift", [ROWS, 1])

        turned_s, turned_d = pb("turned_s", [128, 512]), pb("turned_d", [128, 512])
        q_p, k_p = two(pb, "q_p", [SLOTS, 512]), two(pb, "k_p", [SLOTS, 512])
        score_p = two(pb, "score_p", [H, 512])

        cleared = sem("cleared")
        idx_ready = four(sem, "idx_ready")
        xs_in, xd_in = four(c.pool_dma, "a_xs_in"), four(c.pool_dma, "a_xd_in")
        turned_s_ready, turned_d_ready = two(sem, "turned_s_ready"), two(sem, "turned_d_ready")
        hi_s_ready, hi_d_ready = two(sem, "hi_s_ready"), two(sem, "hi_d_ready")
        lo_s_ready, lo_d_ready = two(sem, "lo_s_ready"), two(sem, "lo_d_ready")
        q_ready, k_ready, q_kept = two(sem, "q_ready"), two(sem, "k_ready"), two(sem, "q_kept")
        prod_ready, aw_ready = two(sem, "prod_ready"), two(sem, "aw_ready")
        score_ready, scanned = two(sem, "score_ready"), two(sem, "scanned")
        xn_in, stats_ready, moments_ready = two(sem, "xn_in"), two(sem, "stats_ready"), two(sem, "moments_ready")
        log_ready, rstd_ready, shift_ready = two(sem, "log_ready"), two(sem, "rstd_ready"), two(sem, "shift_ready")
        x1n_ready, sq_ready, masked = two(sem, "x1n_ready"), two(sem, "sq_ready"), two(sem, "masked")
        summed, summed_sq = two(sem, "summed"), two(sem, "summed_sq")
        cut_kept = sem("cut_kept")
        xs_out, halves_out = four(sem, "xs_out"), two(sem, "halves_out")
        empty_idx_ready, x1n_out = two(sem, "empty_idx_ready"), two(c.pool_dma, "a_x1n_out")

        AHEAD, BEHIND = 3, 2
        with nc.Block() as block:
            @block.sync
            def _(sp):
                wq.load(sp)
                wk.load(sp)

                def load_nodes(x):
                    sp.wait_ge(x1n_ready[x.par], x.turn)
                    sp.wait_ge(stats_ready[x.par], x.turn)
                    for a, b in ROWS_CUT:
                        sp.dma_start(xn[x.par][a:b, :], x_d[ds(ROWS * x.num + a, b - a), :]) \
                            .then_inc(xn_in[x.par], 16)

                def store_own(x):
                    sp.wait_ge(xs_in[x.buf], 16 * (x.lap + 1))
                    sp.dma_start(own_d[ds(SLOTS * x.num, SLOTS), :], xs[x.buf][:, :]).then_inc(xs_out[x.buf], 16)

                def store_other(x):
                    p = x.par
                    sp.wait_ge(hi_d_ready[p], x.turn + 1)
                    sp.dma_start(other_d[0, ds(128 * x.num, 128), :], xd_hi[p][:, :].bitcast(F32)).then_inc(halves_out[p], 16)
                    sp.wait_ge(lo_d_ready[p], x.turn + 1)
                    sp.dma_start(other_d[1, ds(128 * x.num, 128), :], xd_lo[p][:, :].bitcast(F32)).then_inc(halves_out[p], 16)

                def body(at):
                    if x := at(2):
                        store_own(x)
                    if x := at(1):
                        load_nodes(x)
                        store_other(x)
                sweep(sp, body, P, AHEAD, BEHIND, 2)
                for u in range(P):
                    sp.wait_ge(xs_out[u], 16 * (T // P))
                for u in range(2):
                    sp.wait_ge(halves_out[u], 32 * (T // 2))

            @block.gpsimd
            def _(pool):
                g = nc.gpsimd

                def gather(x):
                    p, u = x.par, x.buf
                    if x.again():
                        pool.wait_ge(turned_s_ready[p], x.turn - 1)
                        pool.wait_ge(turned_d_ready[p], x.turn - 1)
                        pool.wait_ge(xs_out[u], 16 * x.lap)
                    g.tensor_copy(src_idx[u][:, :], s.key_row[:, ds(x.num, 1)])
                    g.tensor_copy(dst_idx[u][:, :], s.val_row[:, ds(x.num, 1)]).then_inc(idx_ready[u], 1)
                    pool.wait_ge(idx_ready[u], x.lap + 1)
                    settle(pool)
                    g.indirect_dma_start(xs[u][:, :], None, x_d, bass.IndirectOffsetOnAxis(src_idx[u][:, :], 0)) \
                        .then_inc(xs_in[u], 16)
                    settle(pool)
                    g.indirect_dma_start(xd[u][:, :], None, x_d, bass.IndirectOffsetOnAxis(dst_idx[u][:, :], 0)) \
                        .then_inc(xd_in[u], 16)

                def scatter_empty(x):
                    p = x.par
                    pool.wait_ge(x1n_out[p], 16 * x.turn)
                    g.tensor_copy(empty_idx[p][:, :], s.empty_row[:, ds(x.num, 1)]).then_inc(empty_idx_ready[p], 1)
                    pool.wait_ge(empty_idx_ready[p], x.turn + 1)
                    pool.wait_ge(x1n_ready[p], x.turn + 1)
                    settle(pool)
                    g.indirect_dma_start(x1_d, bass.IndirectOffsetOnAxis(empty_idx[p][:, :], 0), x1n[p][:, :], None,
                                         bounds_check=N - 1, oob_is_err=False).then_inc(x1n_out[p], 16)

                pool.wait_ge(cleared, 1)
                def body(at):
                    if x := at(3):
                        gather(x)
                    if x := at(-1):
                        scatter_empty(x)
                sweep(pool, body, P, AHEAD, BEHIND, 2)
                for u in range(2):
                    pool.wait_ge(x1n_out[u], 16 * (T // 2))

            @block.tensor
            def _(pe):
                t_ = nc.tensor

                def turn(x, x_in, rows, out, lo_ready, ready):
                    p = x.par
                    pe.wait_ge(x_in[x.buf], 16 * (x.lap + 1))
                    if not x.is_zero():
                        b = x.before()
                        pe.wait_ge(lo_ready[b.par], b.turn + 1)
                    for k in range(KC):
                        last = t_.transpose(out[:, k * SLOTS:(k + 1) * SLOTS],
                                            rows[x.buf][:, k * 128:(k + 1) * 128], c.ident[0:SLOTS, 0:SLOTS])
                    last.then_inc(ready[p], 1)

                def query(x):
                    p = x.par
                    if x.is_zero():
                        wq.pe(pe)
                    pe.wait_ge(hi_s_ready[p], x.turn + 1)
                    pe.wait_ge(lo_s_ready[p], x.turn + 1)
                    pe.wait_ge(q_kept[p], x.turn)
                    product(t_, q_p[p][:, 0:D], xs_hi[p], xs_lo[p], wq.hi, wq.lo, SLOTS).then_inc(q_ready[p], 1)

                def keys(x):
                    p = x.par
                    if x.is_zero():
                        wk.pe(pe)
                    pe.wait_ge(hi_d_ready[p], x.turn + 1)
                    pe.wait_ge(lo_d_ready[p], x.turn + 1)
                    pe.wait_ge(prod_ready[p], x.turn)
                    product(t_, k_p[p][:, 0:D], xd_hi[p], xd_lo[p], wk.hi, wk.lo, SLOTS).then_inc(k_ready[p], 1)

                def scores(x):
                    p = x.par
                    pe.wait_ge(aw_ready[p], x.turn + 1)
                    pe.wait_ge(scanned[p], x.turn)
                    t_.transpose(score_p[p][:, 0:SLOTS], aw_col[p][:, :], c.ident[0:SLOTS, 0:SLOTS])
                    t_.transpose(score_p[p][:, SLOTS:2 * SLOTS], cut_col[p][:, :], c.ident[0:SLOTS, 0:SLOTS]) \
                        .then_inc(score_ready[p], 1)

                def body(at):
                    if x := at(0):
                        query(x)
                    if x := at(1):
                        turn(x, xs_in, xs, turned_s, lo_s_ready, turned_s_ready)
                    if x := at(0):
                        keys(x)
                    if x := at(-1):
                        scores(x)
                    if x := at(1):
                        turn(x, xd_in, xd, turned_d, lo_d_ready, turned_d_ready)
                sweep(pe, body, P, AHEAD, BEHIND, 2)

            @block.scalar
            def _(act):
                a = nc.scalar
                a.preload_act_table_set(TABLES)

                def high(x, turned_ready, turned, used, hi, ready):
                    p = x.par
                    act.wait_ge(turned_ready[p], x.turn + 1)
                    act.wait_ge(used[p], x.turn)
                    if hi is xd_hi:
                        act.wait_ge(halves_out[p], 32 * x.turn)
                    a.copy(hi[p][:, :], turned[:, 0:KC * SLOTS]).then_inc(ready[p], 1)

                def deviation(x):
                    p = x.par
                    act.wait_ge(moments_ready[p], x.turn + 1)
                    a.activation(logv[p][:, :], moments[p][:, 1:2], ACT.Ln, bias=c.ln_eps[0:ROWS, :]) \
                        .then_inc(log_ready[p], 1)
                    act.wait_ge(log_ready[p], x.turn + 1)
                    a.activation(rstd[p][:, :], logv[p][:, :], ACT.Exp, scale=-0.5).then_inc(rstd_ready[p], 1)

                def normalise(x):
                    p = x.par
                    act.wait_ge(shift_ready[p], x.turn + 1)
                    act.wait_ge(x1n_out[p], 16 * x.turn)
                    act.wait_ge(summed[p], x.turn)
                    a.activation(x1n[p][0:ROWS, :], xn[p][:, :], ACT.Identity, bias=shift[p][:, :],
                                 scale=rstd[p][:, :]).then_inc(x1n_ready[p], 1)
                    act.wait_ge(x1n_ready[p], x.turn + 1)
                    if not x.is_zero():
                        b = x.before()
                        act.wait_ge(summed_sq[b.par], b.turn + 1)
                    a.activation(sq[:, :], x1n[p][0:ROWS, :], ACT.Square).then_inc(sq_ready[p], 1)

                def keep_q(x):
                    p = x.par
                    act.wait_ge(q_ready[p], x.turn + 1)
                    act.wait_ge(prod_ready[p], x.turn)
                    a.mul(q[p][:, :], q_p[p][:, 0:D], DH ** -0.5).then_inc(q_kept[p], 1)

                act.wait_ge(cleared, 1)
                wq.act(act)
                wk.act(act)

                def body(at):
                    if x := at(0):
                        keep_q(x)
                    if x := at(1):
                        high(x, turned_s_ready, turned_s, q_ready, xs_hi, hi_s_ready)
                    if x := at(-1):
                        normalise(x)
                    if x := at(0):
                        deviation(x)
                    if x := at(1):
                        high(x, turned_d_ready, turned_d, k_ready, xd_hi, hi_d_ready)
                sweep(act, body, P, AHEAD, BEHIND, 2)

            @block.vector
            def _(dve):
                v = nc.vector
                v.memset(o.cut[:, E:E + 1], -BIG)
                v.memset(o.run_max[:, 0:1], -BIG)
                for u in range(2):
                    v.memset(x1n[u][:, :], 0.0)
                for m in acc:
                    v.memset(m[:, :], 0.0)
                v.memset(score_p[0][:, 0:1], 0.0).then_inc(cleared, 1)
                dve.wait_ge(cleared, 1)
                wq.dve(dve)
                wk.dve(dve)

                def low(x, hi_ready, turned, hi, lo, ready):
                    p = x.par
                    dve.wait_ge(hi_ready[p], x.turn + 1)
                    v.tensor_tensor(lo[p][:, :], turned[:, 0:KC * SLOTS], hi[p][:, :].bitcast(F32),
                                    ALU.subtract).then_inc(ready[p], 1)

                def measure(x):
                    p = x.par
                    dve.wait_ge(xn_in[p], 32 * (x.turn + 1))
                    dve.wait_ge(rstd_ready[p], x.turn)
                    v.bn_stats(stats[p][:, :], xn[p][:, :]).then_inc(stats_ready[p], 1)
                    dve.wait_ge(stats_ready[p], x.turn + 1)
                    settle(dve)
                    v.bn_aggr(moments[p][:, :], stats[p][:, :]).then_inc(moments_ready[p], 1)

                def centre(x):
                    p = x.par
                    dve.wait_ge(rstd_ready[p], x.turn + 1)
                    v.tensor_scalar(rstd[p][:, :], rstd[p][:, :], s.empty[:, ds(x.num, 1)], None, ALU.mult) \
                        .then_inc(masked[p], 1)
                    dve.wait_ge(masked[p], x.turn + 1)
                    dve.wait_ge(moments_ready[p], x.turn + 1)
                    v.tensor_scalar(shift[p][:, :], moments[p][:, 0:1], -1.0, rstd[p][:, :], ALU.mult, ALU.mult) \
                        .then_inc(shift_ready[p], 1)

                def sum_up(x):
                    p, b = x.par, x.before()
                    dve.wait_ge(x1n_ready[p], x.turn + 1)
                    if not x.is_zero():
                        dve.wait_ge(summed[b.par], b.turn + 1)
                        dve.wait_ge(summed_sq[b.par], b.turn + 1)
                    v.tensor_tensor(acc[0][0:ROWS, :], acc[0][0:ROWS, :], x1n[p][0:ROWS, :],
                                    ALU.add).then_inc(summed[p], 1)
                    dve.wait_ge(sq_ready[p], x.turn + 1)
                    v.tensor_tensor(acc[1][0:ROWS, :], acc[1][0:ROWS, :], sq[:, :],
                                    ALU.add).then_inc(summed_sq[p], 1)

                def scan(x):
                    p = x.par
                    dve.wait_ge(score_ready[p], x.turn + 1)
                    v.tensor_copy(o.aw[:, ds(ROWS * x.num, ROWS)], score_p[p][:, 1:SLOTS])
                    v.tensor_copy(o.cut[:, ds(ROWS * x.num, ROWS)], score_p[p][:, SLOTS + 1:2 * SLOTS]) \
                        .then_inc(cut_kept, 1)
                    dve.wait_ge(cut_kept, x.num + 1)
                    if not x.is_zero():
                        b = x.before()
                        dve.wait_ge(scanned[b.par], b.turn + 1)
                    v.tensor_tensor_scan(o.run_max[:, ds(ROWS * x.num + 1, ROWS)], o.cut[:, ds(ROWS * x.num, ROWS)],
                                         score_p[p][:, 1:SLOTS], o.run_max[:, ds(ROWS * x.num, 1)],
                                         ALU.add, ALU.max).then_inc(scanned[p], 1)

                def score(x):
                    p = x.par
                    dve.wait_ge(score_ready[p], x.turn)
                    v.tensor_copy(cut_col[p][:, :], s.cut[:, ds(x.num, 1)].to_broadcast([SLOTS, H]))
                    dve.wait_ge(q_kept[p], x.turn + 1)
                    dve.wait_ge(k_ready[p], x.turn + 1)
                    dve.wait_ge(aw_ready[p], x.turn)
                    v.tensor_tensor(qk[p][:, :], q[p][:, :], k_p[p][:, 0:D], ALU.mult).then_inc(prod_ready[p], 1)
                    dve.wait_ge(prod_ready[p], x.turn + 1)
                    v.tensor_reduce(aw_col[p][:, :], qk[p][:, :].rearrange("p (h d) -> p h d", h=H),
                                    op=ALU.add, axis=AX.X).then_inc(aw_ready[p], 1)

                def body(at):
                    if x := at(-2):
                        sum_up(x)
                    if x := at(1):
                        low(x, hi_s_ready, turned_s, xs_hi, xs_lo, lo_s_ready)
                    if x := at(0):
                        measure(x)
                    if x := at(-2):
                        scan(x)
                    if x := at(0):
                        score(x)
                    if x := at(1):
                        low(x, hi_d_ready, turned_d, xd_hi, xd_lo, lo_d_ready)
                    if x := at(0):
                        centre(x)
                sweep(dve, body, P, AHEAD, BEHIND, 2)
    return o


def attend_edges(nc, ctx, c, s, e, w_d, x1_d, own_d, other_d, acc):
    with ExitStack() as own:
        semaphores = Semaphores(nc, own)
        def sb(name, shape, dt=F32):
            return own.enter_context(nc.sbuf_tensor(f"b_{name}", shape, dt))

        def pb(name, shape):
            return own.enter_context(nc.psum_tensor(f"b_{name}", shape, F32))

        def sem(name):
            return semaphores.take(f"b_{name}")

        def two(make, name, *a):
            return [make(f"{name}{u}", *a) for u in range(2)]

        wv = SplitWeights(nc, own, semaphores, "wv", w_d, 2 * D, 3 * D)

        P = 4
        out_idx = two(sb, "out_idx", [SLOTS, 1], U32)
        xr = [sb(f"xr{u}", [SLOTS, D]) for u in range(P)]
        xd_hi, xd_lo = ([sb(f"{n}{u}", [128, KC * SLOTS], F32R) for u in range(P)] for n in ("xd_hi", "xd_lo"))
        top = two(sb, "top", [H, SLOTS])
        gap = two(sb, "gap", [H, ROWS])
        cut_next, run_max = two(sb, "cut_next", [H, ROWS]), two(sb, "run_max", [H, ROWS])
        prob = two(sb, "prob", [H, SLOTS])
        key_col = two(sb, "key_col", [SLOTS, 1])
        group = two(sb, "group", [SLOTS, SLOTS])
        pv = two(sb, "pv", [SLOTS, D + H])
        recip = two(sb, "recip", [SLOTS, H])
        mixed = two(sb, "mixed", [SLOTS, D])
        x1, sq = two(sb, "x1", [SLOTS, D]), two(sb, "sq", [SLOTS, D])
        stats, moments = two(sb, "stats", [SLOTS, 6]), two(sb, "moments", [SLOTS, 2])
        logv, rstd, shift = two(sb, "logv", [SLOTS, 1]), two(sb, "rstd", [SLOTS, 1]), two(sb, "shift", [SLOTS, 1])

        v_p, acc_p = two(pb, "v_p", [SLOTS, 512]), two(pb, "acc_p", [SLOTS, 512])
        small_p = two(pb, "small_p", [SLOTS, 512])
        weight_p = pb("weight_p", [SLOTS, 512])
        KEYS, PROB = slice(0, SLOTS), slice(128, 128 + H)

        cleared = sem("cleared")
        out_idx_ready, x1_out = two(sem, "out_idx_ready"), two(c.pool_dma, "b_x1_out")
        xd_in, xr_in = ([sem(f"{n}{u}") for u in range(P)] for n in ("xd_in", "xr_in"))
        gap_ready, prob_ready, top_ready = two(sem, "gap_ready"), two(sem, "prob_ready"), sem("top_ready")
        col_ready, prob_t_ready, prob_kept = two(sem, "col_ready"), two(sem, "prob_t_ready"), two(sem, "prob_kept")
        keys_ready, group_ready = two(sem, "keys_ready"), two(sem, "group_ready")
        v_ready, pv_ready, carried = two(sem, "v_ready"), two(sem, "pv_ready"), two(sem, "carried")
        sum_ready, mixed_ready = two(sem, "sum_ready"), two(sem, "mixed_ready")
        quotient_ready, stats_ready = two(sem, "quotient_ready"), two(sem, "stats_ready")
        recip_ready = two(sem, "recip_ready")
        scan_in_ready = two(sem, "scan_in_ready")
        moments_ready, log_ready, rstd_ready = two(sem, "moments_ready"), two(sem, "log_ready"), two(sem, "rstd_ready")
        shift_ready, x1_ready = two(sem, "shift_ready"), two(sem, "x1_ready")
        sq_ready, masked = two(sem, "sq_ready"), two(sem, "masked")
        summed, summed_sq = two(sem, "summed"), two(sem, "summed_sq")

        AHEAD, BEHIND = 3, 4

        def place(x):
            return (T - 1) - x.num

        with nc.Block() as block:
            @block.gpsimd
            def _(pool):
                g = nc.gpsimd

                def scatter(x):
                    p = x.par
                    pool.wait_ge(x1_out[p], 16 * x.turn)
                    settle(pool)
                    g.tensor_copy(out_idx[p][:, :], s.first_row[:, ds(place(x), 1)]).then_inc(out_idx_ready[p], 1)
                    pool.wait_ge(out_idx_ready[p], x.turn + 1)
                    pool.wait_ge(x1_ready[p], x.turn + 1)
                    settle(pool)
                    g.indirect_dma_start(x1_d, bass.IndirectOffsetOnAxis(out_idx[p][:, :], 0), x1[p][:, :], None,
                                         bounds_check=N - 1, oob_is_err=False).then_inc(x1_out[p], 16)

                def sum_up(x):
                    p, b = x.par, x.before()
                    pool.wait_ge(x1_ready[p], x.turn + 1)
                    if not x.is_zero():
                        pool.wait_ge(summed[b.par], b.turn + 1)
                    g.tensor_tensor(acc[0][:, :], acc[0][:, :], x1[p][:, :], ALU.add).then_inc(summed[p], 1)

                def add_own(x):
                    p, u = x.par, x.buf
                    pool.wait_ge(quotient_ready[p], x.turn + 1)
                    pool.wait_ge(xr_in[u], 16 * (x.lap + 1))
                    g.tensor_tensor(xr[u][:, :], mixed[p][:, :], xr[u][:, :], ALU.add).then_inc(mixed_ready[p], 1)

                def body(at):
                    if x := at(-2):
                        add_own(x)
                    if x := at(-4):
                        scatter(x)
                        sum_up(x)
                sweep(pool, body, P, AHEAD, BEHIND, 2)
                for u in range(2):
                    pool.wait_ge(x1_out[u], 16 * (T // 2))

            @block.sync
            def _(sp):
                wv.load(sp)

                def load_other(x):
                    if x.again():
                        sp.wait_ge(v_ready[x.par], x.turn - 1)
                    settle(sp)
                    for half, out in ((0, xd_hi), (1, xd_lo)):
                        sp.dma_start(out[x.buf][:, :].bitcast(F32), other_d[half, ds(128 * place(x), 128), :]) \
                            .then_inc(xd_in[x.buf], 16)

                def load_own(x):
                    if x.again():
                        sp.wait_ge(x1_ready[x.par], x.turn - 1)
                    settle(sp)
                    sp.dma_start(xr[x.buf][:, :], own_d[ds(SLOTS * place(x), SLOTS), :]).then_inc(xr_in[x.buf], 16)

                def body(at):
                    if x := at(3):
                        load_other(x)
                    if x := at(0):
                        load_own(x)
                sweep(sp, body, P, AHEAD, BEHIND, 2)

            @block.tensor
            def _(pe):
                t_ = nc.tensor

                def small(x):
                    p = x.par
                    pe.wait_ge(prob_ready[p], x.turn + 1)
                    pe.wait_ge(prob_kept[p], x.turn)
                    pe.wait_ge(group_ready[p], x.turn)
                    settle(pe)
                    t_.transpose(small_p[p][:, PROB], prob[p][:, :], c.ident[0:H, 0:H]).then_inc(prob_t_ready[p], 1)
                    pe.wait_ge(col_ready[p], x.turn + 1)
                    t_.matmul(small_p[p][:, KEYS], key_col[p][:, :].to_broadcast([SLOTS, SLOTS]),
                              c.ident[0:SLOTS, 0:SLOTS], start=True, stop=True).then_inc(keys_ready[p], 1)

                def values(x):
                    p = x.par
                    if x.is_zero():
                        wv.pe(pe)
                    pe.wait_ge(xd_in[x.buf], 32 * (x.lap + 1))
                    pe.wait_ge(pv_ready[p], x.turn)
                    product(t_, v_p[p][:, 0:D], xd_hi[x.buf], xd_lo[x.buf], wv.hi, wv.lo, SLOTS).then_inc(v_ready[p], 1)

                def group_sum(x):
                    p = x.par
                    pe.wait_ge(group_ready[p], x.turn + 1)
                    pe.wait_ge(carried[p], x.turn + 1)
                    pe.wait_ge(quotient_ready[p], x.turn)
                    if not x.is_zero():
                        b = x.before()
                        pe.wait_ge(recip_ready[b.par], b.turn + 1)
                    t_.matmul(acc_p[p][:, 0:D], group[p][:, :], pv[p][:, 0:D], start=True, stop=True)
                    t_.matmul(weight_p[:, 0:H], group[p][:, :], pv[p][:, D:D + H],
                              start=True, stop=True).then_inc(sum_ready[p], 1)

                def body(at):
                    if x := at(0):
                        values(x)
                    if x := at(1):
                        small(x)
                    if x := at(-1):
                        group_sum(x)
                sweep(pe, body, P, AHEAD, BEHIND, 2)

            @block.scalar
            def _(act):
                a = nc.scalar
                a.preload_act_table_set(TABLES)

                def carry(x):
                    p = x.par
                    act.wait_ge(pv_ready[p], x.turn + 1)
                    if not x.is_zero():
                        b = x.before()
                        act.wait_ge(sum_ready[b.par], b.turn + 1)
                    a.copy(pv[p][0:1, 0:D], acc_p[1 - p][0:1, 0:D])
                    a.copy(pv[p][0:1, D:D + H], weight_p[0:1, 0:H]).then_inc(carried[p], 1)

                def take_scores(x):
                    p = x.par
                    at_ = ROWS * place(x)
                    if not isinstance(x.turn, int) or x.turn > 0:
                        act.wait_ge(top_ready, x.num - 1)
                    settle(act)
                    a.copy(cut_next[p][:, :], e.cut[:, ds(at_ + 1, ROWS)])
                    a.copy(run_max[p][:, :], e.run_max[:, ds(at_ + 1, ROWS)]).then_inc(scan_in_ready[p], 1)

                def exps(x):
                    p = x.par
                    act.wait_ge(gap_ready[p], x.turn + 1)
                    act.wait_ge(prob_t_ready[p], x.turn)
                    a.activation(prob[p][:, 1:SLOTS], gap[p][:, :], ACT.Exp).then_inc(prob_ready[p], 1)

                def deviation(x):
                    p = x.par
                    act.wait_ge(moments_ready[p], x.turn + 1)
                    a.activation(logv[p][:, :], moments[p][:, 1:2], ACT.Ln, bias=c.ln_eps[0:SLOTS, :]) \
                        .then_inc(log_ready[p], 1)
                    act.wait_ge(log_ready[p], x.turn + 1)
                    a.activation(rstd[p][:, :], logv[p][:, :], ACT.Exp, scale=-0.5).then_inc(rstd_ready[p], 1)

                def normalise(x):
                    p = x.par
                    act.wait_ge(shift_ready[p], x.turn + 1)
                    act.wait_ge(x1_out[p], 16 * x.turn)
                    act.wait_ge(summed[p], x.turn)
                    a.activation(x1[p][:, :], xr[x.buf][:, :], ACT.Identity, bias=shift[p][:, :],
                                 scale=rstd[p][:, :]).then_inc(x1_ready[p], 1)
                    act.wait_ge(x1_ready[p], x.turn + 1)
                    act.wait_ge(summed_sq[p], x.turn)
                    a.activation(sq[p][:, :], x1[p][:, :], ACT.Square).then_inc(sq_ready[p], 1)

                wv.act(act)
                act.wait_ge(cleared, 1)
                def body(at):
                    if x := at(-1):
                        carry(x)
                    if x := at(-4):
                        normalise(x)
                    if x := at(3):
                        take_scores(x)
                    if x := at(2):
                        exps(x)
                    if x := at(-3):
                        deviation(x)
                sweep(act, body, P, AHEAD, BEHIND, 2)

            @block.vector
            def _(dve):
                v = nc.vector
                for u in range(2):
                    v.memset(prob[u][:, :], 0.0)
                v.memset(top[1][:, :], 0.0)
                v.memset(acc_p[1][:, :], 0.0)
                v.memset(weight_p[:, :], 0.0).then_inc(cleared, 1)
                wv.dve(dve)
                dve.wait_ge(cleared, 1)

                def maximum(x):
                    p = x.par
                    dve.wait_ge(scan_in_ready[p], x.turn + 1)
                    if not x.is_zero():
                        dve.wait_ge(top_ready, x.num)
                    dve.wait_ge(gap_ready[p], x.turn)
                    settle(dve)
                    v.tensor_tensor_scan(top[p][:, 1:SLOTS][:, ::-1], cut_next[p][:, ::-1],
                                         run_max[p][:, ::-1], top[1 - p][:, 1:2],
                                         ALU.add, ALU.max).then_inc(top_ready, 1)

                def below_maximum(x):
                    p = x.par
                    at_ = ROWS * place(x)
                    dve.wait_ge(top_ready, x.num + 1)
                    dve.wait_ge(prob_ready[p], x.turn)
                    settle(dve)
                    v.tensor_tensor(gap[p][:, :], e.aw[:, ds(at_, ROWS)], top[p][:, 1:SLOTS],
                                    ALU.subtract).then_inc(gap_ready[p], 1)

                def take_keys(x):
                    p = x.par
                    dve.wait_ge(keys_ready[p], x.turn)
                    settle(dve)
                    v.tensor_copy(key_col[p][:, :], s.key_out[:, ds(place(x), 1)]).then_inc(col_ready[p], 1)

                def take_weights(x):
                    p = x.par
                    dve.wait_ge(keys_ready[p], x.turn + 1)
                    dve.wait_ge(sum_ready[p], x.turn)
                    v.tensor_copy(pv[p][:, D:D + H], small_p[p][:, PROB]).then_inc(prob_kept[p], 1)

                def same_group(x):
                    p = x.par
                    dve.wait_ge(keys_ready[p], x.turn + 1)
                    settle(dve)
                    v.tensor_scalar(group[p][:, :], small_p[p][:, KEYS], s.key_in[:, ds(place(x), 1)], None,
                                    ALU.is_equal).then_inc(group_ready[p], 1)

                def weigh(x):
                    p = x.par
                    dve.wait_ge(v_ready[p], x.turn + 1)
                    dve.wait_ge(prob_kept[p], x.turn + 1)
                    v.tensor_tensor(pv[p][:, 0:D].rearrange("p (h d) -> p h d", h=H),
                                    v_p[p][:, 0:D].rearrange("p (h d) -> p h d", h=H),
                                    pv[p][:, D:D + H].unsqueeze(2).to_broadcast([SLOTS, H, DH]),
                                    ALU.mult).then_inc(pv_ready[p], 1)

                def invert(x):
                    p = x.par
                    dve.wait_ge(sum_ready[p], x.turn + 1)
                    if not x.is_last():
                        n = x.after()
                        dve.wait_ge(carried[n.par], n.turn + 1)
                    v.reciprocal(recip[p][:, :], weight_p[:, 0:H]).then_inc(recip_ready[p], 1)

                def divide_by_weights(x):
                    p = x.par
                    dve.wait_ge(recip_ready[p], x.turn + 1)
                    dve.wait_ge(mixed_ready[p], x.turn)
                    v.tensor_tensor(mixed[p][:, :].rearrange("p (h d) -> p h d", h=H),
                                    acc_p[p][:, 0:D].rearrange("p (h d) -> p h d", h=H),
                                    recip[p][:, :].unsqueeze(2).to_broadcast([SLOTS, H, DH]), ALU.mult) \
                        .then_inc(quotient_ready[p], 1)

                def sum_squares(x):
                    p, b = x.par, x.before()
                    dve.wait_ge(sq_ready[p], x.turn + 1)
                    if not x.is_zero():
                        dve.wait_ge(summed_sq[b.par], b.turn + 1)
                    v.tensor_tensor(acc[1][:, :], acc[1][:, :], sq[p][:, :], ALU.add).then_inc(summed_sq[p], 1)

                def measure(x):
                    p = x.par
                    dve.wait_ge(mixed_ready[p], x.turn + 1)
                    dve.wait_ge(moments_ready[p], x.turn)
                    settle(dve)
                    v.bn_stats(stats[p][:, :], xr[x.buf][:, :]).then_inc(stats_ready[p], 1)

                def gather_moments(x):
                    p = x.par
                    dve.wait_ge(stats_ready[p], x.turn + 1)
                    dve.wait_ge(shift_ready[p], x.turn)
                    settle(dve)
                    v.bn_aggr(moments[p][:, :], stats[p][:, :]).then_inc(moments_ready[p], 1)

                def centre(x):
                    p = x.par
                    dve.wait_ge(rstd_ready[p], x.turn + 1)
                    settle(dve)
                    v.tensor_scalar(rstd[p][:, :], rstd[p][:, :], s.first[:, ds(place(x), 1)], None, ALU.mult) \
                        .then_inc(masked[p], 1)
                    dve.wait_ge(masked[p], x.turn + 1)
                    dve.wait_ge(moments_ready[p], x.turn + 1)
                    v.tensor_scalar(shift[p][:, :], moments[p][:, 0:1], -1.0, rstd[p][:, :], ALU.mult, ALU.mult) \
                        .then_inc(shift_ready[p], 1)

                def body(at):
                    if x := at(-1):
                        weigh(x)
                    if x := at(-4):
                        centre(x)
                    if x := at(0):
                        take_weights(x)
                        same_group(x)
                    if x := at(2):
                        maximum(x)
                    if x := at(-2):
                        invert(x)
                    if x := at(-3):
                        measure(x)
                    if x := at(2):
                        below_maximum(x)
                    if x := at(-2):
                        divide_by_weights(x)
                    if x := at(-3):
                        gather_moments(x)
                    if x := at(2):
                        take_keys(x)
                    if x := at(-4):
                        sum_squares(x)
                sweep(dve, body, P, AHEAD, BEHIND, 2)


def gather_sums(nc, ctx, c, s, x1_d, sums_d, w):
    P = 4
    with ExitStack() as own:
        semaphores = Semaphores(nc, own)
        def sb(name, shape, dt=F32):
            return own.enter_context(nc.sbuf_tensor(f"g_{name}", shape, dt))

        def sem(name):
            return semaphores.take(f"g_{name}")

        def ring(make, name, *a):
            return [make(f"{name}{u}", *a) for u in range(P)]

        idx = ring(sb, "idx", [SLOTS, 1], U32)
        rows = ring(sb, "rows", [SLOTS, D])
        key_col = ring(sb, "key_col", [SLOTS, 1])
        group = ring(sb, "group", [SLOTS, SLOTS])
        total = ring(sb, "total", [SLOTS, D])
        sum_p = [own.enter_context(nc.psum_tensor(f"g_sum_p{u}", [SLOTS, 512], F32)) for u in range(P)]
        keys_p = [own.enter_context(nc.psum_tensor(f"g_keys_p{u}", [SLOTS, 512], F32)) for u in range(P)]

        cleared = sem("cleared")
        rows_in = ring(c.pool_dma, "g_rows_in")
        idx_ready, col_ready, keys_ready, group_ready, carried, sum_ready, total_ready, total_out = (
            ring(sem, n) for n in ("idx_ready", "col_ready", "keys_ready", "group_ready", "carried",
                                   "sum_ready", "total_ready", "total_out"))
        AHEAD, BEHIND = 4, 1

        def place(x):
            return (T - 1) - x.num

        with nc.Block() as block:
            @block.gpsimd
            def _(pool):
                g = nc.gpsimd

                def body(at):
                    if x := at(3):
                        p = x.par
                        pool.wait_ge(sum_ready[p], x.turn)
                        settle(pool)
                        g.tensor_copy(idx[p][:, :], s.val_row[:, ds(place(x), 1)]).then_inc(idx_ready[p], 1)
                        pool.wait_ge(idx_ready[p], x.turn + 1)
                        settle(pool)
                        g.indirect_dma_start(rows[p][:, :], None, x1_d, bass.IndirectOffsetOnAxis(idx[p][:, :], 0)) \
                            .then_inc(rows_in[p], 16)
                sweep(pool, body, P, AHEAD, BEHIND)

            @block.tensor
            def _(pe):
                t_ = nc.tensor

                def body(at):
                    if x := at(1):
                        p = x.par
                        pe.wait_ge(col_ready[p], x.turn + 1)
                        pe.wait_ge(group_ready[p], x.turn)
                        t_.matmul(keys_p[p][:, 0:SLOTS], key_col[p][:, :].to_broadcast([SLOTS, SLOTS]),
                                  c.ident[0:SLOTS, 0:SLOTS], start=True, stop=True).then_inc(keys_ready[p], 1)
                    if x := at(0):
                        p = x.par
                        pe.wait_ge(group_ready[p], x.turn + 1)
                        pe.wait_ge(carried[p], x.turn + 1)
                        pe.wait_ge(total_ready[p], x.turn)
                        t_.matmul(sum_p[p][:, 0:D], group[p][:, :], rows[p][:, :],
                                  start=True, stop=True).then_inc(sum_ready[p], 1)
                sweep(pe, body, P, AHEAD, BEHIND)

            @block.scalar
            def _(act):
                a = nc.scalar
                act.wait_ge(cleared, 1)

                def body(at):
                    if x := at(0):
                        p = x.par
                        act.wait_ge(rows_in[p], 16 * (x.turn + 1))
                        if not x.is_zero():
                            b = x.before()
                            act.wait_ge(sum_ready[b.par], b.turn + 1)
                        a.copy(rows[p][0:1, :], sum_p[x.before().par][0:1, 0:D]).then_inc(carried[p], 1)
                sweep(act, body, P, AHEAD, BEHIND)

            @block.vector
            def _(dve):
                v = nc.vector
                v.memset(w.bias_row[:, :], 0.0).then_inc(w.cleared, 1)
                v.memset(sum_p[P - 1][:, :], 0.0).then_inc(cleared, 1)

                def body(at):
                    if x := at(2):
                        p = x.par
                        dve.wait_ge(keys_ready[p], x.turn)
                        settle(dve)
                        v.tensor_copy(key_col[p][:, :], s.key_out[:, ds(place(x), 1)]).then_inc(col_ready[p], 1)
                    if x := at(1):
                        p = x.par
                        dve.wait_ge(keys_ready[p], x.turn + 1)
                        dve.wait_ge(sum_ready[p], x.turn)
                        settle(dve)
                        v.tensor_scalar(group[p][:, :], keys_p[p][:, 0:SLOTS], s.key_in[:, ds(place(x), 1)], None,
                                        ALU.is_equal).then_inc(group_ready[p], 1)
                    if x := at(-1):
                        p = x.par
                        dve.wait_ge(sum_ready[p], x.turn + 1)
                        dve.wait_ge(total_out[p], 16 * x.turn)
                        if not x.is_last():
                            n = x.after()
                            dve.wait_ge(carried[n.par], n.turn + 1)
                        v.tensor_copy(total[p][:, :], sum_p[p][:, 0:D]).then_inc(total_ready[p], 1)
                sweep(dve, body, P, AHEAD, BEHIND)

            @block.sync
            def _(sp):
                w.load(sp)
                def body(at):
                    if x := at(-1):
                        p = x.par
                        sp.wait_ge(total_ready[p], x.turn + 1)
                        settle(sp)
                        sp.dma_start(sums_d[ds(SLOTS * place(x), SLOTS), :], total[p][:, :]).then_inc(total_out[p], 16)
                sweep(sp, body, P, AHEAD, BEHIND)
                for u in range(P):
                    sp.wait_ge(total_out[u], 16 * (T // P))


def column_variance(v, link, sums_p, mean, square, var, ready):
    link(v.tensor_scalar(mean[:, :], sums_p[:, 0:KC], 1.0 / N, None, ALU.mult))
    link(v.tensor_scalar(var[:, :], sums_p[:, KC:2 * KC], 1.0 / N, None, ALU.mult))
    link(v.tensor_tensor(square[:, :], mean[:, :], mean[:, :], ALU.mult))
    link(v.tensor_tensor(var[:, :], var[:, :], square[:, :], ALU.subtract))
    v.tensor_scalar(var[:, :], var[:, :], 0.0, BN_EPS, ALU.max, ALU.add).then_inc(ready, 1)


def second_layer_buffers(nc, ctx):
    o, n = Buffers(), Buffers()
    o.first_mix = ctx.enter_context(nc.sbuf_tensor("first_mix", [128, D], F32))
    o.rest_mix = ctx.enter_context(nc.sbuf_tensor("rest_mix", [128, D], F32))

    def keep(name, shape, dt=F32):
        return ctx.enter_context(nc.sbuf_tensor(f"n_{name}", shape, dt))

    n.w_hi, n.w_lo = keep("w_hi", [128, KC, D], F32R), keep("w_lo", [128, KC, D], F32R)
    n.shift_w = keep("shift_w", [128, D])
    n.bias = keep("bias", [64, D], F32R)
    n.ones = keep("ones", [64, ROWS], F32R)
    return o, n


def second_layer_weights(nc, ctx, semaphores, wq_d, wk_d, wv_d, wo_d, proj_d, g_d, b_d, w_d, bias_d):
    w = Buffers()

    def sb(name, shape):
        return ctx.enter_context(nc.sbuf_tensor(f"w_{name}", shape, F32))

    w.wq, w.wk, w.wv, w.wo, w.conv = (sb(m, [128, KC, D]) for m in ("wq", "wk", "wv", "wo", "conv"))
    w.proj = sb("proj", [128, M // 128, DH])
    w.g_col, w.b_col, w.bias_row = sb("g_col", [128, KC]), sb("b_col", [128, KC]), sb("bias_row", [64, D])
    w.loaded, w.cleared = semaphores.take("w_loaded"), semaphores.take("w_cleared")
    w.all = 16 * 10

    def load(sp):
        for into, of in ((w.wq, wq_d), (w.wk, wk_d), (w.wv, wv_d), (w.wo, wo_d), (w.conv, w_d)):
            sp.dma_start(into[:, :, :], of.rearrange("(k p) n -> p k n", p=128)).then_inc(w.loaded, 16)
        sp.dma_start(w.proj[:, :, :], proj_d.rearrange("(c p) d -> p c d", p=128)).then_inc(w.loaded, 16)
        for into, of in ((w.g_col, g_d), (w.b_col, b_d)):
            sp.dma_start(into[:, :], of.rearrange("(k p) -> p k", p=128), allow_slow_non_contiguous=True) \
                .then_inc(w.loaded, 16)
        sp.wait_ge(w.cleared, 1)
        for row in (0, 32):
            sp.dma_start(w.bias_row[row:row + 1, :], bias_d.rearrange("(a n) -> a n", a=1)).then_inc(w.loaded, 16)
    w.load = load
    return w


class FirstNorm:

    def __init__(self, nc, own, semaphores, c, acc, w, o, sums_p, row_p, wide_p):
        self.nc, self.c, self.acc, self.w, self.o = nc, c, acc, w, o
        self.sums_p, self.row_p, self.wide_p = sums_p, row_p, wide_p

        def sb(name, shape):
            return own.enter_context(nc.sbuf_tensor(f"n_{name}", shape, F32))

        self.w_scaled = sb("w_scaled", [128, KC, D])
        self.a_col, self.s_col, self.var, self.mean, self.logv = (
            sb(m, [128, KC]) for m in ("a_col", "s_col", "var", "mean", "logv"))
        self.shift_row = sb("shift_row", [1, D])
        self.sums_ready, self.chain, self.var_ready, self.log_ready, self.rstd_ready, self.shift_ready, \
            self.row_ready, self.row_kept, self.wide_ready, self.scaled, self.high, self.bias_high = (
                semaphores.take(f"n_{m}") for m in (
                    "sums_ready", "chain", "var_ready", "log_ready", "rstd_ready", "shift_ready", "row_ready",
                    "row_kept", "wide_ready", "scaled", "high", "bias_high"))

    def pe_sums(self, pe):
        for j in range(2):
            for k in range(KC):
                last = self.nc.tensor.matmul(self.sums_p[:, j * KC + k:j * KC + k + 1],
                                             self.acc[j][:, k * 128:(k + 1) * 128],
                                             self.c.ones[0:SLOTS, 0:1], start=True, stop=True)
        last.then_inc(self.sums_ready, 1)

    def pe_row(self, pe):
        pe.wait_ge(self.shift_ready, 1)
        for k in range(KC):
            last = self.nc.tensor.matmul(self.row_p[0:1, 0:D], self.s_col[:, k:k + 1], self.w.conv[:, k, :],
                                         start=(k == 0), stop=(k == KC - 1))
        last.then_inc(self.row_ready, 1)

    def pe_wide(self, pe):
        pe.wait_ge(self.row_kept, 1)
        self.nc.tensor.matmul(self.wide_p[:, 0:D], self.c.ones[0:1, :], self.shift_row[:, :],
                              start=True, stop=True).then_inc(self.wide_ready, 1)

    def act_deviation(self, act):
        a = self.nc.scalar
        act.wait_ge(self.var_ready, 1)
        a.activation(self.logv[:, :], self.var[:, :], ACT.Ln).then_inc(self.log_ready, 1)
        act.wait_ge(self.log_ready, 1)
        a.activation(self.var[:, :], self.logv[:, :], ACT.Exp, scale=-0.5).then_inc(self.rstd_ready, 1)
        act.wait_ge(self.scaled, KC)
        a.copy(self.o.w_hi[:, :, :], self.w_scaled[:, :, :]).then_inc(self.high, 1)

    def act_row(self, act):
        act.wait_ge(self.row_ready, 1)
        self.nc.scalar.copy(self.shift_row[:, :], self.row_p[0:1, 0:D]).then_inc(self.row_kept, 1)

    def dve_scale(self, dve):
        v, w, o, done = self.nc.vector, self.w, self.o, [0]

        def link(ins):
            done[0] += 1
            ins.then_inc(self.chain, 1)
            dve.wait_ge(self.chain, done[0])

        dve.wait_ge(self.sums_ready, 1)
        column_variance(v, link, self.sums_p, self.mean, self.a_col, self.var, self.var_ready)
        v.tensor_copy(o.ones[:, :], self.c.ones[0:64, 0:ROWS])
        dve.wait_ge(w.loaded, w.all)
        v.tensor_copy(o.bias[:, :], w.bias_row[:, :]).then_inc(self.bias_high, 1)
        dve.wait_ge(self.bias_high, 1)
        v.tensor_tensor(o.bias[32:64, :], w.bias_row[32:64, :], o.bias[32:64, :].bitcast(F32), ALU.subtract)
        dve.wait_ge(self.rstd_ready, 1)
        link(v.tensor_tensor(self.a_col[:, :], self.var[:, :], w.g_col[:, :], ALU.mult))
        link(v.tensor_tensor(self.mean[:, :], self.mean[:, :], self.a_col[:, :], ALU.mult))
        v.tensor_tensor(self.s_col[:, :], w.b_col[:, :], self.mean[:, :], ALU.subtract).then_inc(self.shift_ready, 1)
        for k in range(KC):
            v.tensor_scalar(self.w_scaled[:, k, :], w.conv[:, k, :], self.a_col[:, k:k + 1], None, ALU.mult) \
                .then_inc(self.scaled, 1)
        dve.wait_ge(self.high, 1)
        v.tensor_tensor(o.w_lo[:, :, :], self.w_scaled[:, :, :], o.w_hi[:, :, :].bitcast(F32), ALU.subtract)

    def dve_shift(self, dve):
        dve.wait_ge(self.wide_ready, 1)
        self.nc.vector.tensor_copy(self.o.shift_w[:, :], self.wide_p[:, 0:D])


def few_node_attention(nc, c, x1_d, w, o, n, acc):
    MC = M // 128
    W1 = DH + 1
    with ExitStack() as own:
        semaphores = Semaphores(nc, own)
        def sb(name, shape, dt=F32):
            return own.enter_context(nc.sbuf_tensor(f"t_{name}", shape, dt))

        def sem(name):
            return semaphores.take(f"t_{name}")

        h = sb("h", [MAXN, D])
        wq, wk, wv, wo, proj = w.wq, w.wk, w.wv, w.wo, w.proj
        proj_t = sb("proj_t", [DH, M])
        h_t = sb("h_t", [128, KC * MAXN])
        q_t, k_t, q_sq, k_sq = (sb(n, [DH, H * MAXN]) for n in ("q_t", "k_t", "q_sq", "k_sq"))
        half = sb("half", [DH, 1])
        v1 = sb("v1", [MAXN, H, W1])
        qf, kf = sb("qf", [MAXN, H * M]), sb("kf", [MAXN, H * M])
        diag, peak, bias = sb("diag", [MAXN, 2 * H]), sb("peak", [MAXN, 2 * H]), sb("bias", [MAXN, 2 * H])
        peak_t = sb("peak_t", [H, 1])
        qf_t = sb("qf_t", [128, H * MC * MAXN])
        kv = sb("kv", [128, H * MC, W1])
        z = sb("z", [MAXN, H])
        attn, attn_t, out = sb("attn", [MAXN, D]), sb("attn_t", [128, KC * MAXN]), sb("out", [MAXN, D])
        last_row, own_row = sb("last_row", [MAXN, 128]), sb("own_row", [MAXN, 128])
        bank = [own.enter_context(nc.psum_tensor(f"t_bank{i}", [128, 512], F32)) for i in range(8)]

        names = ("loaded h_turned h_kept qkv_ready qkv_kept features_ready q_seen k_ready k_seen peak_turned "
                 "peak_down peak_wide biases q_exp k_exp q_done k_done outer_ready outer_kept mixed_ready "
                 "attn_ready attn_turned attn_kept out_ready out_kept wide_ready chain picks picks_made half_made "
                 "squares").split()
        S = {m: sem(m) for m in names}
        norm = FirstNorm(nc, own, semaphores, c, acc, w, n, bank[7], bank[7], bank[3])

        with nc.Block() as block:
            @block.sync
            def _(sp):
                sp.dma_start(h[:, :], x1_d[0:MAXN, :]).then_inc(S["loaded"], 16)

            @block.gpsimd
            def _(pool):
                g = nc.gpsimd
                g.affine_select(out=last_row[:, :], in_=c.ones[0:MAXN, :], compare_op=ALU.is_ge, fill=0.0,
                                base=-(MAXN - 1), pattern=[[0, 128]], channel_multiplier=1).then_inc(S["picks"], 1)
                pool.wait_ge(S["picks"], 1)
                g.affine_select(out=own_row[:, :], in_=last_row[:, :], compare_op=ALU.is_gt, fill=0.0,
                                base=-(MAXN - 1), pattern=[[1, 128]], channel_multiplier=0).then_inc(S["picks"], 1)

            @block.tensor
            def _(pe):
                t_ = nc.tensor
                norm.pe_sums(pe)
                pe.wait_ge(w.loaded, w.all)
                pe.wait_ge(S["loaded"], 16)
                for k in range(KC):
                    t_.transpose(bank[0][:, k * MAXN:(k + 1) * MAXN], h[:, k * 128:(k + 1) * 128], c.ident[0:MAXN, 0:MAXN])
                for m in range(MC):
                    last = t_.transpose(bank[1][0:DH, m * 128:(m + 1) * 128], proj[:, m, :], c.ident[:, :])
                last.then_inc(S["h_turned"], 1)
                pe.wait_ge(S["h_kept"], 1)
                for b, w_ in ((2, wq), (3, wk)):
                    for a in range(H):
                        for k in range(KC):
                            t_.matmul(bank[b][0:DH, a * MAXN:(a + 1) * MAXN], w_[:, k, a * DH:(a + 1) * DH],
                                      h_t[:, k * MAXN:(k + 1) * MAXN], start=(k == 0), stop=(k == KC - 1))
                for k in range(KC):
                    last = t_.matmul(bank[0][0:MAXN, 0:D], h_t[:, k * MAXN:(k + 1) * MAXN], wv[:, k, :],
                                     start=(k == 0), stop=(k == KC - 1))
                last.then_inc(S["qkv_ready"], 1)
                pe.wait_ge(S["qkv_kept"], 1)
                for j, sq in enumerate((q_sq, k_sq)):
                    for a in range(H):
                        t_.matmul(bank[1][0:MAXN, j * H + a:j * H + a + 1], sq[:, a * MAXN:(a + 1) * MAXN], half[:, :],
                                  start=True, stop=True)
                for a in range(H):
                    last = t_.matmul(bank[4 + a // 2][0:MAXN, (a % 2) * M:(a % 2 + 1) * M],
                                     q_t[:, a * MAXN:(a + 1) * MAXN], proj_t[:, :], start=True, stop=True)
                last.then_inc(S["features_ready"], 1)
                pe.wait_ge(S["q_seen"], 1)
                for a in range(H):
                    last = t_.matmul(bank[4 + a // 2][0:MAXN, (a % 2) * M:(a % 2 + 1) * M],
                                     k_t[:, a * MAXN:(a + 1) * MAXN], proj_t[:, :], start=True, stop=True)
                last.then_inc(S["k_ready"], 1)
                pe.wait_ge(S["k_seen"], 1)
                t_.transpose(bank[2][0:H, 0:MAXN], peak[:, H:2 * H], c.ident[0:MAXN, 0:MAXN]).then_inc(S["peak_turned"], 1)
                pe.wait_ge(S["peak_down"], 1)
                t_.matmul(bank[3][0:MAXN, 0:H], peak_t[:, :].to_broadcast([H, MAXN]), c.ident[0:H, 0:H],
                          start=True, stop=True).then_inc(S["peak_wide"], 1)
                norm.pe_row(pe)
                pe.wait_ge(S["q_done"], 1)
                for a in range(H):
                    for m in range(MC):
                        i = a * MC + m
                        t_.transpose(bank[i // 8][:, (i % 8) * MAXN:(i % 8 + 1) * MAXN],
                                     qf[:, a * M + m * 128:a * M + (m + 1) * 128], c.ident[0:MAXN, 0:MAXN])
                norm.pe_wide(pe)
                pe.wait_ge(S["k_done"], 1)
                for a in range(H):
                    for m in range(MC):
                        i = a * MC + m
                        last = t_.matmul(bank[4 + i // 6][:, (i % 6) * W1:(i % 6 + 1) * W1],
                                         kf[:, a * M + m * 128:a * M + (m + 1) * 128], v1[:, a, :],
                                         start=True, stop=True)
                last.then_inc(S["outer_ready"], 1)
                pe.wait_ge(S["outer_kept"], 1)
                for a in range(H):
                    for m in range(MC):
                        i = a * MC + m
                        last = t_.matmul(bank[2 + a // 4][0:MAXN, (a % 4) * W1:(a % 4 + 1) * W1],
                                         qf_t[:, i * MAXN:(i + 1) * MAXN], kv[:, i, :],
                                         start=(m == 0), stop=(m == MC - 1))
                last.then_inc(S["mixed_ready"], 1)
                pe.wait_ge(S["attn_ready"], 1)
                for k in range(KC):
                    last = t_.transpose(bank[0][:, k * MAXN:(k + 1) * MAXN], attn[:, k * 128:(k + 1) * 128],
                                        c.ident[0:MAXN, 0:MAXN])
                last.then_inc(S["attn_turned"], 1)
                pe.wait_ge(S["attn_kept"], 1)
                for k in range(KC):
                    last = t_.matmul(bank[1][0:MAXN, 0:D], attn_t[:, k * MAXN:(k + 1) * MAXN], wo[:, k, :],
                                     start=(k == 0), stop=(k == KC - 1))
                last.then_inc(S["out_ready"], 1)
                pe.wait_ge(S["out_kept"], 1)
                pe.wait_ge(S["picks_made"], 1)
                t_.matmul(bank[4][:, 0:D], own_row[:, :], out[:, :], start=True, stop=True)
                t_.matmul(bank[5][:, 0:D], last_row[:, :], out[:, :], start=True, stop=True).then_inc(S["wide_ready"], 1)

            @block.scalar
            def _(act):
                a_ = nc.scalar
                a_.preload_act_table_set(TABLES)
                norm.act_deviation(act)
                act.wait_ge(S["biases"], 1)
                for j, (f, done) in enumerate(((qf, S["q_exp"]), (kf, S["k_exp"]))):
                    for a in range(H):
                        last = a_.activation(f[:, a * M:(a + 1) * M], f[:, a * M:(a + 1) * M], ACT.Exp,
                                             bias=bias[:, j * H + a:j * H + a + 1])
                    last.then_inc(done, 1)
                    if j == 0:
                        norm.act_row(act)

            @block.vector
            def _(dve):
                v = nc.vector
                done = [0]

                def link(ins):
                    done[0] += 1
                    ins.then_inc(S["chain"], 1)
                    dve.wait_ge(S["chain"], done[0])

                v.memset(half[:, :], 0.5)
                v.memset(v1[:, :, :], 1.0).then_inc(S["half_made"], 1)
                dve.wait_ge(S["half_made"], 1)
                dve.wait_ge(S["picks"], 2)
                v.tensor_tensor(own_row[:, :], own_row[:, :], c.ident[0:MAXN, :], ALU.add).then_inc(S["picks_made"], 1)
                dve.wait_ge(S["h_turned"], 1)
                v.tensor_copy(h_t[:, :], bank[0][:, 0:KC * MAXN])
                v.tensor_copy(proj_t[:, :], bank[1][0:DH, 0:M]).then_inc(S["h_kept"], 1)
                norm.dve_scale(dve)
                dve.wait_ge(S["qkv_ready"], 1)
                v.tensor_scalar(q_t[:, :], bank[2][0:DH, 0:H * MAXN], DH ** -0.25, None, ALU.mult)
                link(v.tensor_scalar(k_t[:, :], bank[3][0:DH, 0:H * MAXN], DH ** -0.25, None, ALU.mult))
                v.tensor_tensor(q_sq[:, :], q_t[:, :], q_t[:, :], ALU.mult)
                v.tensor_tensor(k_sq[:, :], k_t[:, :], k_t[:, :], ALU.mult)
                v.tensor_copy(v1[:, :, 0:DH], bank[0][0:MAXN, 0:D].rearrange("p (h d) -> p h d", h=H)) \
                    .then_inc(S["qkv_kept"], 1)
                dve.wait_ge(S["features_ready"], 1)
                v.tensor_copy(diag[:, :], bank[1][0:MAXN, 0:2 * H])
                for b in range(4):
                    ins = v.tensor_copy(qf[:, b * 512:(b + 1) * 512], bank[4 + b][0:MAXN, :])
                ins.then_inc(S["q_seen"], 1)
                dve.wait_ge(S["q_seen"], 1)
                v.tensor_reduce(peak[:, 0:H], qf[:, :].rearrange("p (h m) -> p h m", h=H), op=ALU.max, axis=AX.X)
                dve.wait_ge(S["k_ready"], 1)
                for b in range(4):
                    ins = v.tensor_copy(kf[:, b * 512:(b + 1) * 512], bank[4 + b][0:MAXN, :])
                link(ins)
                v.tensor_reduce(peak[:, H:2 * H], kf[:, :].rearrange("p (h m) -> p h m", h=H), op=ALU.max,
                                axis=AX.X).then_inc(S["k_seen"], 1)
                dve.wait_ge(S["peak_turned"], 1)
                v.reduce_max(peak_t[:, :], bank[2][0:H, 0:MAXN], AX.X).then_inc(S["peak_down"], 1)
                dve.wait_ge(S["peak_wide"], 1)
                link(v.tensor_copy(peak[:, H:2 * H], bank[3][0:MAXN, 0:H]))
                v.scalar_tensor_tensor(bias[:, :], diag[:, :], -1.0, peak[:, :], ALU.mult, ALU.subtract) \
                    .then_inc(S["biases"], 1)
                dve.wait_ge(S["q_exp"], 1)
                v.tensor_scalar(qf[:, :], qf[:, :], M ** -0.5, KEPS, ALU.mult, ALU.add).then_inc(S["q_done"], 1)
                dve.wait_ge(S["k_exp"], 1)
                v.tensor_scalar(kf[:, :], kf[:, :], M ** -0.5, KEPS, ALU.mult, ALU.add).then_inc(S["k_done"], 1)
                norm.dve_shift(dve)
                dve.wait_ge(S["outer_ready"], 1)
                for b in range(2):
                    v.tensor_copy(qf_t[:, b * 512:(b + 1) * 512], bank[b][:, :])
                for b in range(3):
                    n = min(6, H * MC - 6 * b)
                    ins = v.tensor_copy(kv[:, 6 * b:6 * b + n, :],
                                        bank[4 + b][:, 0:n * W1].rearrange("p (i w) -> p i w", w=W1))
                ins.then_inc(S["outer_kept"], 1)
                dve.wait_ge(S["mixed_ready"], 1)
                for b in range(2):
                    heads = bank[2 + b][0:MAXN, 0:4 * W1].rearrange("p (h w) -> p h w", w=W1)
                    link(v.tensor_scalar(z[:, 4 * b:4 * b + 4], heads[:, :, DH], KEPS, None, ALU.add))
                    link(v.reciprocal(z[:, 4 * b:4 * b + 4], z[:, 4 * b:4 * b + 4]))
                    ins = v.tensor_tensor(attn[:, b * 256:(b + 1) * 256].rearrange("p (h d) -> p h d", h=4),
                                          heads[:, :, 0:DH],
                                          z[:, 4 * b:4 * b + 4].unsqueeze(2).to_broadcast([MAXN, 4, DH]), ALU.mult)
                ins.then_inc(S["attn_ready"], 1)
                dve.wait_ge(S["attn_turned"], 1)
                v.tensor_copy(attn_t[:, :], bank[0][:, 0:KC * MAXN]).then_inc(S["attn_kept"], 1)
                dve.wait_ge(S["out_ready"], 1)
                v.tensor_copy(out[:, :], bank[1][0:MAXN, 0:D]).then_inc(S["out_kept"], 1)
                dve.wait_ge(S["wide_ready"], 1)
                v.tensor_copy(o.first_mix[:, :], bank[4][:, 0:D])
                v.tensor_copy(o.rest_mix[:, :], bank[5][:, 0:D])


def convolve(nc, ctx, c, s, n, mix, x1_d, sums_d, y, acc):
    with ExitStack() as own:
        semaphores = Semaphores(nc, own)
        def sb(name, shape, dt=F32):
            return own.enter_context(nc.sbuf_tensor(f"v_{name}", shape, dt))

        def sem(name):
            return semaphores.take(f"v_{name}")

        def two(make, name, *a):
            return [make(f"{name}{u}", *a) for u in range(2)]

        def pb(name, shape):
            return own.enter_context(nc.psum_tensor(f"v_{name}", shape, F32))

        idx = two(sb, "idx", [SLOTS, 1], U32)
        total = two(sb, "total", [SLOTS, D])
        x1 = two(sb, "x1", [ROWS, D])
        hi, lo = two(sb, "hi", [128, KC * ROWS], F32R), two(sb, "lo", [128, KC * ROWS], F32R)
        sq = pb("sq", [ROWS, D])
        turned_p, conv_p = two(pb, "turned_p", [128, 512]), two(pb, "conv_p", [ROWS, 512])

        cleared = sem("cleared")
        total_in = two(c.pool_dma, "v_total_in")
        idx_ready, mean_ready, turned_ready, hi_ready, lo_ready, conv_ready, conv_read, x1_in, based, y_ready, \
            sq_ready, summed, summed_sq = (two(sem, m) for m in (
                "idx_ready", "mean_ready", "turned_ready", "hi_ready", "lo_ready", "conv_ready",
                "conv_read", "x1_in", "based", "y_ready", "sq_ready", "summed", "summed_sq"))
        AHEAD, BEHIND = 2, 2

        with nc.Block() as block:
            @block.gpsimd
            def _(pool):
                g = nc.gpsimd
                pool.wait_ge(cleared, 1)

                def gather(x):
                    p = x.par
                    pool.wait_ge(turned_ready[p], x.turn)
                    g.tensor_copy(idx[p][:, :], s.sum_row[:, ds(x.num, 1)]).then_inc(idx_ready[p], 1)
                    pool.wait_ge(idx_ready[p], x.turn + 1)
                    settle(pool)
                    g.indirect_dma_start(total[p][:, :], None, sums_d, bass.IndirectOffsetOnAxis(idx[p][:, :], 0),
                                         bounds_check=T * SLOTS - 1, oob_is_err=False).then_inc(total_in[p], 16)

                def base(x):
                    p = x.par
                    pool.wait_ge(x1_in[p], 32 * (x.turn + 1))
                    g.tensor_tensor(x1[p][:, :], x1[p][:, :],
                                    (mix.first_mix if x.is_zero() else mix.rest_mix)[0:ROWS, :],
                                    ALU.add).then_inc(based[p], 1)

                def body(at):
                    if x := at(2):
                        gather(x)
                    if x := at(0):
                        base(x)
                sweep(pool, body, 4, AHEAD, BEHIND, 2)

            @block.sync
            def _(sp):
                def body(at):
                    if x := at(1):
                        p = x.par
                        sp.wait_ge(y_ready[p], x.turn)
                        for a, b in ROWS_CUT:
                            sp.dma_start(x1[p][a:b, :], x1_d[ds(ROWS * x.num + a, b - a), :]).then_inc(x1_in[p], 16)
                sweep(sp, body, 4, AHEAD, BEHIND, 2)

            @block.tensor
            def _(pe):
                t_ = nc.tensor

                def turn(x):
                    p = x.par
                    pe.wait_ge(mean_ready[p], x.turn + 1)
                    pe.wait_ge(lo_ready[p], x.turn)
                    for k in range(KC):
                        last = t_.transpose(turned_p[p][:, k * ROWS:(k + 1) * ROWS],
                                            total[p][0:ROWS, k * 128:(k + 1) * 128], c.ident[0:ROWS, 0:ROWS])
                    last.then_inc(turned_ready[p], 1)

                def first_weights(x):
                    p = x.par
                    pe.wait_ge(hi_ready[p], x.turn + 1)
                    pe.wait_ge(lo_ready[p], x.turn + 1)
                    pe.wait_ge(conv_read[p], x.turn)
                    product(t_, conv_p[p][:, 0:D], hi[p], lo[p], n.w_hi, n.w_lo, ROWS, (0, 1))

                def last_weights(x):
                    p = x.par
                    t_.matmul(conv_p[p][:, 0:D], n.ones[:, :], n.bias[:, :], start=False, stop=False)
                    product(t_, conv_p[p][:, 0:D], hi[p], lo[p], n.w_hi, n.w_lo, ROWS, (2, 3)) \
                        .then_inc(conv_ready[p], 1)

                def body(at):
                    if x := at(0):
                        first_weights(x)
                    if x := at(1):
                        turn(x)
                    if x := at(0):
                        last_weights(x)
                sweep(pe, body, 4, AHEAD, BEHIND, 2)

            @block.scalar
            def _(act):
                a = nc.scalar
                a.preload_act_table_set(TABLES)

                def body(at):
                    if x := at(1):
                        p = x.par
                        act.wait_ge(total_in[p], 16 * (x.turn + 1))
                        a.activation(total[p][:, :], total[p][:, :], ACT.Copy, scale=s.inverse[:, ds(x.num, 1)]) \
                            .then_inc(mean_ready[p], 1)
                        act.wait_ge(turned_ready[p], x.turn + 1)
                        act.wait_ge(conv_ready[p], x.turn)
                        a.copy(hi[p][:, :], turned_p[p][:, 0:KC * ROWS]).then_inc(hi_ready[p], 1)
                    if x := at(-1):
                        p = x.par
                        act.wait_ge(y_ready[p], x.turn + 1)
                        if not x.is_zero():
                            b = x.before()
                            act.wait_ge(summed_sq[b.par], b.turn + 1)
                        a.activation(sq[:, :], y[0:ROWS, ds(D * x.num, D)], ACT.Square).then_inc(sq_ready[p], 1)
                sweep(act, body, 4, AHEAD, BEHIND, 2)

            @block.vector
            def _(dve):
                v = nc.vector
                for m in acc:
                    v.memset(m[:, :], 0.0)
                for u in range(2):
                    ins = v.memset(total[u][:, :], 0.0)
                ins.then_inc(cleared, 1)
                dve.wait_ge(cleared, 1)

                def add(x):
                    p = x.par
                    dve.wait_ge(conv_ready[p], x.turn + 1)
                    z = y[0:ROWS, ds(D * x.num, D)]
                    v.scalar_tensor_tensor(z, n.shift_w[0:ROWS, :], s.has[:, ds(x.num, 1)],
                                           conv_p[p][:, 0:D], ALU.mult, ALU.add).then_inc(conv_read[p], 1)
                    dve.wait_ge(conv_read[p], x.turn + 1)
                    dve.wait_ge(based[p], x.turn + 1)
                    v.scalar_tensor_tensor(z, z, 0.0, x1[p][:, :], ALU.max, ALU.add).then_inc(y_ready[p], 1)

                def sum_up(x):
                    p, b = x.par, x.before()
                    dve.wait_ge(y_ready[p], x.turn + 1)
                    if not x.is_zero():
                        dve.wait_ge(summed[b.par], b.turn + 1)
                        dve.wait_ge(summed_sq[b.par], b.turn + 1)
                    v.tensor_tensor(acc[0][0:ROWS, :], acc[0][0:ROWS, :], y[0:ROWS, ds(D * x.num, D)],
                                    ALU.add).then_inc(summed[p], 1)
                    dve.wait_ge(sq_ready[p], x.turn + 1)
                    v.tensor_tensor(acc[1][0:ROWS, :], acc[1][0:ROWS, :], sq[:, :], ALU.add).then_inc(summed_sq[p], 1)

                def body(at):
                    if x := at(1):
                        p = x.par
                        dve.wait_ge(hi_ready[p], x.turn + 1)
                        v.tensor_tensor(lo[p][:, :], turned_p[p][:, 0:KC * ROWS], hi[p][:, :].bitcast(F32),
                                        ALU.subtract).then_inc(lo_ready[p], 1)
                    if x := at(0):
                        add(x)
                    if x := at(-1):
                        sum_up(x)
                sweep(dve, body, 4, AHEAD, BEHIND, 2)


def second_norm(nc, ctx, c, acc, g_d, b_d):
    o = Buffers()
    o.gain = ctx.enter_context(nc.sbuf_tensor("gain", [128, D], F32))
    o.offset = ctx.enter_context(nc.sbuf_tensor("offset", [128, D], F32))
    with ExitStack() as own:
        semaphores = Semaphores(nc, own)
        def sb(name, shape, dt=F32):
            return own.enter_context(nc.sbuf_tensor(f"m_{name}", shape, dt))

        def sem(name):
            return semaphores.take(f"m_{name}")
        g_col, b_col, a_col, s_col, var, mean, logv = (sb(m, [128, KC]) for m in (
            "g_col", "b_col", "a_col", "s_col", "var", "mean", "logv"))
        diag = [sb(f"diag{j}", [128, D]) for j in range(2)]
        sums_p, gain_p, offset_p = (own.enter_context(nc.psum_tensor(f"m_{m}", [128, 512], F32))
                                    for m in ("sums_p", "gain_p", "offset_p"))
        loaded, sums_ready, chain, var_ready, log_ready, rstd_ready, diag_ready, wide_ready = (
            sem(m) for m in ("loaded", "sums_ready", "chain", "var_ready", "log_ready", "rstd_ready", "diag_ready",
                             "wide_ready"))
        with nc.Block() as block:
            @block.sync
            def _(sp):
                sp.dma_start(g_col[:, :], g_d.rearrange("(k p) -> p k", p=128), allow_slow_non_contiguous=True).then_inc(loaded, 16)
                sp.dma_start(b_col[:, :], b_d.rearrange("(k p) -> p k", p=128), allow_slow_non_contiguous=True).then_inc(loaded, 16)

            @block.tensor
            def _(pe):
                t_ = nc.tensor
                for j in range(2):
                    for k in range(KC):
                        last = t_.matmul(sums_p[:, j * KC + k:j * KC + k + 1], acc[j][0:ROWS, k * 128:(k + 1) * 128],
                                         c.ones[0:ROWS, 0:1], start=True, stop=True)
                last.then_inc(sums_ready, 1)
                pe.wait_ge(diag_ready, 1)
                t_.matmul(gain_p[:, :], c.ones[:, :], diag[0][:, :], start=True, stop=True)
                t_.matmul(offset_p[:, :], c.ones[:, :], diag[1][:, :], start=True, stop=True).then_inc(wide_ready, 1)

            @block.scalar
            def _(act):
                a = nc.scalar
                a.preload_act_table_set(TABLES)
                act.wait_ge(var_ready, 1)
                a.activation(logv[:, :], var[:, :], ACT.Ln).then_inc(log_ready, 1)
                act.wait_ge(log_ready, 1)
                a.activation(var[:, :], logv[:, :], ACT.Exp, scale=-0.5).then_inc(rstd_ready, 1)

            @block.vector
            def _(dve):
                v = nc.vector
                done = [0]

                def link(ins):
                    done[0] += 1
                    ins.then_inc(chain, 1)
                    dve.wait_ge(chain, done[0])

                dve.wait_ge(sums_ready, 1)
                column_variance(v, link, sums_p, mean, a_col, var, var_ready)
                dve.wait_ge(rstd_ready, 1)
                dve.wait_ge(loaded, 32)
                link(v.tensor_tensor(a_col[:, :], var[:, :], g_col[:, :], ALU.mult))
                link(v.tensor_tensor(mean[:, :], mean[:, :], a_col[:, :], ALU.mult))
                link(v.tensor_tensor(s_col[:, :], b_col[:, :], mean[:, :], ALU.subtract))
                for j, col in enumerate((a_col, s_col)):
                    for k in range(KC):
                        ins = v.tensor_scalar(diag[j][:, k * 128:(k + 1) * 128], c.ident[:, :], col[:, k:k + 1], None,
                                              ALU.mult)
                ins.then_inc(diag_ready, 1)
                dve.wait_ge(wide_ready, 1)
                v.tensor_copy(o.gain[:, :], gain_p[:, :])
                v.tensor_copy(o.offset[:, :], offset_p[:, :])
    return o


def finish_nodes(nc, ctx, c, b, x1_d, y, out_d):
    P = 4
    with ExitStack() as own:
        semaphores = Semaphores(nc, own)
        def sb(name, shape, dt=F32):
            return own.enter_context(nc.sbuf_tensor(f"f_{name}", shape, dt))

        def sem(name):
            return semaphores.take(f"f_{name}")

        def ring(make, name, *a):
            return [make(f"{name}{u}", *a) for u in range(P)]

        x1 = ring(sb, "x1", [ROWS, D])
        z_p = [own.enter_context(nc.psum_tensor(f"f_z_p{u}", [ROWS, 512], F32)) for u in range(P)]
        stats, moments = ring(sb, "stats", [ROWS, 6]), ring(sb, "moments", [ROWS, 2])
        logv, rstd, shift = ring(sb, "logv", [ROWS, 1]), ring(sb, "rstd", [ROWS, 1]), ring(sb, "shift", [ROWS, 1])
        x1_in, based, scaled, z_ready, stats_ready, moments_ready, log_ready, rstd_ready, shift_ready, out_ready, \
            stored = (ring(sem, m) for m in (
                "x1_in", "based", "scaled", "z_ready", "stats_ready", "moments_ready", "log_ready", "rstd_ready",
                "shift_ready", "out_ready", "stored"))
        AHEAD, BEHIND = 4, 4
        with nc.Block() as block:
            @block.sync
            def _(sp):
                def body(at):
                    if x := at(3):
                        p = x.par
                        sp.wait_ge(z_ready[p], x.turn)
                        for lo, hi in ROWS_CUT:
                            sp.dma_start(x1[p][lo:hi, :], x1_d[ds(ROWS * x.num + lo, hi - lo), :]).then_inc(x1_in[p], 16)
                sweep(sp, body, P, AHEAD, BEHIND)

            @block.gpsimd
            def _(pool):
                def body(at):
                    if x := at(1):
                        p = x.par
                        pool.wait_ge(x1_in[p], 32 * (x.turn + 1))
                        nc.gpsimd.tensor_tensor(x1[p][:, :], x1[p][:, :], b.offset[0:ROWS, :], ALU.add) \
                            .then_inc(based[p], 1)
                sweep(pool, body, P, AHEAD, BEHIND)

            @block.tensor
            def _(pe):
                t_ = nc.tensor

                def body(at):
                    if x := at(0):
                        p = x.par
                        ident = c.ident[0:ROWS, 0:ROWS]
                        pe.wait_ge(out_ready[p], x.turn)
                        pe.wait_ge(based[p], x.turn + 1)
                        t_.matmul(z_p[p][:, 0:D], ident, x1[p][:, :], start=True, stop=False)
                        pe.wait_ge(scaled[p], x.turn + 1)
                        t_.matmul(z_p[p][:, 0:D], ident, y[0:ROWS, ds(D * x.num, D)], start=False, stop=True) \
                            .then_inc(z_ready[p], 1)
                sweep(pe, body, P, AHEAD, BEHIND)

            @block.scalar
            def _(act):
                a = nc.scalar
                a.preload_act_table_set(TABLES)

                def body(at):
                    if x := at(-2):
                        p = x.par
                        act.wait_ge(moments_ready[p], x.turn + 1)
                        a.activation(logv[p][:, :], moments[p][:, 1:2], ACT.Ln, bias=c.ln_eps[0:ROWS, :]) \
                            .then_inc(log_ready[p], 1)
                        act.wait_ge(log_ready[p], x.turn + 1)
                        a.activation(rstd[p][:, :], logv[p][:, :], ACT.Exp, scale=-0.5).then_inc(rstd_ready[p], 1)
                    if x := at(-3):
                        p = x.par
                        act.wait_ge(shift_ready[p], x.turn + 1)
                        a.activation(y[0:ROWS, ds(D * x.num, D)], z_p[p][:, 0:D], ACT.Identity, bias=shift[p][:, :],
                                     scale=rstd[p][:, :]).then_inc(out_ready[p], 1)
                    if (x := at(-4)) and x.buf % 2:
                        b = x.before()
                        act.wait_ge(out_ready[b.par], b.turn + 1)
                        act.wait_ge(out_ready[x.par], x.turn + 1)
                        settle(act)
                        tiles = out_d[ds(ROWS * x.num - ROWS, 2 * ROWS), :].rearrange("(t p) d -> p t d", t=2)
                        for lo, hi in ROWS_CUT:
                            act.dma_start(tiles[lo:hi, :, :], y[lo:hi, ds(D * x.num - D, 2 * D)]
                                          .rearrange("p (t d) -> p t d", t=2)).then_inc(stored[x.par // 2], 16)
                sweep(act, body, P, AHEAD, BEHIND)
                for u in range(P // 2):
                    act.wait_ge(stored[u], 32 * (T // P))

            @block.vector
            def _(dve):
                v = nc.vector

                def scale(x):
                    z = y[0:ROWS, ds(D * x.num, D)]
                    v.tensor_tensor(z, z, b.gain[0:ROWS, :], ALU.mult).then_inc(scaled[x.par], 1)

                def measure(x):
                    p = x.par
                    dve.wait_ge(z_ready[p], x.turn + 1)
                    settle(dve)
                    v.bn_stats(stats[p][:, :], z_p[p][:, 0:D]).then_inc(stats_ready[p], 1)

                def gather_moments(x):
                    p = x.par
                    dve.wait_ge(stats_ready[p], x.turn + 1)
                    dve.wait_ge(shift_ready[p], x.turn)
                    settle(dve)
                    v.bn_aggr(moments[p][:, :], stats[p][:, :]).then_inc(moments_ready[p], 1)

                def centre(x):
                    p = x.par
                    dve.wait_ge(rstd_ready[p], x.turn + 1)
                    dve.wait_ge(out_ready[p], x.turn)
                    v.tensor_scalar(shift[p][:, :], moments[p][:, 0:1], -1.0, rstd[p][:, :], ALU.mult, ALU.mult) \
                        .then_inc(shift_ready[p], 1)

                def body(at):
                    if x := at(-3):
                        centre(x)
                    if x := at(0):
                        scale(x)
                    if x := at(-2):
                        gather_moments(x)
                    if x := at(-1):
                        measure(x)
                sweep(dve, body, P, AHEAD, BEHIND)


def resnorm_gnn_pair(nc, x, src, dst, w0, g1, b1, g2, b2, w_conv, b_conv, wq, wk, wv, wo, proj, out):
    x1_d = nc.dram_tensor("x1_rows", (N, D), F32, kind="Internal").ap()
    sums_d = nc.dram_tensor("group_sums", (T * SLOTS, D), F32, kind="Internal").ap()
    own_d = nc.dram_tensor("source_rows", (T * SLOTS, D), F32, kind="Internal").ap()
    other_d = nc.dram_tensor("destination_halves", (2, T * 128, KC * SLOTS), F32, kind="Internal").ap()
    with ExitStack() as ctx:
        c = lasting_constants(nc, ctx)
        acc = [ctx.enter_context(nc.sbuf_tensor(f"column_sums{j}", [SLOTS, D], F32)) for j in range(2)]
        by_dst = edge_tables(nc, ctx, "d", True)
        with ExitStack() as first:
            by_src = edge_tables(nc, first, "s", False)
            with ExitStack() as sorting:
                make_constants(nc, sorting, c)
                sort_edges(nc, c, (("s", by_src, src, dst), ("d", by_dst, dst, src)))
            e = edge_scores(nc, first, c, by_src, x, w0, x1_d, own_d, other_d, acc)
            attend_edges(nc, first, c, by_src, e, w0, x1_d, own_d, other_d, acc)
        mix, n = second_layer_buffers(nc, ctx)
        with ExitStack() as weights:
            semaphores = Semaphores(nc, weights)
            w = second_layer_weights(nc, weights, semaphores, wq, wk, wv, wo, proj, g1, b1, w_conv, b_conv)
            gather_sums(nc, ctx, c, by_dst, x1_d, sums_d, w)
            few_node_attention(nc, c, x1_d, w, mix, n, acc)
        y = ctx.enter_context(nc.sbuf_tensor("y", [ROWS, T * D], F32))
        convolve(nc, ctx, c, by_dst, n, mix, x1_d, sums_d, y, acc)
        b = second_norm(nc, ctx, c, acc, g2, b2)
        finish_nodes(nc, ctx, c, b, x1_d, y, out)


_INS = ['x', 'src', 'dst', 'L0_gnn_W', 'L1_gnn_norm1_g', 'L1_gnn_norm1_b', 'L1_gnn_norm2_g', 'L1_gnn_norm2_b',
        'L1_gnn_W_conv', 'L1_gnn_b_conv', 'L1_gnn_Wq', 'L1_gnn_Wk', 'L1_gnn_Wv', 'L1_gnn_Wo', 'L1_gnn_proj']


def kernel(**inputs):
    import numpy as _np
    import concourse.bacc as _bacc
    from concourse import mybir as _mybir
    from concourse.bass_utils import run_bass_kernel_spmd as _run

    nc = _bacc.Bacc("TRN2", target_bir_lowering=False, num_devices=1)
    arrays, args = {}, []
    for name in _INS:
        a = _np.ascontiguousarray(inputs[name])
        arrays[f"in_{name}"] = a
        args.append(nc.dram_tensor(f"in_{name}", a.shape, _mybir.dt.from_np(a.dtype), kind="ExternalInput").ap())
    out = nc.dram_tensor("out", (N, D), _mybir.dt.float32, kind="ExternalOutput").ap()
    resnorm_gnn_pair(nc, *args, out)
    r = _run(nc, [arrays], core_ids=[0])
    return r.results[0]["out"]
```
